# Optimizing a Trainium2 kernel written in Bass

```python
import numpy as np
import jax
import jax.numpy as jnp

def _softmax(x, axis=-1):
    return jax.nn.softmax(x, axis=axis)

def _gelu(x):
    return jax.nn.gelu(x, approximate=True)

def _silu(x):
    return jax.nn.silu(x)

def _sigmoid(x):
    return jax.nn.sigmoid(x)

def _layernorm(x, axis=-1, eps=1e-05):
    m = jnp.mean(x, axis=axis, keepdims=True)
    v = jnp.var(x, axis=axis, keepdims=True)
    return (x - m) / jnp.sqrt(v + eps)

def _scatter_add(tgt, idx, src, axis=0):
    return tgt.at[idx].add(src)

def _segment_sum(src, seg, n):
    return jax.ops.segment_sum(src, seg, n)
kernel_name = 'mk_xattn_ffn_d1_seqx_r2_fbfd72'

def setup_inputs(seed: int=0):
    np.random.seed(seed)
    _w = jnp.asarray

    def _rec_inputs():
        import jax
        import jax.numpy as jnp
        _rk = jax.random.key(seed)
        x = -0.0002928 + 1 * jax.random.normal(jax.random.fold_in(_rk, 1), (8, 1024, 512), jnp.float32)
        _lenS = 1024 - jax.random.randint(jax.random.fold_in(_rk, 7), (8,), 0, max(1, 1024 // 4) + 1, jnp.int32)
        _lenS2 = 64 - jax.random.randint(jax.random.fold_in(_rk, 8), (8,), 0, max(1, 64 // 4) + 1, jnp.int32)
        _ctx_1024P = jax.random.normal(jax.random.fold_in(_rk, 11), (8, 16, 512), jnp.float32)
        _ctx_1024c = jax.random.dirichlet(jax.random.fold_in(_rk, 511), 0.3 * jnp.ones((16,), jnp.float32), (8, 64))
        _ctx_1024t = jnp.einsum('bsk,bkd->bsd', _ctx_1024c, _ctx_1024P)
        _ctx_1024t = _ctx_1024t * jax.lax.rsqrt(jnp.mean(jnp.square(_ctx_1024t)) + 1e-12) * 0.953939
        ctx_1024 = -1.39393e-06 + 0.999914 * (_ctx_1024t + 0.3 * jax.random.normal(jax.random.fold_in(_rk, 611), (8, 64, 512), jnp.float32))
        return (x, ctx_1024)
    x, ctx_1024 = _rec_inputs()

    def _L0_xattn_setup():
        import jax, jax.numpy as jnp
        import numpy as np
        import math
        D_MODEL = 512
        N_HEADS = 16
        D_K = D_MODEL // N_HEADS

        def _split_heads(x, B):
            return x.reshape(B, -1, N_HEADS, D_K).transpose(0, 2, 1, 3)

        def _phase_sync(x, phase):
            half = D_K // 2
            xr, xi = (x[..., :half], x[..., half:])
            c = jnp.cos(phase)[None]
            s = jnp.sin(phase)[None]
            return jnp.concatenate([xr * c - xi * s, xr * s + xi * c], axis=-1)
        key = jax.random.key(seed)
        ks = jax.random.split(key, 12)
        B, S = (2, 1024)
        scale = 1.0 / math.sqrt(D_MODEL)
        inp = {'q': jax.random.normal(ks[0], (B, S, D_MODEL), jnp.float32), 'k': jax.random.normal(ks[1], (B, S, D_MODEL), jnp.float32), 'v': jax.random.normal(ks[2], (B, S, D_MODEL), jnp.float32), 'Wq': jax.random.normal(ks[3], (D_MODEL, D_MODEL), jnp.float32) * scale, 'bq': jnp.zeros((D_MODEL,), jnp.float32), 'Wk': jax.random.normal(ks[4], (D_MODEL, D_MODEL), jnp.float32) * scale, 'bk': jnp.zeros((D_MODEL,), jnp.float32), 'Wv': jax.random.normal(ks[5], (D_MODEL, D_MODEL), jnp.float32) * scale, 'bv': jnp.zeros((D_MODEL,), jnp.float32), 'Wo': jax.random.normal(ks[6], (D_MODEL, D_MODEL), jnp.float32) * scale, 'bo': jnp.zeros((D_MODEL,), jnp.float32), 'phase': jax.random.normal(ks[7], (N_HEADS, 1, 1), jnp.float32)}
        return inp
    _L0_xattn_all = _L0_xattn_setup()
    _L0_xattn_in = {k: v for k, v in _L0_xattn_all.items() if k in ('Wq', 'bq', 'Wk', 'bk', 'Wv', 'bv', 'Wo', 'bo', 'phase')}
    del _L0_xattn_all

    def _L0_ffn_setup():
        import jax, jax.numpy as jnp
        import numpy as np
        B, S, DIM = (4, 2048, 512)
        BASE_COUPLING = 0.1
        NUM_CYCLES = 3

        def _gelu(x):
            return jax.nn.gelu(x, approximate=False)

        def _coupling_net(h, w1, b1, w2, b2, w3, b3, w4, b4):
            h = _gelu(h @ w1 + b1)
            h = _gelu(h @ w2 + b2)
            h = _gelu(h @ w3 + b3)
            return jax.nn.sigmoid(h @ w4 + b4)

        def _global_net(h, w1, b1, w2, b2, w3, b3):
            h = _gelu(h @ w1 + b1)
            h = _gelu(h @ w2 + b2)
            return jax.nn.sigmoid(h @ w3 + b3)

        def _twist(x):
            o_r, o_i, p_r, p_i = jnp.split(x, 4, axis=-1)
            return jnp.concatenate([p_r, -p_i, -o_r, o_i], axis=-1)
        key = jax.random.key(seed)
        ks = jax.random.split(key, 9)
        d = DIM

        def w(k, fan_in, fan_out):
            return jax.random.normal(k, (fan_in, fan_out), dtype=jnp.float32) / np.sqrt(fan_in).astype(np.float32)
        inp = {'x': jax.random.normal(ks[0], (B, S, d), dtype=jnp.float32)}
        cn_dims = [(d, d), (d, d // 2), (d // 2, d // 4), (d // 4, 1)]
        for i, (a, b) in enumerate(cn_dims):
            inp[f'cn_w{i + 1}'] = w(ks[1 + i], a, b)
            inp[f'cn_b{i + 1}'] = jnp.zeros((b,), dtype=jnp.float32)
        gc_dims = [(d, d // 2), (d // 2, d // 4), (d // 4, 1)]
        for i, (a, b) in enumerate(gc_dims):
            inp[f'gc_w{i + 1}'] = w(ks[5 + i], a, b)
            inp[f'gc_b{i + 1}'] = jnp.zeros((b,), dtype=jnp.float32)
        inp['adaptive_range'] = jnp.full((1,), 0.2, dtype=jnp.float32)
        return inp
    _L0_ffn_all = _L0_ffn_setup()
    _L0_ffn_in = {k: v for k, v in _L0_ffn_all.items() if k in ('cn_w1', 'cn_b1', 'cn_w2', 'cn_b2', 'cn_w3', 'cn_b3', 'cn_w4', 'cn_b4', 'gc_w1', 'gc_b1', 'gc_w2', 'gc_b2', 'gc_w3', 'gc_b3', 'adaptive_range')}
    del _L0_ffn_all
    return {'x': x, 'ctx_1024': ctx_1024, 'L0_xattn_Wq': _L0_xattn_in['Wq'], 'L0_xattn_bq': _L0_xattn_in['bq'], 'L0_xattn_Wk': _L0_xattn_in['Wk'], 'L0_xattn_bk': _L0_xattn_in['bk'], 'L0_xattn_Wv': _L0_xattn_in['Wv'], 'L0_xattn_bv': _L0_xattn_in['bv'], 'L0_xattn_Wo': _L0_xattn_in['Wo'], 'L0_xattn_bo': _L0_xattn_in['bo'], 'L0_xattn_phase': _L0_xattn_in['phase'], 'L0_ffn_cn_w1': _L0_ffn_in['cn_w1'], 'L0_ffn_cn_b1': _L0_ffn_in['cn_b1'], 'L0_ffn_cn_w2': _L0_ffn_in['cn_w2'], 'L0_ffn_cn_b2': _L0_ffn_in['cn_b2'], 'L0_ffn_cn_w3': _L0_ffn_in['cn_w3'], 'L0_ffn_cn_b3': _L0_ffn_in['cn_b3'], 'L0_ffn_cn_w4': _L0_ffn_in['cn_w4'], 'L0_ffn_cn_b4': _L0_ffn_in['cn_b4'], 'L0_ffn_gc_w1': _L0_ffn_in['gc_w1'], 'L0_ffn_gc_b1': _L0_ffn_in['gc_b1'], 'L0_ffn_gc_w2': _L0_ffn_in['gc_w2'], 'L0_ffn_gc_b2': _L0_ffn_in['gc_b2'], 'L0_ffn_gc_w3': _L0_ffn_in['gc_w3'], 'L0_ffn_gc_b3': _L0_ffn_in['gc_b3'], 'L0_ffn_adaptive_range': _L0_ffn_in['adaptive_range']}

def reference(x, ctx_1024, L0_xattn_Wq, L0_xattn_bq, L0_xattn_Wk, L0_xattn_bk, L0_xattn_Wv, L0_xattn_bv, L0_xattn_Wo, L0_xattn_bo, L0_xattn_phase, L0_ffn_cn_w1, L0_ffn_cn_b1, L0_ffn_cn_w2, L0_ffn_cn_b2, L0_ffn_cn_w3, L0_ffn_cn_b3, L0_ffn_cn_w4, L0_ffn_cn_b4, L0_ffn_gc_w1, L0_ffn_gc_b1, L0_ffn_gc_w2, L0_ffn_gc_b2, L0_ffn_gc_w3, L0_ffn_gc_b3, L0_ffn_adaptive_range):
    import jax
    import jax.numpy as jnp

    def _L0_xattn_ref(q, k, v, Wq, bq, Wk, bk, Wv, bv, Wo, bo, phase):
        import jax, jax.numpy as jnp
        import numpy as np
        import math
        D_MODEL = 512
        N_HEADS = 16
        D_K = D_MODEL // N_HEADS

        def _split_heads(x, B):
            return x.reshape(B, -1, N_HEADS, D_K).transpose(0, 2, 1, 3)

        def _phase_sync(x, phase):
            half = D_K // 2
            xr, xi = (x[..., :half], x[..., half:])
            c = jnp.cos(phase)[None]
            s = jnp.sin(phase)[None]
            return jnp.concatenate([xr * c - xi * s, xr * s + xi * c], axis=-1)
        B = q.shape[0]
        qh = _split_heads(q @ Wq.T + bq, B)
        kh = _split_heads(k @ Wk.T + bk, B)
        vh = _split_heads(v @ Wv.T + bv, B)
        qh = _phase_sync(qh, phase)
        kh = _phase_sync(kh, phase)
        scores = jnp.einsum('bhqd,bhkd->bhqk', qh, kh) / math.sqrt(D_K)
        attn = jax.nn.softmax(scores, axis=-1)
        out = jnp.einsum('bhqk,bhkd->bhqd', attn, vh)
        out = out.transpose(0, 2, 1, 3).reshape(B, -1, D_MODEL)
        return out @ Wo.T + bo

    def _L0_ffn_ref(x, cn_w1, cn_b1, cn_w2, cn_b2, cn_w3, cn_b3, cn_w4, cn_b4, gc_w1, gc_b1, gc_w2, gc_b2, gc_w3, gc_b3, adaptive_range):
        import jax, jax.numpy as jnp
        import numpy as np
        B, S, DIM = (4, 2048, 512)
        BASE_COUPLING = 0.1
        NUM_CYCLES = 3

        def _gelu(x):
            return jax.nn.gelu(x, approximate=False)

        def _coupling_net(h, w1, b1, w2, b2, w3, b3, w4, b4):
            h = _gelu(h @ w1 + b1)
            h = _gelu(h @ w2 + b2)
            h = _gelu(h @ w3 + b3)
            return jax.nn.sigmoid(h @ w4 + b4)

        def _global_net(h, w1, b1, w2, b2, w3, b3):
            h = _gelu(h @ w1 + b1)
            h = _gelu(h @ w2 + b2)
            return jax.nn.sigmoid(h @ w3 + b3)

        def _twist(x):
            o_r, o_i, p_r, p_i = jnp.split(x, 4, axis=-1)
            return jnp.concatenate([p_r, -p_i, -o_r, o_i], axis=-1)
        global_context = x.mean(axis=1, keepdims=True)
        gf = _global_net(global_context, gc_w1, gc_b1, gc_w2, gc_b2, gc_w3, gc_b3)
        out = x
        for _ in range(NUM_CYCLES):
            tf = _coupling_net(out, cn_w1, cn_b1, cn_w2, cn_b2, cn_w3, cn_b3, cn_w4, cn_b4)
            combined = 0.7 * gf + 0.3 * tf
            coupling = BASE_COUPLING + adaptive_range * (combined - 0.5) * 2.0
            out = out + coupling * _twist(out)
        return out
    x = x + _L0_xattn_ref(_layernorm(x, axis=-1), ctx_1024, ctx_1024, L0_xattn_Wq, L0_xattn_bq, L0_xattn_Wk, L0_xattn_bk, L0_xattn_Wv, L0_xattn_bv, L0_xattn_Wo, L0_xattn_bo, L0_xattn_phase)
    x = x + _L0_ffn_ref(_layernorm(x, axis=-1), L0_ffn_cn_w1, L0_ffn_cn_b1, L0_ffn_cn_w2, L0_ffn_cn_b2, L0_ffn_cn_w3, L0_ffn_cn_b3, L0_ffn_cn_w4, L0_ffn_cn_b4, L0_ffn_gc_w1, L0_ffn_gc_b1, L0_ffn_gc_w2, L0_ffn_gc_b2, L0_ffn_gc_w3, L0_ffn_gc_b3, L0_ffn_adaptive_range)
    return x

_drawn_inputs = setup_inputs


def setup_inputs(seed=0):
    import zlib

    import numpy as np

    out = dict(_drawn_inputs(seed))
    spreads = {'L0_xattn_bq': (0.0, 0.391),
     'L0_xattn_bk': (0.0, 0.8),
     'L0_xattn_bv': (0.0, 0.1),
     'L0_xattn_bo': (0.0, 0.1),
     'L0_ffn_cn_b1': (0.0, 0.8),
     'L0_ffn_cn_b2': (0.0, 0.8),
     'L0_ffn_cn_b3': (0.0, 0.8),
     'L0_ffn_gc_b1': (0.0, 0.8),
     'L0_ffn_gc_b2': (0.0, 0.8)}
    factors = {'L0_xattn_phase': 8.0,
     'L0_ffn_cn_w1': 8.0,
     'L0_ffn_cn_w2': 8.0,
     'L0_ffn_cn_w3': 8.0,
     'L0_ffn_cn_w4': 8.0,
     'L0_ffn_gc_w1': 5.737,
     'L0_ffn_gc_w2': 2.697,
     'L0_ffn_gc_w3': 4.089}
    for name, (base, spread) in spreads.items():
        noise = np.random.default_rng([zlib.crc32(name.encode()), seed]).standard_normal(out[name].shape)
        drawn = base * np.exp(spread * noise) if base else spread * noise
        out[name] = jnp.asarray(drawn.astype(out[name].dtype))
    for name, factor in factors.items():
        out[name] = (out[name] * factor).astype(out[name].dtype)
    return out
```

```python
from contextlib import ExitStack

import numpy as np

import concourse.bass as bass
from concourse import mybir
from concourse.alu_op_type import AluOpType as ALU

F32 = mybir.dt.float32
F16 = mybir.dt.float16
I32 = mybir.dt.int32
ACT = mybir.ActivationFunctionType
AX = mybir.AxisListType

P = 128
B, S, D = 8, 1024, 512
H, DK, KEYS = 16, 32, 64
BLK = 512
NB = S // BLK
TPB = BLK // P
C = D // P
HPC = P // DK
PAIRS = H // 2
D2, D3 = D // 2, D // 4
C2 = D2 // P
WSCALE = 64.0
EPS = 1e-5
TWO_PI_HI = 6.28125
TWO_PI_LO = 2 * np.pi - 6.28125
HI, LO = 0, 1
FT = 3
KV = C * HPC * KEYS + PAIRS * 2 * DK


class Stream:

    def __init__(self, name, sems, credit):
        self.name, self.sems, self.credit = name, sems, credit
        self.ops, self.at, self.count, self.done_cost = [], {}, {}, 0.0

    def op(self, engine, name, waits, emit, cost=0.0, dma=None):
        key = dma or engine
        self.count[key] = self.count.get(key, 0) + 1
        assert name not in self.at, name
        self.at[name] = (key, self.count[key])
        self.ops.append((engine, name, waits, emit, cost, dma))

    def earlier(self, fmt, n, gap, total):
        return (self, fmt.format(n - gap), 0) if n >= gap else (self, fmt.format(n - gap + total), 1)


class Ring:

    def __init__(self, stream, size):
        self.stream, self.size, self.uses = stream, size, []

    def take(self, readers):
        n = len(self.uses)
        waits = [(self.stream, r, 0) for r in self.uses[n - self.size][0]] if n >= self.size else []
        self.uses.append((readers, waits))
        return n % self.size, waits

    def close(self):
        assert len(self.uses) % self.size == 0, len(self.uses)
        for n in range(self.size):
            readers = self.uses[len(self.uses) - self.size + n][0]
            self.uses[n][1].extend((self.stream, r, 1) for r in readers)


def issue(eng, stream, step, offset, op, seen):
    _, _, waits, emit, _, dma = op
    for w in waits:
        src, what, back = w if isinstance(w, tuple) else (stream, w, 0)
        if step is None and offset < back:
            continue
        key, n = src.at[what]
        per = src.count[key]
        unit = 1 if key in ENGINES else 16
        value = (offset - back + src.credit) * per + n
        if seen.get((src.name, key), -1 << 30) >= value:
            continue
        seen[(src.name, key)] = value
        value *= unit
        eng.wait_ge(src.sems[key], value if step is None else step * (per * unit) + value)
        if step is not None and apart(op):
            eng.sem_inc(stream.sems["apart"], 1)
    batch = offset if step is None else (step + offset if offset else step)
    emit(eng, batch).then_inc(stream.sems[dma or op[0]], 16 if dma else 1)


def apart(op):
    return op[0] == "sync" or op[1].startswith(("mv1", "mv2", "tb", "keep0", "keep1"))


ENGINES = ("tensor", "scalar", "vector", "gpsimd", "sync")


def weave(first, second):
    merged, heads = [], []
    for offset, stream in (first, second):
        total = sum(o[4] for o in stream.ops) or 1.0
        run = 0.0
        for n, o in enumerate(stream.ops):
            merged.append((run / total, len(heads), n, offset, stream, o))
            run += o[4]
        heads.append(stream)
    merged.sort(key=lambda m: m[:3])
    return [(m[3], m[4], m[5]) for m in merged]


def passes(parts_a, parts_b):
    return ((parts_a[HI], parts_b[HI]), (parts_a[HI], parts_b[LO]), (parts_a[LO], parts_b[HI]))


def program(nc, x, ctxT, wq, bq, wk, bk, wvT, bv, woT, bo, phase, cw1, cb1, cw2, cb2, cw3, cb3, cw4, cb4,
            gw1, gb1, gw2, gb2, gw3, gb3, arange, ident_in, turn_in, headsel_in, out):
    kv_dram = nc.dram_tensor("kv_blocks", (B, P, 2 * KV), F16).ap()
    with ExitStack() as ctx:
        def sb(name, shape, dt=F32, stack=ctx):
            return stack.enter_context(nc.sbuf_tensor(name, shape, dt))

        def sem(name):
            return ctx.enter_context(nc.semaphore(name))

        WQ = sb("WQ", [P, 2, C, D], F16)
        WO = sb("WO", [P, 2, C, D], F16)
        W1 = sb("W1", [P, 2, C + 2, D], F16)
        W2 = sb("W2", [P, 2, C, D2], F16)
        W3 = sb("W3", [P, 2, C2, D3], F16)
        W4 = sb("W4", [P, 2, P], F16)
        G1 = sb("G1", [P, 2, C, D2], F16)
        G2 = sb("G2", [P, 2, C2, D3], F16)
        G3 = sb("G3", [P, 2, P], F16)
        ident = sb("ident", [P, P])
        bo_rows = sb("bo_rows", [P, D])
        bq_col = sb("bq_col", [P, C])
        b1_col = sb("b1_col", [P, C])
        b2_col = sb("b2_col", [P, C2])
        b3_col = sb("b3_col", [P, 1])
        gb1_col = sb("gb1_col", [P, C2])
        gb2_col = sb("gb2_col", [P, 1])
        scal = sb("scal", [P, 5])
        minus_half = sb("minus_half", [P, TPB])

        names = ["tensor", "scalar", "vector", "gpsimd"]
        kv_stored = [sem(f"kv_stored{b}") for b in range(B)]
        attn_sems = {e: sem(f"attn_{e}") for e in names}
        attn_sems.update({f"x_loaded{b}": sem(f"x_loaded{b}") for b in range(NB)})
        attn_sems["kv_loaded"] = sem("kv_loaded")
        ffn_sems = {e: sem(f"ffn_{e}") for e in names}
        ffn_sems.update({f"stored{b}": sem(f"stored{b}") for b in range(2)})
        attn_sems["apart"] = ffn_sems["apart"] = sem("apart")
        A = Stream("attn", attn_sems, 0)
        F = Stream("ffn", ffn_sems, 1)

        setup(nc, sem, dict(
            kv_stored=kv_stored, kv_dram=kv_dram, ctxT=ctxT, wq=wq, bq=bq, wk=wk, bk=bk, wvT=wvT, bv=bv, woT=woT,
            bo=bo, phase=phase, cw1=cw1, cb1=cb1, cw2=cw2, cb2=cb2, cw3=cw3, cb3=cb3, cw4=cw4, cb4=cb4, gw1=gw1,
            gb1=gb1, gw2=gw2, gb2=gb2, gw3=gw3, gb3=gb3, arange=arange, ident_in=ident_in, turn_in=turn_in,
            headsel_in=headsel_in, WQ=WQ, WO=WO, W1=W1, W2=W2, W3=W3, W4=W4, G1=G1, G2=G2, G3=G3, ident=ident,
            bo_rows=bo_rows, bq_col=bq_col, b1_col=b1_col, b2_col=b2_col, b3_col=b3_col, gb1_col=gb1_col,
            gb2_col=gb2_col, scal=scal, minus_half=minus_half))

        kvb = sb("kvb", [P, 2, KV], F16)
        kb = [kvb[:, p, 0:C * HPC * KEYS].rearrange("p (c n) -> p c n", c=C) for p in (HI, LO)]
        vb = [kvb[:, p, C * HPC * KEYS:KV].rearrange("p (r n) -> p r n", r=PAIRS) for p in (HI, LO)]
        xin = sb("xin", [P, NB, TPB, D])
        x1p = sb("x1p", [P, NB, TPB, D])
        xn = sb("xn", [P, TPB, D])
        xoT = sb("xoT", [P, 2, C, BLK], F16)
        qT = sb("qT", [P, 2, C, BLK], F16)
        prob = sb("prob", [P, TPB, H * KEYS])
        pT = sb("pT", [P, 2, PAIRS, BLK], F16)
        x2T = sb("x2T", [P, NB, 2, C, BLK], F16)
        Y0 = sb("Y0", [P, C, BLK])
        Y1 = sb("Y1", [P, C, BLK])
        ft = sb("ft", [P, FT, BLK])
        h1 = sb("h1", [P, 2, C, BLK], F16)
        h2 = sb("h2", [P, 2, C2, BLK], F16)
        h3 = sb("h3", [P, 2, BLK], F16)
        cpl = sb("cpl", [P, BLK])
        c1 = sb("c1", [P, BLK])
        a2 = sb("a2", [P, BLK])
        b2 = sb("b2", [P, BLK])
        ot = sb("ot", [P, 2, D])
        stat = sb("stat", [P, NB, TPB, 6])
        mv1 = sb("mv1", [P, NB, TPB, 2])
        mv2 = sb("mv2", [P, NB, TPB, 2])
        ve = sb("ve", [P, NB, TPB])
        rs1 = sb("rs1", [P, NB, TPB])
        nm1 = sb("nm1", [P, NB, TPB])
        rs2 = sb("rs2", [P, NB, TPB])
        nm2 = sb("nm2", [P, NB, TPB])
        rs2p = sb("rs2p", [P, NB, TPB])
        nm2p = sb("nm2p", [P, NB, TPB])
        gs = sb("gs", [P, NB, C])
        mx = sb("mx", [P, TPB, H])
        sm = sb("sm", [P, TPB, H])
        rc = sb("rc", [P, TPB, H])
        gm = sb("gm", [P, C])
        gmh = sb("gmh", [P, 2, C], F16)
        g1 = sb("g1", [P, C2])
        g1h = sb("g1h", [P, 2, C2], F16)
        g2 = sb("g2", [P, 1])
        g2h = sb("g2h", [P, 2, 1], F16)
        gt = sb("gt", [P, 1])
        alpha = sb("alpha", [P, 1])
        ab = sb("ab", [P, 2, TPB])
        an = sb("an", [P, 2, TPB])
        co = sb("co", [P, 5, TPB])

        psS = ctx.enter_context(nc.psum_tensor("psS", [P, H * KEYS], F32))
        psA = ctx.enter_context(nc.psum_tensor("psA", [P, 2, BLK], F32))
        psF = ctx.enter_context(nc.psum_tensor("psF", [P, 4, BLK], F32))

        ringA, ringF, ringT, ringO = Ring(A, 2), Ring(F, 4), Ring(F, FT), Ring(F, 2)
        x_dram = x.rearrange("b (k p j) d -> b k p (j d)", k=NB, j=TPB)
        out_dram = out.rearrange("b (k p j) d -> b k p (j d)", k=NB, j=TPB)
        cols = lambda j: slice(j * P, (j + 1) * P)

        def batch_of(dram, batch):
            return dram[batch] if isinstance(batch, int) else dram[bass.ds(batch, 1)].squeeze(0)

        def load(k):
            A.op("sync", f"load{k}", [(F, f"keep{k}", 1)], lambda e, b: e.dma_start(
                xin[:, k].rearrange("p j d -> p (j d)"), batch_of(x_dram, b)[k]), dma=f"x_loaded{k}")

        def load_kv():
            A.op("sync", "kv", [(A, "s7", 1), (A, f"pv{NB - 1}_{C - 1}", 1)], lambda e, b: e.dma_start(
                kvb[:].rearrange("p a n -> p (a n)"), batch_of(kv_dram, b)), dma="kv_loaded")

        def norm_rows(k, tag, ready, mv, rs, nm, guard):
            for j in range(TPB):
                A.op("vector", f"st{tag}{k}_{j}", ready(j) + [(A, f"mv{'2' if tag == '1' else '1'}{k}_{j}", 1 if tag == "1" else 0)],
                     lambda e, b, j=j: e.bn_stats(stat[:, k, j], xin[:, k, j]))
            for j in range(TPB):
                A.op("vector", f"mv{tag}{k}_{j}", [f"st{tag}{k}_{j}"] + guard,
                     lambda e, b, j=j: e.bn_aggr(mv[:, k, j], stat[:, k, j]))
            other = (A, f"rs2{k}", 1) if tag == "1" else (A, f"rs1{k}", 0)
            A.op("vector", f"ve{tag}{k}", [f"mv{tag}{k}_{TPB - 1}", other], lambda e, b: e.tensor_scalar(
                ve[:, k], mv[:, k, :, 1], EPS, None, ALU.add))
            A.op("gpsimd", f"rs{tag}{k}", [f"ve{tag}{k}"] + guard, lambda e, b: e.tensor_tensor(
                rs[:, k], ve[:, k], minus_half[:], ALU.pow))
            A.op("vector", f"nm{tag}{k}", [f"rs{tag}{k}"], lambda e, b: e.scalar_tensor_tensor(
                nm[:, k], mv[:, k, :, 0], -1.0, rs[:, k], ALU.mult, ALU.mult))

        turns = {("1", 0): ("tr21_3", 1), ("1", 1): ("tr10_3", 0), ("2", 0): ("tr11_3", 0), ("2", 1): ("tr20_3", 0)}

        def rows_out(k, tag, rs, nm):
            last, back = turns[tag, k]
            for j in range(TPB):
                A.op("scalar", f"xn{tag}{k}_{j}", [f"nm{tag}{k}", (A, last, back)], lambda e, b, j=j: e.activation(
                    xn[:, j], xin[:, k, j], ACT.Identity, bias=nm[:, k, j:j + 1], scale=rs[:, k, j:j + 1]))

        def turn_rows(k, tag, c, dst, readers, sums=None):
            hi, lo = f"xh{tag}{k}_{c}", f"xl{tag}{k}_{c}"
            bank, waits = ringA.take([hi, lo])

            def turn(e, b):
                for j in range(TPB):
                    mm = e.transpose(psA[:, bank, cols(j)], xn[:, j, cols(c)], ident[:])
                return mm
            A.op("tensor", f"tr{tag}{k}_{c}", waits_first(waits, [f"xn{tag}{k}_{j}" for j in range(TPB)]), turn, 0.44)
            A.op("scalar", hi, [f"tr{tag}{k}_{c}"] + readers, lambda e, b: e.activation(
                dst[HI][:, c], psA[:, bank], ACT.Copy, accum_out=sums) if sums is not None else e.activation(
                dst[HI][:, c], psA[:, bank], ACT.Copy))
            A.op("vector", lo, [hi], lambda e, b: e.tensor_tensor(
                dst[LO][:, c], psA[:, bank], dst[HI][:, c], ALU.subtract))

        def waits_first(waits, more):
            waits.extend(more)
            return waits

        def queries(k, m):
            hi, lo = f"qh{k}_{m}", f"ql{k}_{m}"
            bank, waits = ringA.take([hi, lo])

            def mul(e, b):
                n = 0
                for c in range(C):
                    for w, v in passes([WQ[:, p, c, cols(m)] for p in (HI, LO)], [xoT[:, p, c] for p in (HI, LO)]):
                        mm = e.matmul(psA[:, bank], w, v, start=(n == 0), stop=(n == 3 * C - 1))
                        n += 1
                return mm
            A.op("tensor", f"q{k}_{m}", waits_first(waits, [f"xl1{k}_{c}" for c in range(C)]), mul, 2.6)
            free = A.earlier("s{}", TPB * k + TPB - 1, TPB, NB * TPB)
            A.op("scalar", hi, [f"q{k}_{m}", free], lambda e, b: e.activation(
                qT[:, HI, m], psA[:, bank], ACT.Identity, bias=bq_col[:, m:m + 1]))
            A.op("vector", lo, [hi], lambda e, b: e.scalar_tensor_tensor(
                qT[:, LO, m], psA[:, bank], bq_col[:, m:m + 1], qT[:, HI, m], ALU.add, ALU.subtract))

        def scores(t):
            k, j = divmod(t, TPB)
            T = NB * TPB

            def mul(e, b):
                for c in range(C):
                    for n, (w, v) in enumerate(passes([qT[:, p, c, cols(j)] for p in (HI, LO)], [kb[p][:, c] for p in (HI, LO)])):
                        mm = e.matmul(psS[:, c * HPC * KEYS:(c + 1) * HPC * KEYS], w, v, start=(n == 0), stop=(n == 2))
                return mm
            A.op("tensor", f"s{t}", [f"ql{k}_{m}" for m in range(C)] + ["kv", A.earlier("sub{}", t, 1, T)], mul, 1.3)
            by_head = lambda a: a.rearrange("p (h n) -> p h n", h=H)
            wide = lambda a: a.unsqueeze(2).to_broadcast([P, H, KEYS])
            A.op("vector", f"max{t}", [f"s{t}", A.earlier("sub{}", t, TPB, T)], lambda e, b: e.tensor_reduce(
                mx[:, j], by_head(psS[:]), AX.X, ALU.max))
            A.op("vector", f"sub{t}", [f"max{t}", A.earlier("pt{}_1", t, TPB, T)], lambda e, b: e.tensor_tensor(
                by_head(prob[:, j]), by_head(psS[:]), wide(mx[:, j]), ALU.subtract))
            A.op("scalar", f"exp{t}", [f"sub{t}"], lambda e, b: e.activation(
                prob[:, j], prob[:, j], ACT.Exp, scale=1.0 / (WSCALE * DK ** 0.5)))
            A.op("vector", f"sum{t}", [f"exp{t}", A.earlier("rec{}", t, TPB, T)], lambda e, b: e.tensor_reduce(
                sm[:, j], by_head(prob[:, j]), AX.X, ALU.add))
            A.op("vector", f"rec{t}", [f"sum{t}", A.earlier("nrm{}", t, TPB, T)], lambda e, b: e.reciprocal(rc[:, j], sm[:, j]))
            A.op("gpsimd", f"nrm{t}", [f"rec{t}"], lambda e, b: e.tensor_tensor(
                by_head(prob[:, j]), by_head(prob[:, j]), wide(rc[:, j]), ALU.mult))

        def turn_probs(t):
            k, j = divmod(t, TPB)
            for g in range(2):
                hi, lo = f"ph{t}_{g}", f"pl{t}_{g}"
                bank, waits = ringA.take([hi, lo])
                pairs = slice(4 * g, 4 * g + 4)

                def turn(e, b, g=g, bank=bank):
                    for r in range(4):
                        mm = e.transpose(psA[:, bank, cols(r)], prob[:, j, cols(4 * g + r)], ident[:])
                    return mm
                A.op("tensor", f"pt{t}_{g}", waits_first(waits, [f"nrm{t}"]), turn, 0.44)
                free = (A, f"pv{0}_{C - 1}", 0) if k else (A, f"pv{NB - 1}_{C - 1}", 1)
                four = lambda a: a.rearrange("p (r n) -> p r n", r=4)
                A.op("scalar", hi, [f"pt{t}_{g}", free], lambda e, b, bank=bank, pairs=pairs: e.activation(
                    pT[:, HI, pairs, cols(j)], four(psA[:, bank]), ACT.Copy))
                A.op("vector", lo, [hi], lambda e, b, bank=bank, pairs=pairs: e.tensor_tensor(
                    pT[:, LO, pairs, cols(j)], four(psA[:, bank]), pT[:, HI, pairs, cols(j)], ALU.subtract))

        def values(k, c):
            hi, lo = f"oh{k}_{c}", f"ol{k}_{c}"
            bank, waits = ringA.take([hi, lo])

            def mul(e, b):
                for n in range(3):
                    for half in range(2):
                        r = 2 * c + half
                        w, v = passes([vb[p][:, r] for p in (HI, LO)], [pT[:, p, r] for p in (HI, LO)])[n]
                        mm = e.matmul(psA[64 * half:64 * half + 64, bank], w, v, start=(n == 0), stop=(n == 2))
                return mm
            ready = [f"pl{TPB * k + j}_{g}" for j in range(TPB) for g in range(2)]
            A.op("tensor", f"pv{k}_{c}", waits_first(waits, ready), mul, 0.75)
            free = [f"q{NB - 1}_{C - 1}"] if k == 0 else [f"wo{TPB - 1}"]
            A.op("scalar", hi, [f"pv{k}_{c}"] + free, lambda e, b: e.activation(xoT[:, HI, c], psA[:, bank], ACT.Copy))
            A.op("vector", lo, [hi], lambda e, b: e.tensor_tensor(xoT[:, LO, c], psA[:, bank], xoT[:, HI, c], ALU.subtract))

        def project(t):
            k, j = divmod(t, TPB)
            bank, waits = ringA.take([f"res{t}"])

            def mul(e, b):
                n = 0
                for c in range(C):
                    for w, v in passes([xoT[:, p, c, cols(j)] for p in (HI, LO)], [WO[:, p, c] for p in (HI, LO)]):
                        mm = e.matmul(psA[:, bank], w, v, start=(n == 0), stop=(n == 3 * C - 1))
                        n += 1
                return mm
            A.op("tensor", f"wo{t}", waits_first(waits, [f"ol{k}_{c}" for c in range(C)]), mul, 2.6)
            A.op("vector", f"res{t}", [f"wo{t}", f"xb{t}"], lambda e, b: e.scalar_tensor_tensor(
                xin[:, k, j], psA[:, bank], 1.0 / WSCALE, xin[:, k, j], ALU.mult, ALU.add))

        def first_rows(k):
            norm_rows(k, "1", lambda j: [f"load{k}"], mv1, rs1, nm1, [(A, f"nm1{k}", 1)])
            rows_out(k, "1", rs1, nm1)
            for j in range(TPB):
                A.op("gpsimd", f"xb{TPB * k + j}", [f"xn1{k}_{j}", f"st1{k}_{j}"], lambda e, b, j=j: e.tensor_tensor(
                    xin[:, k, j], xin[:, k, j], bo_rows[:], ALU.add))

        def second_rows(k):
            norm_rows(k, "2", lambda j: [f"res{TPB * k + j}"], mv2, rs2, nm2, [(F, "keep_stats", 1)])
            rows_out(k, "2", rs2, nm2)

        def second_turn(k, c):
            turn_rows(k, "2", c, [x2T[:, k, HI], x2T[:, k, LO]], [(F, f"y1{k}_{C - 1}", 1), (F, "gsum", 1)],
                      sums=gs[:, k, c:c + 1])

        def first_turn(k, c):
            free = [f"q0_{C - 1}"] if k else [(A, f"wo{NB * TPB - 1}", 1)]
            turn_rows(k, "1", c, [xoT[:, HI], xoT[:, LO]], free)

        load(0)
        load(1)
        load_kv()
        first_rows(0)
        for c in range(C):
            first_turn(0, c)
        for m in range(C):
            queries(0, m)
        first_rows(1)
        scores(0)
        scores(1)
        first_turn(1, 0)
        first_turn(1, 1)
        scores(2)
        first_turn(1, 2)
        first_turn(1, 3)
        scores(3)
        for m in range(C):
            queries(1, m)
        turn_probs(0)
        turn_probs(1)
        scores(4)
        turn_probs(2)
        turn_probs(3)
        scores(5)
        for c in range(C):
            values(0, c)
        scores(6)
        project(0)
        project(1)
        scores(7)
        project(2)
        project(3)
        turn_probs(4)
        turn_probs(5)
        second_rows(0)
        for c in range(C):
            second_turn(0, c)
        turn_probs(6)
        turn_probs(7)
        for c in range(C):
            values(1, c)
        for t in range(TPB, NB * TPB):
            project(t)
        second_rows(1)
        for c in range(C):
            second_turn(1, c)
        ringA.close()

        def keep(k):
            F.op("gpsimd", f"keep{k}", [(A, f"res{TPB * k + TPB - 1}", 0), (A, f"xn2{k}_{TPB - 1}", 0),
                                       (A, f"mv2{k}_{TPB - 1}", 0), (F, f"out{NB - 1}_{TPB - 1}", 1)],
                 lambda e, b: e.tensor_scalar(x1p[:, k], xin[:, k], 1.0, None, ALU.mult))

        def keep_stats():
            ready = [(A, f"xn2{NB - 1}_{TPB - 1}", 0), (A, f"nm2{NB - 1}", 0), (F, f"coef{NB - 1}", 1)]
            F.op("vector", "keep_rs", ready, lambda e, b: e.tensor_copy(rs2p[:], rs2[:]))
            F.op("vector", "keep_stats", [(F, f"coef{NB - 1}", 1)], lambda e, b: e.tensor_copy(nm2p[:], nm2[:]))

        def split(src, dst, name, ready, free):
            F.op("vector", f"{name}h", ready + free, lambda e, b: e.tensor_copy(dst[HI], src))
            F.op("vector", f"{name}l", [f"{name}h"], lambda e, b: e.tensor_tensor(dst[LO], src, dst[HI], ALU.subtract))

        def global_context():
            F.op("vector", "gsum", [(A, f"xh2{NB - 1}_{C - 1}", 0), (F, "gml", 1)], lambda e, b: e.tensor_tensor(
                gm[:], gs[:, 0], gs[:, 1], ALU.add))
            F.op("vector", "gmh", ["gsum", (F, "gz1", 1)], lambda e, b: e.tensor_scalar(
                gmh[:, HI], gm[:], WSCALE / S, None, ALU.mult))
            F.op("vector", "gml", ["gmh"], lambda e, b: e.scalar_tensor_tensor(
                gmh[:, LO], gm[:], WSCALE / S, gmh[:, HI], ALU.mult, ALU.subtract))

            def small(name, w, src, n_out, n_in, ready, place, at=0):
                bank, waits = place

                def mul(e, b):
                    for m in range(n_out):
                        n = 0
                        for c in range(n_in):
                            for a, v in passes([w(p, c, m) for p in (HI, LO)], [src[:, p, c:c + 1] for p in (HI, LO)]):
                                mm = e.matmul(psF[:, bank, at + m:at + m + 1], a, v, start=(n == 0), stop=(n == 3 * n_in - 1))
                                n += 1
                    return mm
                F.op("tensor", name, waits_first(waits, ready), mul, 0.3)
                return bank
            bank1 = small("gz1", lambda p, c, m: G1[:, p, c, cols(m)], gmh, C2, C, ["gml"],
                          ringF.take(["gb1"]))
            F.op("vector", "gb1", ["gz1", (F, "gg1", 1), (F, "g1l", 1)], lambda e, b: e.scalar_tensor_tensor(
                g1[:], psF[:, bank1, 0:C2], WSCALE ** -2, gb1_col[:], ALU.mult, ALU.add))
            F.op("scalar", "gg1", ["gb1"], lambda e, b: e.activation(g1[:], g1[:], ACT.Gelu))
            split(g1[:], [g1h[:, HI], g1h[:, LO]], "g1", ["gg1"], [(F, "gz2", 1)])
            bank2 = small("gz2", lambda p, c, m: G2[:, p, c], g1h, 1, C2, ["g1l"],
                          ringF.take(["gg2", "gt"]))
            F.op("scalar", "gg2", ["gz2", (F, "g2l", 1)], lambda e, b: e.activation(
                g2[:], psF[:, bank2, 0:1], ACT.Gelu, bias=gb2_col[:], scale=1.0 / WSCALE))
            split(g2[:], [g2h[:, HI], g2h[:, LO]], "g2", ["gg2"], [(F, "gz3", 1)])
            bank3 = small("gz3", lambda p, c, m: G3[:, p], g2h, 1, 1, ["g2l"], (bank2, []), at=1)
            F.op("scalar", "gt", ["gz3", (F, "alpha", 1)], lambda e, b: e.activation(
                gt[:], psF[:, bank3, 1:2], ACT.Tanh, bias=scal[:, 2:3], scale=0.5 / WSCALE))
            F.op("vector", "alpha", ["gt", (F, f"cc{NB - 1}_2", 1)], lambda e, b: e.tensor_scalar(
                alpha[:], gt[:], scal[:, 4:5], 0.1, ALU.mult, ALU.add))

        def first_products(k, m):
            for name, order, dst in (("y0", ((0, 0), (1, 1), (2, 2), (3, 3)), Y0),
                                     ("y1", ((0, 2), (4, 3), (5, 0), (3, 1)), Y1)):
                copy = f"{name}c{k}_{m}"
                bank, waits = ringF.take([copy, f"g{k}_0_{m}"] if name == "y0" else [copy])

                def mul(e, b, order=order, bank=bank):
                    n = 0
                    for wc, xc in order:
                        for w, v in passes([W1[:, p, wc, cols(m)] for p in (HI, LO)], [x2T[:, k, p, xc] for p in (HI, LO)]):
                            mm = e.matmul(psF[:, bank], w, v, start=(n == 0), stop=(n == 3 * C - 1))
                            n += 1
                    return mm
                F.op("tensor", f"{name}{k}_{m}", waits_first(waits, [(A, f"xl2{k}_{C - 1}", 0), (A, f"xh2{k}_{C - 1}", 0)]), mul, 1.6)
                if name == "y0":
                    first_activation(k, 0, m, psF[:, bank], 1.0 / WSCALE, [f"y0{k}_{m}"])
                free = F.earlier("pre{}_2_" + str(m), k, 1, NB)
                F.op("scalar", copy, [f"{name}{k}_{m}", free], lambda e, b, bank=bank, dst=dst: e.activation(
                    dst[:, m], psF[:, bank], ACT.Copy, scale=1.0 / WSCALE))

        def activate(name, src, slot, bias, scale, ready, dst, free, cost=0.0):
            F.op("scalar", f"g{name}", ready, lambda e, b: e.activation(
                ft[:, slot], src, ACT.Gelu, bias=bias, scale=scale), cost)
            split(ft[:, slot], dst, f"h{name}", [f"g{name}"], free)

        def first_activation(k, y, m, src, scale, ready, slot=None):
            if slot is None:
                slot, waits = ringT.take([f"h{k}_{y}_{m}l"])
                ready = waits_first(waits, ready)
            prev = F.earlier("l2{}_1", 3 * k + y, 1, 3 * NB)
            activate(f"{k}_{y}_{m}", src, slot, b1_col[:, m:m + 1], scale, ready,
                     [h1[:, HI, m], h1[:, LO, m]], [prev])

        def combine(k, y, m):
            slot, waits = ringT.take([f"h{k}_{y}_{m}l"])
            u, v = f"mul{k}_{y}_{m}", f"pre{k}_{y}_{m}"
            F.op("vector", u, waits_first(waits, [f"y1c{k}_{m}", f"cc{k}_0" if y == 1 else f"b2_{k}"]), lambda e, b: e.tensor_tensor(
                ft[:, slot], Y1[:, m], c1[:] if y == 1 else b2[:], ALU.mult))
            if y == 2:
                F.op("gpsimd", f"am{k}_{m}", [f"a2_{k}"] + [f"pre{k}_1_{m}"], lambda e, b: e.tensor_tensor(
                    Y0[:, m], Y0[:, m], a2[:], ALU.mult))
            F.op("vector", v, [u] + ([f"am{k}_{m}"] if y == 2 else []) + [f"y1c{k}_{m}"], lambda e, b: e.tensor_tensor(
                ft[:, slot], ft[:, slot], Y0[:, m], ALU.add))
            first_activation(k, y, m, ft[:, slot], 1.0, [v], slot)

        def later_layers(k, y):
            i, N = 3 * k + y, 3 * NB
            for m in range(C2):
                name = f"{i}_{m}"
                bank, waits = ringF.take([f"gb{name}"])

                def mul(e, b, m=m, bank=bank):
                    n = 0
                    for c in range(C):
                        for w, v in passes([W2[:, p, c, cols(m)] for p in (HI, LO)], [h1[:, p, c] for p in (HI, LO)]):
                            mm = e.matmul(psF[:, bank], w, v, start=(n == 0), stop=(n == 3 * C - 1))
                            n += 1
                    return mm
                F.op("tensor", f"l2{name}", waits_first(waits, [f"h{k}_{y}_{c}l" for c in range(C)]), mul, 4.0)
                slot, waits = ringT.take([f"hb{name}l"])
                activate(f"b{name}", psF[:, bank], slot, b2_col[:, m:m + 1], 1.0 / WSCALE,
                         waits_first(waits, [f"l2{name}"]), [h2[:, HI, m], h2[:, LO, m]], [F.earlier("l3{}", i, 1, N)])
            bank, waits = ringF.take([f"gc{i}"])

            def mul3(e, b, bank=bank):
                for c in range(C2):
                    for n, (w, v) in enumerate(passes([W3[:, p, c] for p in (HI, LO)], [h2[:, p, c] for p in (HI, LO)])):
                        mm = e.matmul(psF[:, bank], w, v, start=(n + c == 0), stop=(n + c == C2 + 1))
                return mm
            F.op("tensor", f"l3{i}", waits_first(waits, [f"hb{i}_{m}l" for m in range(C2)]), mul3, 4.0)
            slot, waits = ringT.take([f"hc{i}l"])
            activate(f"c{i}", psF[:, bank], slot, b3_col[:], 1.0 / WSCALE, waits_first(waits, [f"l3{i}"]),
                     [h3[:, HI], h3[:, LO]], [F.earlier("l4{}", i, 1, N)])
            bank, waits = ringF.take([f"u{i}"])

            def mul4(e, b, bank=bank):
                for n, (w, v) in enumerate(passes([W4[:, p] for p in (HI, LO)], [h3[:, p] for p in (HI, LO)])):
                    mm = e.matmul(psF[:, bank], w, v, start=(n == 0), stop=(n == 2))
                return mm
            F.op("tensor", f"l4{i}", waits_first(waits, [f"hc{i}l"]), mul4, 4.0)
            last = F.earlier({0: "tb{}", 1: "cc{}_0", 2: "b2_{}"}[y], k, 1 if y == 0 else 0, NB)
            dst = c1 if y == 0 else cpl
            F.op("scalar", f"u{i}", [f"l4{i}", last] + ([f"a2_{k}", f"b2_{k}"] if y == 2 else []),
                 lambda e, b: e.activation(dst[:], psF[:, bank], ACT.Tanh, bias=scal[:, 1:2], scale=0.5 / WSCALE))
            F.op("vector", f"cc{k}_{y}", [f"u{i}", "alpha"], lambda e, b: e.tensor_scalar(
                dst[:], dst[:], scal[:, 3:4], alpha[:], ALU.mult, ALU.add), 1.0)

        def second_factor(k):
            F.op("vector", f"b2_{k}", [f"cc{k}_1", F.earlier("b3_{}", k, 1, NB)], lambda e, b: e.tensor_tensor(
                b2[:], c1[:], cpl[:], ALU.add))
            F.op("vector", f"cc12_{k}", [f"cc{k}_1", F.earlier("b3_{}", k, 1, NB)], lambda e, b: e.tensor_tensor(
                a2[:], c1[:], cpl[:], ALU.mult))
            F.op("vector", f"a2_{k}", [f"cc12_{k}"], lambda e, b: e.tensor_scalar(
                a2[:], a2[:], -1.0, 1.0, ALU.mult, ALU.add))

        def finish(k):
            row = slice(0, 1)
            F.op("vector", f"m1_{k}", [f"cc{k}_2", f"pre{k}_1_{C - 1}"], lambda e, b: e.tensor_tensor(
                c1[row], cpl[row], b2[row], ALU.mult))
            F.op("vector", f"m2_{k}", [f"m1_{k}"], lambda e, b: e.tensor_tensor(cpl[row], cpl[row], a2[row], ALU.mult))
            F.op("vector", f"a3_{k}", [f"m1_{k}"], lambda e, b: e.tensor_tensor(c1[row], a2[row], c1[row], ALU.subtract))
            F.op("vector", f"b3_{k}", [f"m2_{k}"], lambda e, b: e.tensor_tensor(cpl[row], b2[row], cpl[row], ALU.add))
            bank, waits = ringF.take([f"ar{k}", f"coef0{k}"])

            def turn(e, b):
                for n, src in enumerate((c1, cpl)):
                    for j in range(TPB):
                        mm = e.transpose(psF[:, bank, n * TPB + j:n * TPB + j + 1], src[row, cols(j)], ident[row, 0:1])
                return mm
            F.op("tensor", f"tb{k}", waits_first(waits, [f"a3_{k}", f"b3_{k}"]), turn, 1.0)
            prev = F.earlier("coef{}", k, 1, NB)
            F.op("vector", f"ar{k}", [f"tb{k}", "keep_rs", prev], lambda e, b: e.tensor_tensor(
                ab[:], psF[:, bank, 0:2 * TPB].rearrange("p (n j) -> p n j", n=2),
                rs2p[:, k].unsqueeze(1).to_broadcast([P, 2, TPB]), ALU.mult))
            done = [F.earlier("t{}_" + f"{TPB - 1}b", k, 1, NB), F.earlier("out{}_" + str(TPB - 1), k, 1, NB)]
            F.op("vector", f"co0{k}", [f"ar{k}"] + done, lambda e, b: e.tensor_scalar(co[:, 0], ab[:, 0], 1.0, None, ALU.add))
            F.op("vector", f"co1{k}", done, lambda e, b: e.tensor_copy(co[:, 1], ab[:, 1]))
            F.op("vector", f"co2{k}", done, lambda e, b: e.tensor_scalar(co[:, 2], ab[:, 1], -1.0, None, ALU.mult))
            F.op("vector", f"coef0{k}", [f"ar{k}", "keep_stats"], lambda e, b: e.tensor_tensor(
                an[:], psF[:, bank, 0:2 * TPB].rearrange("p (n j) -> p n j", n=2),
                nm2p[:, k].unsqueeze(1).to_broadcast([P, 2, TPB]), ALU.mult), 0.5)
            F.op("vector", f"co3{k}", [f"coef0{k}"], lambda e, b: e.tensor_tensor(co[:, 3], an[:, 0], an[:, 1], ALU.add))
            F.op("vector", f"coef{k}", [f"coef0{k}"], lambda e, b: e.tensor_tensor(co[:, 4], an[:, 0], an[:, 1], ALU.subtract))
            chunk = lambda a: a.rearrange("p (c n) -> p c n", c=C)
            for j in range(TPB):
                slot, waits = ringO.take([f"store{k}_{j}"])
                dst, src = chunk(ot[:, slot]), chunk(x1p[:, k, j])
                F.op("scalar", f"t{k}_{j}a", waits_first(waits, [f"coef{k}", f"keep{k}"]), lambda e, b, dst=dst, src=src, j=j: e.activation(
                    dst[:, 0::3], src[:, 0::3], ACT.Identity, bias=co[:, 3, j:j + 1], scale=co[:, 0, j:j + 1]), 0.2)
                F.op("scalar", f"t{k}_{j}b", [], lambda e, b, dst=dst, src=src, j=j: e.activation(
                    dst[:, 1:3], src[:, 1:3], ACT.Identity, bias=co[:, 4, j:j + 1], scale=co[:, 0, j:j + 1]), 0.2)

                def add(e, b, dst=dst, src=src, j=j):
                    for to, of, sign in ((0, 2, 1), (3, 1, 1), (1, 3, 2), (2, 0, 2)):
                        ins = e.scalar_tensor_tensor(dst[:, to], src[:, of], co[:, sign, j:j + 1], dst[:, to], ALU.mult, ALU.add)
                    return ins
                F.op("vector", f"out{k}_{j}", [f"t{k}_{j}b"], add)
                F.op("sync", f"store{k}_{j}", [f"out{k}_{j}"], lambda e, b, slot=slot, j=j: e.dma_start(
                    batch_of(out_dram, b)[k][:, j * D:(j + 1) * D], ot[:, slot]), dma=f"stored{slot}")

        keep(0)
        keep(1)
        keep_stats()
        for k in range(NB):
            for m in range(C):
                first_products(k, m)
                if k == 0 and m == 0:
                    global_context()
            later_layers(k, 0)
            for m in range(C):
                combine(k, 1, m)
            later_layers(k, 1)
            second_factor(k)
            for m in range(C):
                combine(k, 2, m)
            later_layers(k, 2)
            finish(k)
        ringF.close()
        ringT.close()
        ringO.close()

        def run(step, parts):
            order = weave(*parts) if len(parts) == 2 else [(parts[0][0], parts[0][1], o) for o in parts[0][1].ops]

            def on(name, eng):
                seen = {}
                for offset, stream, op in order:
                    if op[0] == name:
                        issue(eng, stream, step, offset, op, seen)
            return on

        def engine_program(name, eng):
            if name == "sync":
                eng.wait_ge(kv_stored[0], 16)
            run(None, [(0, A)])(name, eng)
            if name == "sync":
                for b in range(1, B):
                    eng.wait_ge(kv_stored[b], 16)
            with eng.Fori(1, B) as i:
                run(i, [(-1, F), (0, A)])(name, eng)
            run(None, [(B - 1, F)])(name, eng)
            if name == "sync":
                for slot in range(2):
                    key = f"stored{slot}"
                    eng.wait_ge(F.sems[key], 16 * F.count[key] * (B + 1))

        with nc.Block() as credit:
            @credit.sync
            def _(eng):
                for key, n in F.count.items():
                    eng.sem_inc(F.sems[key], n * (1 if key in ENGINES else 16))

        with nc.Block() as main:
            @main.sync
            def _(eng):
                engine_program("sync", eng)

            @main.tensor
            def _(eng):
                engine_program("tensor", eng)

            @main.scalar
            def _(eng):
                engine_program("scalar", eng)

            @main.vector
            def _(eng):
                engine_program("vector", eng)

            @main.gpsimd
            def _(eng):
                engine_program("gpsimd", eng)


def setup(nc, sem, g):
    sems = {e: sem(f"setup_{e}") for e in ENGINES[:4]}
    W = Stream("setup", sems, 0)
    with ExitStack() as ctx:
        def sb(name, shape, dt=F32):
            return ctx.enter_context(nc.sbuf_tensor(name, shape, dt))

        wq_s, wk_s = sb("wq_s", [P, C, D]), sb("wk_s", [P, C, D])
        wv_s, wo_s, w1_s = sb("wv_s", [P, C, D]), sb("wo_s", [P, C, D]), sb("w1_s", [P, C, D])
        w2_s, w3_s, gw1_s, gw2_s = (sb("w2_s", [P, C, D2]), sb("w3_s", [P, C2, D3]), sb("gw1_s", [P, C, D2]),
                                    sb("gw2_s", [P, C2, D3]))
        last_s = sb("last_s", [P, 2])
        last64 = sb("last64", [P, 2])
        ctx_s = sb("ctx_s", [P, C, B, 2, KEYS])
        wkT = sb("wkT", [P, C, D])
        k32 = sb("k32", [P, C, B, KEYS])
        kv = sb("kv", [P, B, 2, KV], F16)
        turn = sb("turn", [P, P])
        headsel = sb("headsel", [P, C, H])
        phases = sb("phases", [P, H])
        picked = sb("picked", [P, C, H])
        ang = sb("ang", [P, 6, C])
        turns = sb("turns", [P, C], I32)
        rot = sb("rot", [P, C, P])
        b_s = sb("b_s", [P, 2, C])
        bk_col = sb("bk_col", [P, C])
        scal_s = sb("scal_s", [P, 3])
        ones = sb("ones", [P, P])
        bv_s = sb("bv_s", [1, D])
        ps = ctx.enter_context(nc.psum_tensor("ps_setup", [P, 8, BLK], F32))
        cols = lambda j: slice(j * P, (j + 1) * P)

        def load(name, dst, src):
            sems[f"in_{name}"] = sem(f"in_{name}")
            W.op("sync", name, [], lambda e, b: e.dma_start(dst, src), dma=f"in_{name}")
        by_chunk = lambda a: a.rearrange("(c p) n -> p c n", p=P)
        load("phase", phases[:], g["phase"].rearrange("h a b -> (a b) h").partition_broadcast(P))
        load("headsel", headsel[:].rearrange("p c h -> p (c h)"), g["headsel_in"])
        load("ident", g["ident"][:], g["ident_in"])
        load("turn", turn[:], g["turn_in"])
        load("wk", wk_s[:], by_chunk(g["wk"]))
        load("bq", b_s[:, 0], g["bq"])
        load("bk", b_s[:, 1], g["bk"])
        ctx_view = g["ctxT"].rearrange("(c p) b n -> p c b n", p=P)
        for twin in range(2):
            for c in range(C):
                load(f"ctx{twin}{c}", ctx_s[:, c, :, twin], ctx_view[:, c])
        load("wv", wv_s[:], by_chunk(g["wvT"]))
        load("bv", bv_s[:], g["bv"].rearrange("(a n) -> a n", a=1))
        load("wq", wq_s[:], by_chunk(g["wq"]))
        load("wo", wo_s[:], by_chunk(g["woT"]))
        load("bo", g["bo_rows"][:], g["bo"].rearrange("(a n) -> a n", a=1).partition_broadcast(P))
        load("w1", w1_s[:], by_chunk(g["cw1"]))
        load("b1", g["b1_col"][:], g["cb1"])
        load("w2", w2_s[:], by_chunk(g["cw2"]))
        load("b2", g["b2_col"][:], g["cb2"])
        load("w3", w3_s[:], by_chunk(g["cw3"]))
        load("b3", g["b3_col"][:], g["cb3"])
        load("w4", last_s[:, 0:1], g["cw4"])
        load("g3", last_s[:, 1:2], g["gw3"])
        load("g1", gw1_s[:], by_chunk(g["gw1"]))
        load("gb1", g["gb1_col"][:], g["gb1"])
        load("g2", gw2_s[:], by_chunk(g["gw2"]))
        load("gb2", g["gb2_col"][:], g["gb2"])
        for n, a in enumerate(("arange", "cb4", "gb3")):
            load(a, scal_s[:, n:n + 1], g[a].rearrange("(a n) -> a n", a=1).partition_broadcast(P))

        V, S_, G = "vector", "scalar", "gpsimd"
        W.op(G, "ones", [], lambda e, b: e.memset(ones[:], 1.0))
        W.op(G, "half", [], lambda e, b: e.memset(g["minus_half"][:], -0.5))
        W.op(V, "zero0", [], lambda e, b: e.memset(kv[:, 0:B // 2].bitcast(F32), 0.0))
        W.op(G, "zero1", [], lambda e, b: e.memset(kv[:, B // 2:B].bitcast(F32), 0.0))

        W.op(V, "pick", ["phase", "headsel"], lambda e, b: e.tensor_tensor(
            picked[:], headsel[:], phases[:].unsqueeze(1).to_broadcast([P, C, H]), ALU.mult))
        W.op(V, "ph", ["pick"], lambda e, b: e.tensor_reduce(ang[:, 0], picked[:], AX.X, ALU.add))
        W.op(V, "turns", ["ph"], lambda e, b: e.tensor_scalar(turns[:], ang[:, 0], 1 / (2 * np.pi), None, ALU.mult))
        W.op(V, "turnsf", ["turns"], lambda e, b: e.tensor_copy(ang[:, 1], turns[:]))
        W.op(V, "red1", ["turnsf"], lambda e, b: e.scalar_tensor_tensor(
            ang[:, 2], ang[:, 1], -TWO_PI_HI, ang[:, 0], ALU.mult, ALU.add))
        W.op(V, "red2", ["red1"], lambda e, b: e.scalar_tensor_tensor(
            ang[:, 2], ang[:, 1], -TWO_PI_LO, ang[:, 2], ALU.mult, ALU.add))
        W.op(V, "clamp", ["red2"], lambda e, b: e.tensor_scalar(
            ang[:, 2], ang[:, 2], -3.1415925, 3.1415925, ALU.max, ALU.min))
        W.op(S_, "sin", ["clamp"], lambda e, b: e.activation(ang[:, 3], ang[:, 2], ACT.Sin))
        W.op(S_, "sinh", ["clamp"], lambda e, b: e.activation(ang[:, 4], ang[:, 2], ACT.Sin, scale=0.5))
        W.op(V, "sq", ["sinh"], lambda e, b: e.tensor_tensor(ang[:, 5], ang[:, 4], ang[:, 4], ALU.mult))
        W.op(V, "cos", ["sq"], lambda e, b: e.tensor_scalar(ang[:, 5], ang[:, 5], -2.0, 1.0, ALU.mult, ALU.add))
        for c in range(C):
            W.op(V, f"rc{c}", ["cos", "ident"], lambda e, b, c=c: e.tensor_scalar(
                rot[:, c], g["ident"][:], ang[:, 5, c:c + 1], None, ALU.mult))
            W.op(V, f"rot{c}", [f"rc{c}", "sin", "turn"], lambda e, b, c=c: e.scalar_tensor_tensor(
                rot[:, c], turn[:], ang[:, 3, c:c + 1], rot[:, c], ALU.mult, ALU.add))

        ring = Ring(W, 8)

        def bias_mul(e, b, n, bank):
            for c in range(C):
                mm = e.matmul(ps[:, bank, c:c + 1], rot[:, c], b_s[:, n, c:c + 1], start=True, stop=True)
            return mm
        for n, (name, dst, scale) in enumerate((("bq", g["bq_col"], WSCALE), ("bk", bk_col, 1.0))):
            bank, waits = ring.take([f"{name}c"])
            W.op("tensor", f"{name}m", waits + [f"rot{C - 1}", name], lambda e, b, n=n, bank=bank: bias_mul(e, b, n, bank))
            W.op(V, f"{name}c", [f"{name}m"], lambda e, b, bank=bank, dst=dst, scale=scale: e.tensor_scalar(
                dst[:], ps[:, bank, 0:C], scale, None, ALU.mult))

        def rotate(name, src, c, readers):
            bank, waits = ring.take(readers)

            def mul(e, b):
                for o in range(C):
                    mm = e.matmul(ps[:, bank, cols(o)], src[:, o, cols(c)], rot[:, o], start=True, stop=True)
                return mm
            W.op("tensor", f"{name}r{c}", waits + [f"rot{C - 1}", name], mul)
            return bank
        for c in range(C):
            bank = rotate("wk", wk_s, c, [f"wkT{c}"])
            W.op(S_, f"wkT{c}", [f"wkr{c}"], lambda e, b, c=c, bank=bank: e.activation(wkT[:, c], ps[:, bank], ACT.Copy))

        def split(name, dst_hi, dst_lo, src, ready, scale=WSCALE):
            W.op(S_, f"{name}_hi", ready, lambda e, b: e.activation(dst_hi, src, ACT.Copy, scale=scale))
            W.op(V, f"{name}_lo", [f"{name}_hi"], lambda e, b: e.scalar_tensor_tensor(
                dst_lo, src, scale, dst_hi, ALU.mult, ALU.subtract))

        kpart = lambda p: kv[:, :, p, 0:C * HPC * KEYS].rearrange("q b (c h n) -> q b c h n", c=C, h=HPC)
        for m in range(C):
            bank, waits = ring.take([f"k32{m}"])

            def mul(e, b, m=m, bank=bank):
                for c in range(C):
                    mm = e.matmul(ps[:, bank], wkT[:, c, cols(m)], ctx_s[:, c, :, 0], start=(c == 0), stop=(c == C - 1))
                return mm
            W.op("tensor", f"km{m}", waits + [f"wkT{c}" for c in range(C)] + [f"ctx0{c}" for c in range(C)], mul)
            W.op(S_, f"k32{m}", [f"km{m}", "bkc"], lambda e, b, m=m, bank=bank: e.activation(
                k32[:, m], ps[:, bank].rearrange("p (b n) -> p b n", b=B), ACT.Identity, bias=bk_col[:, m:m + 1]))
            for h in range(HPC):
                rows = slice(DK * h, DK * h + DK)
                W.op(S_, f"kh{m}_{h}", [f"k32{m}", "zero0", "zero1"], lambda e, b, m=m, h=h, rows=rows: e.activation(
                    kpart(HI)[rows, :, m, h], k32[rows, m], ACT.Copy))
                W.op(V, f"kl{m}_{h}", [f"kh{m}_{h}"], lambda e, b, m=m, h=h, rows=rows: e.tensor_tensor(
                    kpart(LO)[rows, :, m, h], k32[rows, m], kpart(HI)[rows, :, m, h], ALU.subtract))

        for c in range(C):
            bank = rotate("wq", wq_s, c, [f"wqs{c}_hi", f"wqs{c}_lo"])
            split(f"wqs{c}", g["WQ"][:, HI, c], g["WQ"][:, LO, c], ps[:, bank], [f"wqr{c}"])

        vpart = lambda p: kv[:, :, p, C * HPC * KEYS:KV].rearrange("q b (r h n) -> q b r h n", r=PAIRS, h=2)
        for bt in range(B):
            bank, waits = ring.take([f"vh{bt}_1", f"vl{bt}_1"])

            def mul(e, b, bt=bt, bank=bank):
                for c in range(C):
                    e.matmul(ps[:, bank], ctx_s[:, c, bt].rearrange("p a n -> p (a n)"), wv_s[:, c], start=(c == 0), stop=False)
                return e.matmul(ps[:, bank], ones[0:1], bv_s[:], start=False, stop=True)
            W.op("tensor", f"vm{bt}", waits + ["wv", "bv", "ones"] + [f"ctx{a}{c}" for a in range(2) for c in range(C)], mul)
            for h in range(2):
                rows = slice(KEYS * h, KEYS * h + KEYS)
                src = ps[rows, bank].rearrange("p (r h n) -> p r h n", r=PAIRS, h=2)[:, :, h]
                W.op(S_, f"vh{bt}_{h}", [f"vm{bt}", "zero0", "zero1"], lambda e, b, bt=bt, h=h, rows=rows, src=src: e.activation(
                    vpart(HI)[rows, bt, :, h], src, ACT.Copy))
                W.op(V, f"vl{bt}_{h}", [f"vh{bt}_{h}"], lambda e, b, bt=bt, h=h, rows=rows, src=src: e.tensor_tensor(
                    vpart(LO)[rows, bt, :, h], src, vpart(HI)[rows, bt, :, h], ALU.subtract))
            sems[f"kv_stored{bt}"] = g["kv_stored"][bt]
            W.op("sync", f"store{bt}", [f"vh{bt}_1", f"vl{bt}_1", f"kl{C - 1}_{HPC - 1}"], lambda e, b, bt=bt: e.dma_start(
                g["kv_dram"][bt], kv[:, bt].rearrange("p a n -> p (a n)")), dma=f"kv_stored{bt}")

        split("wos", g["WO"][:, HI], g["WO"][:, LO], wo_s[:], ["wo"])
        split("w1s", g["W1"][:, HI, 0:C], g["W1"][:, LO, 0:C], w1_s[:], ["w1"])
        for p in (HI, LO):
            W.op(V, f"w1n{p}", ["w1s_lo"], lambda e, b, p=p: e.tensor_scalar(
                g["W1"][:, p, C:C + 2], g["W1"][:, p, 1:3], -1.0, None, ALU.mult))
        split("w2s", g["W2"][:, HI], g["W2"][:, LO], w2_s[:], ["w2"])
        split("w3s", g["W3"][:, HI], g["W3"][:, LO], w3_s[:], ["w3"])
        split("g1s", g["G1"][:, HI], g["G1"][:, LO], gw1_s[:], ["g1"])
        split("g2s", g["G2"][:, HI], g["G2"][:, LO], gw2_s[:], ["g2"])
        W.op(V, "last", ["w4", "g3"], lambda e, b: e.tensor_scalar(last64[:], last_s[:], WSCALE, None, ALU.mult))
        for n, dst in enumerate((g["W4"], g["G3"])):
            W.op(V, f"last{n}_hi", ["last", "ones"], lambda e, b, n=n, dst=dst: e.tensor_scalar(
                dst[:, HI], ones[:], last64[:, n:n + 1], None, ALU.mult))
            W.op(V, f"last{n}_lo", [f"last{n}_hi"], lambda e, b, n=n, dst=dst: e.scalar_tensor_tensor(
                dst[:, LO], ones[:], last64[:, n:n + 1], dst[:, HI], ALU.mult, ALU.subtract))
        for n, (src, scale) in enumerate(((0, 1.0), (1, 0.5), (2, 0.5), (0, 0.3), (0, 0.7))):
            W.op(V, f"scal{n}", ["arange", "cb4", "gb3"], lambda e, b, n=n, src=src, scale=scale: e.tensor_scalar(
                g["scal"][:, n:n + 1], scal_s[:, src:src + 1], scale, None, ALU.mult))

        def run(name, eng):
            seen = {}
            for op in W.ops:
                if op[0] == name:
                    issue(eng, W, None, 0, op, seen)
            if name == "vector":
                for key in ("ident", "bo", "b1", "b2", "b3", "gb1", "gb2"):
                    eng.wait_ge(sems[f"in_{key}"], 16)
                for s in g["kv_stored"]:
                    eng.wait_ge(s, 16)

        with nc.Block() as block:
            @block.sync
            def _(eng):
                run("sync", eng)

            @block.tensor
            def _(eng):
                run("tensor", eng)

            @block.scalar
            def _(eng):
                run("scalar", eng)

            @block.vector
            def _(eng):
                run("vector", eng)

            @block.gpsimd
            def _(eng):
                run("gpsimd", eng)


def kernel(**inputs):
    import concourse.bacc as bacc
    from concourse.bass_utils import run_bass_kernel_spmd

    a = {k.replace("L0_xattn_", "").replace("L0_ffn_", ""): np.asarray(v) for k, v in inputs.items()}
    half = DK // 2
    turn = np.zeros((P, P), np.float32)
    for o in range(P):
        if o % DK < half:
            turn[o, o + half] = 1.0
        else:
            turn[o, o - half] = -1.0
    headsel = np.zeros((P, C, H), np.float32)
    for o in range(D):
        headsel[o % P, o // P, o // DK] = 1.0
    columns = lambda b: np.ascontiguousarray(b.reshape(-1, P).T)
    arrays = {
        "x": a["x"], "ctxT": np.ascontiguousarray(a["ctx_1024"].transpose(2, 0, 1)),
        "wq": a["Wq"], "bq": columns(a["bq"]), "wk": a["Wk"], "bk": columns(a["bk"]),
        "wvT": np.ascontiguousarray(a["Wv"].T), "bv": a["bv"],
        "woT": np.ascontiguousarray(a["Wo"].T), "bo": a["bo"], "phase": a["phase"],
        "cw1": a["cn_w1"], "cb1": columns(a["cn_b1"]), "cw2": a["cn_w2"], "cb2": columns(a["cn_b2"]),
        "cw3": a["cn_w3"], "cb3": columns(a["cn_b3"]), "cw4": a["cn_w4"], "cb4": a["cn_b4"],
        "gw1": a["gc_w1"], "gb1": columns(a["gc_b1"]), "gw2": a["gc_w2"], "gb2": columns(a["gc_b2"]),
        "gw3": a["gc_w3"], "gb3": a["gc_b3"], "arange": a["adaptive_range"],
        "ident_in": np.eye(P, dtype=np.float32), "turn_in": turn, "headsel_in": headsel.reshape(P, C * H),
    }
    nc = bacc.Bacc("TRN2", target_bir_lowering=False, num_devices=1)
    args = [nc.dram_tensor(n, v.shape, mybir.dt.from_np(v.dtype), kind="ExternalInput").ap() for n, v in arrays.items()]
    args.append(nc.dram_tensor("out", (B, S, D), F32, kind="ExternalOutput").ap())
    program(nc, *args)
    result = run_bass_kernel_spmd(nc, [arrays], core_ids=[0])
    return result.results[0]["out"]
```

```python
from contextlib import ExitStack

import numpy as np

import concourse.bass as bass
from concourse import mybir
from concourse.alu_op_type import AluOpType as ALU

F32 = mybir.dt.float32
F16 = mybir.dt.float16
I32 = mybir.dt.int32
ACT = mybir.ActivationFunctionType
AX = mybir.AxisListType

P = 128
B, S, D = 8, 1024, 512
H, DK, KEYS = 16, 32, 64
BLK = 512
NB = S // BLK
TPB = BLK // P
C = D // P
HPC = P // DK
PAIRS = H // 2
D2, D3 = D // 2, D // 4
C2 = D2 // P
WSCALE = 64.0
EPS = 1e-5
TWO_PI_HI = 6.28125
TWO_PI_LO = 2 * np.pi - 6.28125
HI, LO = 0, 1
LANES = 2
LBLK, TPL = BLK // LANES, TPB // LANES
POOL_LOW = ("gpsimd", "vector", "gpsimd", "vector")
FT = 3
KV = C * HPC * KEYS + PAIRS * 2 * DK


class Stream:

    def __init__(self, name, sems, credit):
        self.name, self.sems, self.credit = name, sems, credit
        self.ops, self.at, self.count, self.done_cost = [], {}, {}, 0.0

    def op(self, engine, name, waits, emit, cost=0.0, dma=None):
        key = dma or engine
        self.count[key] = self.count.get(key, 0) + 1
        assert name not in self.at, name
        self.at[name] = (key, self.count[key])
        self.ops.append((engine, name, waits, emit, cost, dma))

    def number(self, ops):
        self.ops, self.at, self.count = ops, {}, {}
        for engine, name, _, _, _, dma in ops:
            key = dma or engine
            self.count[key] = self.count.get(key, 0) + 1
            self.at[name] = (key, self.count[key])

    def earlier(self, fmt, n, gap, total):
        return (self, fmt.format(n - gap), 0) if n >= gap else (self, fmt.format(n - gap + total), 1)


class Ring:

    def __init__(self, stream, size):
        self.stream, self.size, self.uses = stream, size, []

    def take(self, readers):
        n = len(self.uses)
        waits = [(self.stream, r, 0) for r in self.uses[n - self.size][0]] if n >= self.size else []
        self.uses.append((readers, waits))
        return n % self.size, waits

    def close(self):
        assert len(self.uses) % self.size == 0, len(self.uses)
        for n in range(self.size):
            readers = self.uses[len(self.uses) - self.size + n][0]
            self.uses[n][1].extend((self.stream, r, 1) for r in readers)


def issue(eng, stream, step, offset, op, seen):
    _, _, waits, emit, _, dma = op
    need = {}
    for w in waits:
        src, what, back = w if isinstance(w, tuple) else (stream, w, 0)
        if step is None and offset < back:
            continue
        key, n = src.at[what]
        value = (offset - back + src.credit) * src.count[key] + n
        if seen.get((src.name, key), -1 << 30) < value:
            seen[src.name, key] = value
            need[src.name, key] = (src, key, value)
    for src, key, value in need.values():
        unit = 1 if key in ENGINES else 16
        eng.wait_ge(src.sems[key], value * unit if step is None else step * (src.count[key] * unit) + value * unit)
        if step is not None and apart(op):
            eng.sem_inc(stream.sems["apart"], 1)
    batch = offset if step is None else (step + offset if offset else step)
    emit(eng, batch).then_inc(stream.sems[dma or op[0]], 16 if dma else 1)


def apart(op):
    return op[0] == "sync" or op[1].startswith(("mv1", "mv2", "tb", "keep0", "keep1"))


ENGINES = ("tensor", "scalar", "vector", "gpsimd", "sync")


HOLDS = {
    "tensor": {"tr": .44, "q": 2.6, "s": 1.31, "pt": .44, "pv": .73, "wo": 2.6, "y": 1.31, "gz1": .8, "gz2": .2,
               "gz3": .1, "l2": 1.31, "l3": .66, "l4": .33, "tb": .45},
    "scalar": {"xn": .71, "xh": .48, "qh": .57, "exp": .95, "ph": .48, "oh": .48, "y": .26, "g": .38, "h": .38,
               "u": .36, "t": .9, "gt": .2, "gg": .2},
    "vector": {"st": .6, "mv": .08, "ve": .07, "nm": .07, "xl": .6, "ql": .67, "max": 1.14, "sub": 1.14, "sum": 1.14,
               "rec": .17, "pl": .6, "ol": .6, "res": .6, "h": .34, "mul": .34, "pre": .34, "cc": .32, "b2": .34,
               "a2": .26, "m": .34, "a3": .34, "b3": .34, "out": 1.05, "": .1},
    "gpsimd": {"h": .66, "rs": .1, "xb": 1.23, "nrm": 1.86, "keep": 7., "am": .63},
    "sync": {"": .1},
}
LAG = .2
LAND = 5.
TABLE = 1.3


def hold(op):
    table = HOLDS[op[0]]
    return table[max((p for p in table if op[1].startswith(p)), key=len)]


def weave(parts, free_order):
    place = {id(st): k for k, (_, st) in enumerate(parts)}
    nodes = {}
    for k, (offset, st) in enumerate(parts):
        last = {}
        for n, o in enumerate(st.ops):
            before = []
            for w in o[2]:
                src, what, back = w if isinstance(w, tuple) else (st, w, 0)
                if id(src) in place and offset - back == parts[place[id(src)]][0]:
                    before.append((place[id(src)], what))
            if not free_order and o[0] in last:
                before.append((k, last[o[0]]))
            last[o[0]] = o[1]
            nodes[k, o[1]] = (o, before, n)
    follows = {key: [] for key in nodes}
    for key, (_, before, _) in nodes.items():
        for b in before:
            follows[b].append(key)
    way = {}

    def longest(key):
        stack = [key]
        while stack:
            top = stack[-1]
            if top in way:
                stack.pop()
                continue
            more = [f for f in follows[top] if f not in way]
            if more:
                stack.extend(more)
                continue
            way[top] = max((way[f] for f in follows[top]), default=0.) + hold(nodes[top][0]) + LAG
            stack.pop()
    for key in nodes:
        longest(key)
    missing = {key: len(set(before)) for key, (_, before, _) in nodes.items()}
    ready_at = dict.fromkeys(nodes, 0.)
    ready = {e: [] for e in ENGINES}
    for key, n in missing.items():
        if n == 0:
            ready[nodes[key][0][0]].append(key)
    free, order, table, done = dict.fromkeys(ENGINES, 0.), [], "Gelu", {}
    ahead = AHEAD[len(parts)]
    while len(order) < len(nodes):
        best = None
        for e, keys in ready.items():
            if not keys:
                continue
            starts = {}
            for key in keys:
                kind = table_of(nodes[key][0], table)
                starts[key] = max(free[e], ready_at[key]) + (TABLE * SWITCH if kind != table and e == "scalar" else 0.)
            first = min(starts.values())
            if best is not None and first >= best[0]:
                continue
            pick = min((key for key in keys if starts[key] <= first + NEAR),
                       key=lambda key: (-way[key] - ahead[key[0]], nodes[key][2]))
            best = (first, e, pick)
        _, e, key = best
        o = nodes[key][0]
        start = max(free[e], ready_at[key])
        if e == "scalar":
            kind = table_of(o, table)
            start += TABLE if kind != table else 0.
            table = kind
        end = start + hold(o)
        free[e] = end
        done[key] = end
        ready[e].remove(key)
        order.append((parts[key[0]][0], parts[key[0]][1], o))
        for f in set(follows[key]):
            ready_at[f] = max(ready_at[f], end + (LAND if o[5] else LAG))
            missing[f] -= 1
            if missing[f] == 0:
                ready[nodes[f][0][0]].append(f)
    if free_order:
        for k, (_, st) in enumerate(parts):
            st.number([o for _, s, o in order if s is st])
    global SPAN, LOG
    SPAN, LOG = max(free.values()), done
    if VERBOSE:
        print("woven", len(parts), {e: round(f, 1) for e, f in free.items()})
    return order


def table_of(op, table):
    if op[1].startswith("exp"):
        return "Exp"
    return "Gelu" if op[1][0] in "hgu" else table


VERBOSE = False
NEAR = .1
SWITCH = 1.
AHEAD = {1: (0.,), 2: (0., 0.), 3: (90., 0., 0.)}


def passes(parts_a, parts_b):
    return ((parts_a[HI], parts_b[HI]), (parts_a[HI], parts_b[LO]), (parts_a[LO], parts_b[HI]))


def program(nc, x, ctxT, wq, bq, wk, bk, wvT, bv, woT, bo, phase, cw1, cb1, cw2, cb2, cw3, cb3, cw4, cb4,
            gw1, gb1, gw2, gb2, gw3, gb3, arange, ident_in, turn_in, headsel_in, out):
    kv_dram = nc.dram_tensor("kv_blocks", (B, P, 2 * KV), F16).ap()
    with ExitStack() as ctx:
        def sb(name, shape, dt=F32, stack=ctx):
            return stack.enter_context(nc.sbuf_tensor(name, shape, dt))

        def sem(name):
            return ctx.enter_context(nc.semaphore(name))

        WQ = sb("WQ", [P, 2, C, D], F16)
        WO = sb("WO", [P, 2, C, D], F16)
        W1 = sb("W1", [P, 2, C + 2, D], F16)
        W2 = sb("W2", [P, 2, C, D2], F16)
        W3 = sb("W3", [P, 2, C2, D3], F16)
        W4 = sb("W4", [P, 2, P], F16)
        G1 = sb("G1", [P, 2, C, D2], F16)
        G2 = sb("G2", [P, 2, C2, D3], F16)
        G3 = sb("G3", [P, 2, P], F16)
        ident = sb("ident", [P, P])
        bo_rows = sb("bo_rows", [P, D])
        bq_col = sb("bq_col", [P, C])
        b1_col = sb("b1_col", [P, C])
        b2_col = sb("b2_col", [P, C2])
        b3_col = sb("b3_col", [P, 1])
        gb1_col = sb("gb1_col", [P, C2])
        gb2_col = sb("gb2_col", [P, 1])
        scal = sb("scal", [P, 5])
        minus_half = sb("minus_half", [P, TPB])

        names = ["tensor", "scalar", "vector", "gpsimd"]
        kv_stored = [sem(f"kv_stored{b}") for b in range(B)]
        attn_sems = {e: sem(f"attn_{e}") for e in names}
        attn_sems.update({f"x_loaded{b}": sem(f"x_loaded{b}") for b in range(NB)})
        attn_sems["kv_loaded"] = sem("kv_loaded")
        attn_sems["apart"] = apart_sem = sem("apart")
        A = Stream("attn", attn_sems, 0)
        FL = []
        for L in range(LANES):
            ffn_sems = {e: sem(f"ffn{L}_{e}") for e in names}
            ffn_sems.update({f"stored{b}": sem(f"stored{L}_{b}") for b in range(2)})
            ffn_sems["apart"] = apart_sem
            FL.append(Stream(f"ffn{L}", ffn_sems, 1))

        setup(nc, sem, dict(
            kv_stored=kv_stored, kv_dram=kv_dram, ctxT=ctxT, wq=wq, bq=bq, wk=wk, bk=bk, wvT=wvT, bv=bv, woT=woT,
            bo=bo, phase=phase, cw1=cw1, cb1=cb1, cw2=cw2, cb2=cb2, cw3=cw3, cb3=cb3, cw4=cw4, cb4=cb4, gw1=gw1,
            gb1=gb1, gw2=gw2, gb2=gb2, gw3=gw3, gb3=gb3, arange=arange, ident_in=ident_in, turn_in=turn_in,
            headsel_in=headsel_in, WQ=WQ, WO=WO, W1=W1, W2=W2, W3=W3, W4=W4, G1=G1, G2=G2, G3=G3, ident=ident,
            bo_rows=bo_rows, bq_col=bq_col, b1_col=b1_col, b2_col=b2_col, b3_col=b3_col, gb1_col=gb1_col,
            gb2_col=gb2_col, scal=scal, minus_half=minus_half))

        kvb = sb("kvb", [P, 2, KV], F16)
        kb = [kvb[:, p, 0:C * HPC * KEYS].rearrange("p (c n) -> p c n", c=C) for p in (HI, LO)]
        vb = [kvb[:, p, C * HPC * KEYS:KV].rearrange("p (r n) -> p r n", r=PAIRS) for p in (HI, LO)]
        xin = sb("xin", [P, NB, TPB, D])
        x1p = sb("x1p", [P, NB, TPB, D])
        xn = sb("xn", [P, TPB, D])
        xoT = sb("xoT", [P, 2, C, BLK], F16)
        qT = sb("qT", [P, 2, C, BLK], F16)
        prob = sb("prob", [P, TPB, H * KEYS])
        pT = sb("pT", [P, 2, PAIRS, BLK], F16)
        x2T = sb("x2T", [P, NB, 2, C, BLK], F16)
        Y0 = sb("Y0", [P, LANES, C, LBLK])
        Y1 = sb("Y1", [P, LANES, C, LBLK])
        ft = sb("ft", [P, LANES, FT, LBLK])
        h1 = sb("h1", [P, LANES, 2, C, LBLK], F16)
        h2 = sb("h2", [P, LANES, 2, C2, LBLK], F16)
        h3 = sb("h3", [P, LANES, 2, LBLK], F16)
        cpl = sb("cpl", [P, LANES, LBLK])
        c1 = sb("c1", [P, LANES, LBLK])
        a2 = sb("a2", [P, LANES, LBLK])
        b2 = sb("b2", [P, LANES, LBLK])
        ot = sb("ot", [P, LANES, 2, D])
        stat = sb("stat", [P, NB, TPB, 6])
        mv1 = sb("mv1", [P, NB, TPB, 2])
        mv2 = sb("mv2", [P, NB, TPB, 2])
        ve = sb("ve", [P, NB, TPB])
        rs1 = sb("rs1", [P, NB, TPB])
        nm1 = sb("nm1", [P, NB, TPB])
        rs2 = sb("rs2", [P, NB, TPB])
        nm2 = sb("nm2", [P, NB, TPB])
        rs2p = sb("rs2p", [P, NB, TPB])
        nm2p = sb("nm2p", [P, NB, TPB])
        gs = sb("gs", [P, NB, C])
        mx = sb("mx", [P, TPB, H])
        sm = sb("sm", [P, TPB, H])
        rc = sb("rc", [P, TPB, H])
        gm = sb("gm", [P, C])
        gmh = sb("gmh", [P, 2, C], F16)
        g1 = sb("g1", [P, C2])
        g1h = sb("g1h", [P, 2, C2], F16)
        g2 = sb("g2", [P, 1])
        g2h = sb("g2h", [P, 2, 1], F16)
        gt = sb("gt", [P, 1])
        alpha = sb("alpha", [P, 1])
        ab = sb("ab", [P, LANES, 2, TPL])
        an = sb("an", [P, LANES, 2, TPL])
        co = sb("co", [P, LANES, 5, TPL])

        psS = ctx.enter_context(nc.psum_tensor("psS", [P, H * KEYS], F32))
        psA = ctx.enter_context(nc.psum_tensor("psA", [P, 2, BLK], F32))
        psF = ctx.enter_context(nc.psum_tensor("psF", [P, 4, BLK], F32))

        ringA = Ring(A, 2)
        x_dram = x.rearrange("b (k p j) d -> b k p (j d)", k=NB, j=TPB)
        out_dram = out.rearrange("b (k p j) d -> b k p (j d)", k=NB, j=TPB)
        cols = lambda j: slice(j * P, (j + 1) * P)

        def each(src, fmt, count, back=0):
            return [(src, fmt.format(n), back) for n in range(count)]

        def batch_of(dram, batch):
            return dram[batch] if isinstance(batch, int) else dram[bass.ds(batch, 1)].squeeze(0)

        def load(k):
            A.op("sync", f"load{k}", [(FL[0], f"keep{k}", 1)], lambda e, b: e.dma_start(
                xin[:, k].rearrange("p j d -> p (j d)"), batch_of(x_dram, b)[k]), dma=f"x_loaded{k}")

        def load_kv():
            A.op("sync", "kv", each(A, "s{}", NB * TPB, 1) + each(A, "pv0_{}", C, 1) + each(A, "pv1_{}", C, 1), lambda e, b: e.dma_start(
                kvb[:].rearrange("p a n -> p (a n)"), batch_of(kv_dram, b)), dma="kv_loaded")

        def norm_rows(k, tag, ready, mv, rs, nm, guard):
            for j in range(TPB):
                A.op("vector", f"st{tag}{k}_{j}", ready(j) + [(A, f"mv{'2' if tag == '1' else '1'}{k}_{j}", 1 if tag == "1" else 0)],
                     lambda e, b, j=j: e.bn_stats(stat[:, k, j], xin[:, k, j]))
            for j in range(TPB):
                A.op("vector", f"mv{tag}{k}_{j}", [f"st{tag}{k}_{j}"] + guard,
                     lambda e, b, j=j: e.bn_aggr(mv[:, k, j], stat[:, k, j]))
            other = (A, f"rs2{k}", 1) if tag == "1" else (A, f"rs1{k}", 0)
            A.op("vector", f"ve{tag}{k}", [f"mv{tag}{k}_{j}" for j in range(TPB)] + [other], lambda e, b: e.tensor_scalar(
                ve[:, k], mv[:, k, :, 1], EPS, None, ALU.add))
            A.op("gpsimd", f"rs{tag}{k}", [f"ve{tag}{k}"] + guard, lambda e, b: e.tensor_tensor(
                rs[:, k], ve[:, k], minus_half[:], ALU.pow))
            A.op("vector", f"nm{tag}{k}", [f"rs{tag}{k}"], lambda e, b: e.scalar_tensor_tensor(
                nm[:, k], mv[:, k, :, 0], -1.0, rs[:, k], ALU.mult, ALU.mult))

        turns = {("1", 0): ("tr21_{}", 1), ("1", 1): ("tr10_{}", 0), ("2", 0): ("tr11_{}", 0), ("2", 1): ("tr20_{}", 0)}

        def rows_out(k, tag, rs, nm):
            last, back = turns[tag, k]
            for j in range(TPB):
                A.op("scalar", f"xn{tag}{k}_{j}", [f"nm{tag}{k}"] + each(A, last, C, back), lambda e, b, j=j: e.activation(
                    xn[:, j], xin[:, k, j], ACT.Identity, bias=nm[:, k, j:j + 1], scale=rs[:, k, j:j + 1]))

        def turn_rows(k, tag, c, dst, readers, sums=None):
            hi, lo = f"xh{tag}{k}_{c}", f"xl{tag}{k}_{c}"
            bank, waits = ringA.take([hi, lo])

            def turn(e, b):
                for j in range(TPB):
                    mm = e.transpose(psA[:, bank, cols(j)], xn[:, j, cols(c)], ident[:])
                return mm
            A.op("tensor", f"tr{tag}{k}_{c}", waits_first(waits, [f"xn{tag}{k}_{j}" for j in range(TPB)]), turn, 0.44)
            A.op("scalar", hi, [f"tr{tag}{k}_{c}"] + readers, lambda e, b: e.activation(
                dst[HI][:, c], psA[:, bank], ACT.Copy, accum_out=sums) if sums is not None else e.activation(
                dst[HI][:, c], psA[:, bank], ACT.Copy))
            A.op("vector", lo, [hi], lambda e, b: e.tensor_tensor(
                dst[LO][:, c], psA[:, bank], dst[HI][:, c], ALU.subtract))

        def waits_first(waits, more):
            waits.extend(more)
            return waits

        def queries(k, m):
            hi, lo = f"qh{k}_{m}", f"ql{k}_{m}"
            bank, waits = ringA.take([hi, lo])

            def mul(e, b):
                n = 0
                for c in range(C):
                    for w, v in passes([WQ[:, p, c, cols(m)] for p in (HI, LO)], [xoT[:, p, c] for p in (HI, LO)]):
                        mm = e.matmul(psA[:, bank], w, v, start=(n == 0), stop=(n == 3 * C - 1))
                        n += 1
                return mm
            A.op("tensor", f"q{k}_{m}", waits_first(waits, [f"xl1{k}_{c}" for c in range(C)]), mul, 2.6)
            free = [A.earlier("s{}", TPB * k + j, TPB, NB * TPB) for j in range(TPB)]
            A.op("scalar", hi, [f"q{k}_{m}"] + free, lambda e, b: e.activation(
                qT[:, HI, m], psA[:, bank], ACT.Identity, bias=bq_col[:, m:m + 1]))
            A.op("vector", lo, [hi], lambda e, b: e.scalar_tensor_tensor(
                qT[:, LO, m], psA[:, bank], bq_col[:, m:m + 1], qT[:, HI, m], ALU.add, ALU.subtract))

        def scores(t):
            k, j = divmod(t, TPB)
            T = NB * TPB

            def mul(e, b):
                for c in range(C):
                    for n, (w, v) in enumerate(passes([qT[:, p, c, cols(j)] for p in (HI, LO)], [kb[p][:, c] for p in (HI, LO)])):
                        mm = e.matmul(psS[:, c * HPC * KEYS:(c + 1) * HPC * KEYS], w, v, start=(n == 0), stop=(n == 2))
                return mm
            A.op("tensor", f"s{t}", [f"ql{k}_{m}" for m in range(C)] + ["kv", A.earlier("sub{}", t, 1, T)], mul, 1.3)
            by_head = lambda a: a.rearrange("p (h n) -> p h n", h=H)
            wide = lambda a: a.unsqueeze(2).to_broadcast([P, H, KEYS])
            A.op("vector", f"max{t}", [f"s{t}", A.earlier("sub{}", t, TPB, T)], lambda e, b: e.tensor_reduce(
                mx[:, j], by_head(psS[:]), AX.X, ALU.max))
            A.op("vector", f"sub{t}", [f"max{t}", A.earlier("pt{}_0", t, TPB, T), A.earlier("pt{}_1", t, TPB, T)], lambda e, b: e.tensor_tensor(
                by_head(prob[:, j]), by_head(psS[:]), wide(mx[:, j]), ALU.subtract))
            A.op("scalar", f"exp{t}", [f"sub{t}"], lambda e, b: e.activation(
                prob[:, j], prob[:, j], ACT.Exp, scale=1.0 / (WSCALE * DK ** 0.5)))
            A.op("vector", f"sum{t}", [f"exp{t}", A.earlier("rec{}", t, TPB, T)], lambda e, b: e.tensor_reduce(
                sm[:, j], by_head(prob[:, j]), AX.X, ALU.add))
            A.op("vector", f"rec{t}", [f"sum{t}", A.earlier("nrm{}", t, TPB, T)], lambda e, b: e.reciprocal(rc[:, j], sm[:, j]))
            A.op("gpsimd", f"nrm{t}", [f"rec{t}"], lambda e, b: e.tensor_tensor(
                by_head(prob[:, j]), by_head(prob[:, j]), wide(rc[:, j]), ALU.mult))

        def turn_probs(t):
            k, j = divmod(t, TPB)
            for g in range(2):
                hi, lo = f"ph{t}_{g}", f"pl{t}_{g}"
                bank, waits = ringA.take([hi, lo])
                pairs = slice(4 * g, 4 * g + 4)

                def turn(e, b, g=g, bank=bank):
                    for r in range(4):
                        mm = e.transpose(psA[:, bank, cols(r)], prob[:, j, cols(4 * g + r)], ident[:])
                    return mm
                A.op("tensor", f"pt{t}_{g}", waits_first(waits, [f"nrm{t}"]), turn, 0.44)
                free = each(A, "pv0_{}", C) if k else each(A, "pv1_{}", C, 1)
                four = lambda a: a.rearrange("p (r n) -> p r n", r=4)
                A.op("scalar", hi, [f"pt{t}_{g}"] + free, lambda e, b, bank=bank, pairs=pairs: e.activation(
                    pT[:, HI, pairs, cols(j)], four(psA[:, bank]), ACT.Copy))
                A.op("vector", lo, [hi], lambda e, b, bank=bank, pairs=pairs: e.tensor_tensor(
                    pT[:, LO, pairs, cols(j)], four(psA[:, bank]), pT[:, HI, pairs, cols(j)], ALU.subtract))

        def values(k, c):
            hi, lo = f"oh{k}_{c}", f"ol{k}_{c}"
            bank, waits = ringA.take([hi, lo])

            def mul(e, b):
                for n in range(3):
                    for half in range(2):
                        r = 2 * c + half
                        w, v = passes([vb[p][:, r] for p in (HI, LO)], [pT[:, p, r] for p in (HI, LO)])[n]
                        mm = e.matmul(psA[64 * half:64 * half + 64, bank], w, v, start=(n == 0), stop=(n == 2))
                return mm
            ready = [f"pl{TPB * k + j}_{g}" for j in range(TPB) for g in range(2)] + ["kv"]
            A.op("tensor", f"pv{k}_{c}", waits_first(waits, ready), mul, 0.75)
            free = each(A, "q1_{}", C) if k == 0 else each(A, "wo{}", TPB)
            A.op("scalar", hi, [f"pv{k}_{c}"] + free, lambda e, b: e.activation(xoT[:, HI, c], psA[:, bank], ACT.Copy))
            A.op("vector", lo, [hi], lambda e, b: e.tensor_tensor(xoT[:, LO, c], psA[:, bank], xoT[:, HI, c], ALU.subtract))

        def project(t):
            k, j = divmod(t, TPB)
            bank, waits = ringA.take([f"res{t}"])

            def mul(e, b):
                n = 0
                for c in range(C):
                    for w, v in passes([xoT[:, p, c, cols(j)] for p in (HI, LO)], [WO[:, p, c] for p in (HI, LO)]):
                        mm = e.matmul(psA[:, bank], w, v, start=(n == 0), stop=(n == 3 * C - 1))
                        n += 1
                return mm
            A.op("tensor", f"wo{t}", waits_first(waits, [f"ol{k}_{c}" for c in range(C)]), mul, 2.6)
            A.op("vector", f"res{t}", [f"wo{t}", f"xb{t}"], lambda e, b: e.scalar_tensor_tensor(
                xin[:, k, j], psA[:, bank], 1.0 / WSCALE, xin[:, k, j], ALU.mult, ALU.add))

        def first_rows(k):
            norm_rows(k, "1", lambda j: [f"load{k}"], mv1, rs1, nm1, [(A, f"nm1{k}", 1)])
            rows_out(k, "1", rs1, nm1)
            for j in range(TPB):
                A.op("gpsimd", f"xb{TPB * k + j}", [f"xn1{k}_{j}", f"st1{k}_{j}"], lambda e, b, j=j: e.tensor_tensor(
                    xin[:, k, j], xin[:, k, j], bo_rows[:], ALU.add))

        def second_rows(k):
            norm_rows(k, "2", lambda j: [f"res{TPB * k + j}"], mv2, rs2, nm2, [(FL[0], "keep_stats", 1), (FL[0], "keep_rs", 1)])
            rows_out(k, "2", rs2, nm2)

        def second_turn(k, c):
            turn_rows(k, "2", c, [x2T[:, k, HI], x2T[:, k, LO]], [
                w for F in FL for w in each(F, f"y0{k}_{{}}", C, 1) + each(F, f"y1{k}_{{}}", C, 1)] + [(FL[0], "gsum", 1)],
                      sums=gs[:, k, c:c + 1])

        def first_turn(k, c):
            free = each(A, "q0_{}", C) if k else [(A, f"wo{TPB + j}", 1) for j in range(TPB)]
            turn_rows(k, "1", c, [xoT[:, HI], xoT[:, LO]], free)

        load(0)
        load(1)
        load_kv()
        first_rows(0)
        for c in range(C):
            first_turn(0, c)
        for m in range(C):
            queries(0, m)
        first_rows(1)
        scores(0)
        scores(1)
        first_turn(1, 0)
        first_turn(1, 1)
        scores(2)
        first_turn(1, 2)
        first_turn(1, 3)
        scores(3)
        for m in range(C):
            queries(1, m)
        turn_probs(0)
        turn_probs(1)
        scores(4)
        turn_probs(2)
        turn_probs(3)
        scores(5)
        for c in range(C):
            values(0, c)
        scores(6)
        project(0)
        project(1)
        scores(7)
        project(2)
        project(3)
        turn_probs(4)
        turn_probs(5)
        second_rows(0)
        for c in range(C):
            second_turn(0, c)
        turn_probs(6)
        turn_probs(7)
        for c in range(C):
            values(1, c)
        for t in range(TPB, NB * TPB):
            project(t)
        second_rows(1)
        for c in range(C):
            second_turn(1, c)
        ringA.close()

        def lane(F, L):
            ringF, ringT, ringO = Ring(F, 2), Ring(F, FT), Ring(F, 2)
            psL = psF[:, 2 * L:2 * L + 2, 0:LBLK]
            part, tiles = slice(L * LBLK, (L + 1) * LBLK), slice(TPL * L, TPL * L + TPL)

            def keep(k):
                F.op("gpsimd", f"keep{k}", each(A, f"xn2{k}_{{}}", TPB) + each(A, f"st2{k}_{{}}", TPB)
                     + [w for G in FL for w in each(G, f"out{k}_{{}}", TPL, 1)],
                     lambda e, b: e.tensor_scalar(x1p[:, k], xin[:, k], 1.0, None, ALU.mult))

            def keep_stats():
                ready = each(A, "nm2{}", NB) + [w for G in FL for w in each(G, "ar{}", NB, 1) + each(G, "coef0{}", NB, 1)]
                F.op("vector", "keep_rs", ready, lambda e, b: e.tensor_copy(rs2p[:], rs2[:]))
                F.op("vector", "keep_stats", ready, lambda e, b: e.tensor_copy(nm2p[:], nm2[:]))

            def split(src, dst, name, ready, free):
                F.op("vector", f"{name}h", ready + free, lambda e, b: e.tensor_copy(dst[HI], src))
                F.op("vector", f"{name}l", [f"{name}h"], lambda e, b: e.tensor_tensor(dst[LO], src, dst[HI], ALU.subtract))

            def global_context():
                F.op("vector", "gsum", each(A, "xh20_{}", C) + each(A, "xh21_{}", C) + [(F, "gml", 1)], lambda e, b: e.tensor_tensor(
                    gm[:], gs[:, 0], gs[:, 1], ALU.add))
                F.op("vector", "gmh", ["gsum", (F, "gz1", 1)], lambda e, b: e.tensor_scalar(
                    gmh[:, HI], gm[:], WSCALE / S, None, ALU.mult))
                F.op("vector", "gml", ["gmh"], lambda e, b: e.scalar_tensor_tensor(
                    gmh[:, LO], gm[:], WSCALE / S, gmh[:, HI], ALU.mult, ALU.subtract))

                def small(name, w, src, n_out, n_in, ready, place, at=0):
                    bank, waits = place

                    def mul(e, b):
                        for m in range(n_out):
                            n = 0
                            for c in range(n_in):
                                for a, v in passes([w(p, c, m) for p in (HI, LO)], [src[:, p, c:c + 1] for p in (HI, LO)]):
                                    mm = e.matmul(psL[:, bank, at + m:at + m + 1], a, v, start=(n == 0), stop=(n == 3 * n_in - 1))
                                    n += 1
                        return mm
                    F.op("tensor", name, waits_first(waits, ready), mul, 0.3)
                    return bank
                bank1 = small("gz1", lambda p, c, m: G1[:, p, c, cols(m)], gmh, C2, C, ["gml"],
                              ringF.take(["gb1"]))
                F.op("vector", "gb1", ["gz1", (F, "gg1", 1), (F, "g1l", 1)], lambda e, b: e.scalar_tensor_tensor(
                    g1[:], psL[:, bank1, 0:C2], WSCALE ** -2, gb1_col[:], ALU.mult, ALU.add))
                F.op("scalar", "gg1", ["gb1"], lambda e, b: e.activation(g1[:], g1[:], ACT.Gelu))
                split(g1[:], [g1h[:, HI], g1h[:, LO]], "g1", ["gg1"], [(F, "gz2", 1)])
                bank2 = small("gz2", lambda p, c, m: G2[:, p, c], g1h, 1, C2, ["g1l"],
                              ringF.take(["gg2", "gt"]))
                F.op("scalar", "gg2", ["gz2", (F, "g2l", 1)], lambda e, b: e.activation(
                    g2[:], psL[:, bank2, 0:1], ACT.Gelu, bias=gb2_col[:], scale=1.0 / WSCALE))
                split(g2[:], [g2h[:, HI], g2h[:, LO]], "g2", ["gg2"], [(F, "gz3", 1)])
                bank3 = small("gz3", lambda p, c, m: G3[:, p], g2h, 1, 1, ["g2l"], (bank2, []), at=1)
                F.op("scalar", "gt", ["gz3", (F, "alpha", 1)], lambda e, b: e.activation(
                    gt[:], psL[:, bank3, 1:2], ACT.Tanh, bias=scal[:, 2:3], scale=0.5 / WSCALE))
                F.op("vector", "alpha", ["gt"] + [w for G in FL for k in range(NB) for w in each(G, f"cc{k}_{{}}", 3, 1)], lambda e, b: e.tensor_scalar(
                    alpha[:], gt[:], scal[:, 4:5], 0.1, ALU.mult, ALU.add))

            def first_products(k, m):
                for name, order, dst in (("y0", ((0, 0), (1, 1), (2, 2), (3, 3)), Y0),
                                         ("y1", ((0, 2), (4, 3), (5, 0), (3, 1)), Y1)):
                    copy = f"{name}c{k}_{m}"
                    bank, waits = ringF.take([copy, f"g{k}_0_{m}", f"h{k}_0_{m}h"] if name == "y0" else [copy])

                    def mul(e, b, order=order, bank=bank):
                        n = 0
                        for wc, xc in order:
                            for w, v in passes([W1[:, p, wc, cols(m)] for p in (HI, LO)], [x2T[:, k, p, xc, part] for p in (HI, LO)]):
                                mm = e.matmul(psL[:, bank], w, v, start=(n == 0), stop=(n == 3 * C - 1))
                                n += 1
                        return mm
                    F.op("tensor", f"{name}{k}_{m}", waits_first(waits, each(A, f"xl2{k}_{{}}", C)), mul, 1.6)
                    if name == "y0":
                        first_activation(k, 0, m, psL[:, bank], 1.0 / WSCALE, [f"y0{k}_{m}"])
                    free = F.earlier("pre{}_2_" + str(m), k, 1, NB)
                    F.op("scalar", copy, [f"{name}{k}_{m}", free], lambda e, b, bank=bank, dst=dst: e.activation(
                        dst[:, L, m], psL[:, bank], ACT.Copy, scale=1.0 / WSCALE))

            def activate(name, src, slot, bias, scale, ready, dst, free, low="vector", inplace=False):
                F.op("scalar", f"h{name}h", ready + free, lambda e, b: e.activation(
                    dst[HI], src, ACT.Gelu, bias=bias, scale=scale))
                if inplace:
                    ready.append(f"h{name}h")
                F.op("scalar", f"g{name}", ready, lambda e, b: e.activation(
                    ft[:, L, slot], src, ACT.Gelu, bias=bias, scale=scale))
                F.op(low, f"h{name}l", [f"g{name}", f"h{name}h"], lambda e, b: e.tensor_tensor(
                    dst[LO], ft[:, L, slot], dst[HI], ALU.subtract))

            def first_activation(k, y, m, src, scale, ready, slot=None):
                if slot is None:
                    slot, waits = ringT.take([f"h{k}_{y}_{m}l"])
                    ready = waits_first(waits, ready)
                prev = [F.earlier(f"l2{{}}_{n}", 3 * k + y, 1, 3 * NB) for n in range(C2)]
                activate(f"{k}_{y}_{m}", src, slot, b1_col[:, m:m + 1], scale, ready,
                         [h1[:, L, HI, m], h1[:, L, LO, m]], prev, POOL_LOW[m], y > 0)

            def combine(k, y, m):
                slot, waits = ringT.take([f"h{k}_{y}_{m}l"])
                u, v = f"mul{k}_{y}_{m}", f"pre{k}_{y}_{m}"
                F.op("vector", u, waits_first(waits, [f"y1c{k}_{m}", f"cc{k}_0" if y == 1 else f"b2_{k}"]), lambda e, b: e.tensor_tensor(
                    ft[:, L, slot], Y1[:, L, m], c1[:, L] if y == 1 else b2[:, L], ALU.mult))
                if y == 2:
                    F.op("gpsimd", f"am{k}_{m}", [f"a2_{k}"] + [f"pre{k}_1_{m}"], lambda e, b: e.tensor_tensor(
                        Y0[:, L, m], Y0[:, L, m], a2[:, L], ALU.mult))
                F.op("vector", v, [u] + ([f"am{k}_{m}"] if y == 2 else []) + [f"y0c{k}_{m}"], lambda e, b: e.tensor_tensor(
                    ft[:, L, slot], ft[:, L, slot], Y0[:, L, m], ALU.add))
                first_activation(k, y, m, ft[:, L, slot], 1.0, [v], slot)

            def later_layers(k, y):
                i, N = 3 * k + y, 3 * NB
                for m in range(C2):
                    name = f"{i}_{m}"
                    bank, waits = ringF.take([f"gb{name}", f"hb{name}h"])

                    def mul(e, b, m=m, bank=bank):
                        n = 0
                        for c in range(C):
                            for w, v in passes([W2[:, p, c, cols(m)] for p in (HI, LO)], [h1[:, L, p, c] for p in (HI, LO)]):
                                mm = e.matmul(psL[:, bank], w, v, start=(n == 0), stop=(n == 3 * C - 1))
                                n += 1
                        return mm
                    F.op("tensor", f"l2{name}", waits_first(waits, [f"h{k}_{y}_{c}l" for c in range(C)]), mul, 4.0)
                    slot, waits = ringT.take([f"hb{name}l"])
                    activate(f"b{name}", psL[:, bank], slot, b2_col[:, m:m + 1], 1.0 / WSCALE,
                             waits_first(waits, [f"l2{name}"]), [h2[:, L, HI, m], h2[:, L, LO, m]], [F.earlier("l3{}", i, 1, N)])
                bank, waits = ringF.take([f"gc{i}", f"hc{i}h"])

                def mul3(e, b, bank=bank):
                    for c in range(C2):
                        for n, (w, v) in enumerate(passes([W3[:, p, c] for p in (HI, LO)], [h2[:, L, p, c] for p in (HI, LO)])):
                            mm = e.matmul(psL[:, bank], w, v, start=(n + c == 0), stop=(n + c == C2 + 1))
                    return mm
                F.op("tensor", f"l3{i}", waits_first(waits, [f"hb{i}_{m}l" for m in range(C2)]), mul3, 4.0)
                slot, waits = ringT.take([f"hc{i}l"])
                activate(f"c{i}", psL[:, bank], slot, b3_col[:], 1.0 / WSCALE, waits_first(waits, [f"l3{i}"]),
                         [h3[:, L, HI], h3[:, L, LO]], [F.earlier("l4{}", i, 1, N)])
                bank, waits = ringF.take([f"u{i}"])

                def mul4(e, b, bank=bank):
                    for n, (w, v) in enumerate(passes([W4[:, p] for p in (HI, LO)], [h3[:, L, p] for p in (HI, LO)])):
                        mm = e.matmul(psL[:, bank], w, v, start=(n == 0), stop=(n == 2))
                    return mm
                F.op("tensor", f"l4{i}", waits_first(waits, [f"hc{i}l"]), mul4, 4.0)
                last = [f"a2_{k}", f"b2_{k}"] if y == 2 else [F.earlier("tb{}", k, 1, NB)]
                dst = c1 if y == 0 else cpl
                F.op("scalar", f"u{i}", [f"l4{i}"] + last,
                     lambda e, b: e.activation(dst[:, L], psL[:, bank], ACT.Tanh, bias=scal[:, 1:2], scale=0.5 / WSCALE))
                F.op("vector", f"cc{k}_{y}", [f"u{i}", (FL[0], "alpha", 0)], lambda e, b: e.tensor_scalar(
                    dst[:, L], dst[:, L], scal[:, 3:4], alpha[:], ALU.mult, ALU.add), 1.0)

            def second_factor(k):
                before = [F.earlier(f"mul{{}}_2_{m}", k, 1, NB) for m in range(C)] + [
                    F.earlier(f"am{{}}_{m}", k, 1, NB) for m in range(C)] + [F.earlier("tb{}", k, 1, NB), f"cc{k}_0"]
                F.op("vector", f"b2_{k}", [f"cc{k}_1"] + before, lambda e, b: e.tensor_tensor(
                    b2[:, L], c1[:, L], cpl[:, L], ALU.add))
                F.op("vector", f"cc12_{k}", [f"cc{k}_1"] + before, lambda e, b: e.tensor_tensor(
                    a2[:, L], c1[:, L], cpl[:, L], ALU.mult))
                F.op("vector", f"a2_{k}", [f"cc12_{k}"], lambda e, b: e.tensor_scalar(
                    a2[:, L], a2[:, L], -1.0, 1.0, ALU.mult, ALU.add))

            def finish(k):
                row = slice(0, 1)
                F.op("vector", f"m1_{k}", [f"cc{k}_2"] + each(F, f"mul{k}_1_{{}}", C), lambda e, b: e.tensor_tensor(
                    c1[row, L], cpl[row, L], b2[row, L], ALU.mult))
                F.op("vector", f"m2_{k}", [f"m1_{k}"], lambda e, b: e.tensor_tensor(cpl[row, L], cpl[row, L], a2[row, L], ALU.mult))
                F.op("vector", f"a3_{k}", [f"m1_{k}"], lambda e, b: e.tensor_tensor(c1[row, L], a2[row, L], c1[row, L], ALU.subtract))
                F.op("vector", f"b3_{k}", [f"m2_{k}"], lambda e, b: e.tensor_tensor(cpl[row, L], b2[row, L], cpl[row, L], ALU.add))
                bank, waits = ringF.take([f"ar{k}", f"coef0{k}"])

                def turn(e, b):
                    for n, src in enumerate((c1, cpl)):
                        for j in range(TPL):
                            mm = e.transpose(psL[:, bank, n * TPL + j:n * TPL + j + 1], src[row, L, cols(j)], ident[row, 0:1])
                    return mm
                F.op("tensor", f"tb{k}", waits_first(waits, [f"a3_{k}", f"b3_{k}"]), turn, 1.0)
                prev = [F.earlier(f"co{n}{{}}", k, 1, NB) for n in range(3)]
                F.op("vector", f"ar{k}", [f"tb{k}", (FL[0], "keep_rs", 0)] + prev, lambda e, b: e.tensor_tensor(
                    ab[:, L], psL[:, bank, 0:2 * TPL].rearrange("p (n j) -> p n j", n=2),
                    rs2p[:, k, tiles].unsqueeze(1).to_broadcast([P, 2, TPL]), ALU.mult))
                done = [F.earlier(f"{n}{{}}_{j}", k, 1, NB) for n in ("t", "out") for j in range(TPL)]
                F.op("vector", f"co0{k}", [f"ar{k}"] + done, lambda e, b: e.tensor_scalar(co[:, L, 0], ab[:, L, 0], 1.0, None, ALU.add))
                F.op("vector", f"co1{k}", [f"ar{k}"] + done, lambda e, b: e.tensor_copy(co[:, L, 1], ab[:, L, 1]))
                F.op("vector", f"co2{k}", [f"ar{k}"] + done, lambda e, b: e.tensor_scalar(co[:, L, 2], ab[:, L, 1], -1.0, None, ALU.mult))
                F.op("vector", f"coef0{k}", [f"tb{k}", (FL[0], "keep_stats", 0), F.earlier("co3{}", k, 1, NB), F.earlier("co4{}", k, 1, NB)], lambda e, b: e.tensor_tensor(
                    an[:, L], psL[:, bank, 0:2 * TPL].rearrange("p (n j) -> p n j", n=2),
                    nm2p[:, k, tiles].unsqueeze(1).to_broadcast([P, 2, TPL]), ALU.mult), 0.5)
                F.op("vector", f"co3{k}", [f"coef0{k}"] + done, lambda e, b: e.tensor_tensor(co[:, L, 3], an[:, L, 0], an[:, L, 1], ALU.add))
                F.op("vector", f"co4{k}", [f"coef0{k}"] + done, lambda e, b: e.tensor_tensor(co[:, L, 4], an[:, L, 0], an[:, L, 1], ALU.subtract))
                chunk = lambda a: a.rearrange("p (c n) -> p c n", c=C)
                for j in range(TPL):
                    slot, waits = ringO.take([f"store{k}_{j}"])
                    dst, src = chunk(ot[:, L, slot]), chunk(x1p[:, k, TPL * L + j])
                    def straight(e, b, dst=dst, src=src, j=j):
                        e.activation(dst[:, 0::3], src[:, 0::3], ACT.Identity, bias=co[:, L, 3, j:j + 1], scale=co[:, L, 0, j:j + 1])
                        return e.activation(dst[:, 1:3], src[:, 1:3], ACT.Identity, bias=co[:, L, 4, j:j + 1], scale=co[:, L, 0, j:j + 1])
                    F.op("scalar", f"t{k}_{j}", waits_first(waits, [f"co0{k}", f"co3{k}", f"co4{k}", (FL[0], f"keep{k}", 0)]), straight)

                    def add(e, b, dst=dst, src=src, j=j):
                        for to, of, sign in ((0, 2, 1), (3, 1, 1), (1, 3, 2), (2, 0, 2)):
                            ins = e.scalar_tensor_tensor(dst[:, to], src[:, of], co[:, L, sign, j:j + 1], dst[:, to], ALU.mult, ALU.add)
                        return ins
                    F.op("vector", f"out{k}_{j}", [f"t{k}_{j}", f"co1{k}", f"co2{k}"], add)
                    F.op("sync", f"store{k}_{j}", [f"out{k}_{j}"], lambda e, b, slot=slot, j=j: e.dma_start(
                        batch_of(out_dram, b)[k][:, (TPL * L + j) * D:(TPL * L + j + 1) * D], ot[:, L, slot]), dma=f"stored{slot}")

            if L == 0:
                keep(0)
                keep(1)
                keep_stats()
            for k in range(NB):
                for m in range(C):
                    first_products(k, m)
                    if k == 0 and m == 0 and L == 0:
                        global_context()
                later_layers(k, 0)
                for m in range(C):
                    combine(k, 1, m)
                later_layers(k, 1)
                second_factor(k)
                for m in range(C):
                    combine(k, 2, m)
                later_layers(k, 2)
                finish(k)
            ringF.close()
            ringT.close()
            ringO.close()

        for L in range(LANES):
            lane(FL[L], L)

        both = weave([(-1, FL[0]), (-1, FL[1]), (0, A)], True)
        first = weave([(0, A)], False)
        final = weave([(B - 1, F) for F in FL], False)

        def run(step, order, name, eng):
            seen = {}
            for offset, stream, op in order:
                if op[0] == name:
                    issue(eng, stream, step, offset, op, seen)

        def engine_program(name, eng):
            if name == "sync":
                eng.wait_ge(kv_stored[0], 16)
            run(None, first, name, eng)
            if name == "sync":
                for b in range(1, B):
                    eng.wait_ge(kv_stored[b], 16)
            with eng.Fori(1, B) as i:
                run(i, both, name, eng)
            run(None, final, name, eng)
            if name == "sync":
                for F in FL:
                    for slot in range(2):
                        key = f"stored{slot}"
                        eng.wait_ge(F.sems[key], 16 * F.count[key] * (B + 1))

        with nc.Block() as credit:
            @credit.sync
            def _(eng):
                for F in FL:
                    for key, n in F.count.items():
                        eng.sem_inc(F.sems[key], n * (1 if key in ENGINES else 16))

        with nc.Block() as main:
            @main.sync
            def _(eng):
                engine_program("sync", eng)

            @main.tensor
            def _(eng):
                engine_program("tensor", eng)

            @main.scalar
            def _(eng):
                engine_program("scalar", eng)

            @main.vector
            def _(eng):
                engine_program("vector", eng)

            @main.gpsimd
            def _(eng):
                engine_program("gpsimd", eng)


def setup(nc, sem, g):
    sems = {e: sem(f"setup_{e}") for e in ENGINES[:4]}
    W = Stream("setup", sems, 0)
    with ExitStack() as ctx:
        def sb(name, shape, dt=F32):
            return ctx.enter_context(nc.sbuf_tensor(name, shape, dt))

        wq_s, wk_s = sb("wq_s", [P, C, D]), sb("wk_s", [P, C, D])
        wv_s, wo_s, w1_s = sb("wv_s", [P, C, D]), sb("wo_s", [P, C, D]), sb("w1_s", [P, C, D])
        w2_s, w3_s, gw1_s, gw2_s = (sb("w2_s", [P, C, D2]), sb("w3_s", [P, C2, D3]), sb("gw1_s", [P, C, D2]),
                                    sb("gw2_s", [P, C2, D3]))
        last_s = sb("last_s", [P, 2])
        last64 = sb("last64", [P, 2])
        ctx_s = sb("ctx_s", [P, C, B, 2, KEYS])
        wkT = sb("wkT", [P, C, D])
        k32 = sb("k32", [P, C, B, KEYS])
        kv = sb("kv", [P, B, 2, KV], F16)
        turn = sb("turn", [P, P])
        headsel = sb("headsel", [P, C, H])
        phases = sb("phases", [P, H])
        picked = sb("picked", [P, C, H])
        ang = sb("ang", [P, 6, C])
        turns = sb("turns", [P, C], I32)
        rot = sb("rot", [P, C, P])
        b_s = sb("b_s", [P, 2, C])
        bk_col = sb("bk_col", [P, C])
        scal_s = sb("scal_s", [P, 3])
        ones = sb("ones", [P, P])
        bv_s = sb("bv_s", [1, D])
        ps = ctx.enter_context(nc.psum_tensor("ps_setup", [P, 8, BLK], F32))
        cols = lambda j: slice(j * P, (j + 1) * P)

        def load(name, dst, src):
            sems[f"in_{name}"] = sem(f"in_{name}")
            W.op("sync", name, [], lambda e, b: e.dma_start(dst, src), dma=f"in_{name}")
        by_chunk = lambda a: a.rearrange("(c p) n -> p c n", p=P)
        load("phase", phases[:], g["phase"].rearrange("h a b -> (a b) h").partition_broadcast(P))
        load("headsel", headsel[:].rearrange("p c h -> p (c h)"), g["headsel_in"])
        load("ident", g["ident"][:], g["ident_in"])
        load("turn", turn[:], g["turn_in"])
        load("wk", wk_s[:], by_chunk(g["wk"]))
        load("bq", b_s[:, 0], g["bq"])
        load("bk", b_s[:, 1], g["bk"])
        ctx_view = g["ctxT"].rearrange("(c p) b n -> p c b n", p=P)
        for twin in range(2):
            for c in range(C):
                load(f"ctx{twin}{c}", ctx_s[:, c, :, twin], ctx_view[:, c])
        load("wv", wv_s[:], by_chunk(g["wvT"]))
        load("bv", bv_s[:], g["bv"].rearrange("(a n) -> a n", a=1))
        load("wq", wq_s[:], by_chunk(g["wq"]))
        load("wo", wo_s[:], by_chunk(g["woT"]))
        load("bo", g["bo_rows"][:], g["bo"].rearrange("(a n) -> a n", a=1).partition_broadcast(P))
        load("w1", w1_s[:], by_chunk(g["cw1"]))
        load("b1", g["b1_col"][:], g["cb1"])
        load("w2", w2_s[:], by_chunk(g["cw2"]))
        load("b2", g["b2_col"][:], g["cb2"])
        load("w3", w3_s[:], by_chunk(g["cw3"]))
        load("b3", g["b3_col"][:], g["cb3"])
        load("w4", last_s[:, 0:1], g["cw4"])
        load("g3", last_s[:, 1:2], g["gw3"])
        load("g1", gw1_s[:], by_chunk(g["gw1"]))
        load("gb1", g["gb1_col"][:], g["gb1"])
        load("g2", gw2_s[:], by_chunk(g["gw2"]))
        load("gb2", g["gb2_col"][:], g["gb2"])
        for n, a in enumerate(("arange", "cb4", "gb3")):
            load(a, scal_s[:, n:n + 1], g[a].rearrange("(a n) -> a n", a=1).partition_broadcast(P))

        V, S_, G = "vector", "scalar", "gpsimd"
        W.op(G, "ones", [], lambda e, b: e.memset(ones[:], 1.0))
        W.op(G, "half", [], lambda e, b: e.memset(g["minus_half"][:], -0.5))
        W.op(V, "zero0", [], lambda e, b: e.memset(kv[:, 0:B // 2].bitcast(F32), 0.0))
        W.op(G, "zero1", [], lambda e, b: e.memset(kv[:, B // 2:B].bitcast(F32), 0.0))

        W.op(V, "pick", ["phase", "headsel"], lambda e, b: e.tensor_tensor(
            picked[:], headsel[:], phases[:].unsqueeze(1).to_broadcast([P, C, H]), ALU.mult))
        W.op(V, "ph", ["pick"], lambda e, b: e.tensor_reduce(ang[:, 0], picked[:], AX.X, ALU.add))
        W.op(V, "turns", ["ph"], lambda e, b: e.tensor_scalar(turns[:], ang[:, 0], 1 / (2 * np.pi), None, ALU.mult))
        W.op(V, "turnsf", ["turns"], lambda e, b: e.tensor_copy(ang[:, 1], turns[:]))
        W.op(V, "red1", ["turnsf"], lambda e, b: e.scalar_tensor_tensor(
            ang[:, 2], ang[:, 1], -TWO_PI_HI, ang[:, 0], ALU.mult, ALU.add))
        W.op(V, "red2", ["red1"], lambda e, b: e.scalar_tensor_tensor(
            ang[:, 2], ang[:, 1], -TWO_PI_LO, ang[:, 2], ALU.mult, ALU.add))
        W.op(V, "clamp", ["red2"], lambda e, b: e.tensor_scalar(
            ang[:, 2], ang[:, 2], -3.1415925, 3.1415925, ALU.max, ALU.min))
        W.op(S_, "sin", ["clamp"], lambda e, b: e.activation(ang[:, 3], ang[:, 2], ACT.Sin))
        W.op(S_, "sinh", ["clamp"], lambda e, b: e.activation(ang[:, 4], ang[:, 2], ACT.Sin, scale=0.5))
        W.op(V, "sq", ["sinh"], lambda e, b: e.tensor_tensor(ang[:, 5], ang[:, 4], ang[:, 4], ALU.mult))
        W.op(V, "cos", ["sq"], lambda e, b: e.tensor_scalar(ang[:, 5], ang[:, 5], -2.0, 1.0, ALU.mult, ALU.add))
        for c in range(C):
            W.op(V, f"rc{c}", ["cos", "ident"], lambda e, b, c=c: e.tensor_scalar(
                rot[:, c], g["ident"][:], ang[:, 5, c:c + 1], None, ALU.mult))
            W.op(V, f"rot{c}", [f"rc{c}", "sin", "turn"], lambda e, b, c=c: e.scalar_tensor_tensor(
                rot[:, c], turn[:], ang[:, 3, c:c + 1], rot[:, c], ALU.mult, ALU.add))

        ring = Ring(W, 8)

        def bias_mul(e, b, n, bank):
            for c in range(C):
                mm = e.matmul(ps[:, bank, c:c + 1], rot[:, c], b_s[:, n, c:c + 1], start=True, stop=True)
            return mm
        for n, (name, dst, scale) in enumerate((("bq", g["bq_col"], WSCALE), ("bk", bk_col, 1.0))):
            bank, waits = ring.take([f"{name}c"])
            W.op("tensor", f"{name}m", waits + [f"rot{C - 1}", name], lambda e, b, n=n, bank=bank: bias_mul(e, b, n, bank))
            W.op(V, f"{name}c", [f"{name}m"], lambda e, b, bank=bank, dst=dst, scale=scale: e.tensor_scalar(
                dst[:], ps[:, bank, 0:C], scale, None, ALU.mult))

        def rotate(name, src, c, readers):
            bank, waits = ring.take(readers)

            def mul(e, b):
                for o in range(C):
                    mm = e.matmul(ps[:, bank, cols(o)], src[:, o, cols(c)], rot[:, o], start=True, stop=True)
                return mm
            W.op("tensor", f"{name}r{c}", waits + [f"rot{C - 1}", name], mul)
            return bank
        for c in range(C):
            bank = rotate("wk", wk_s, c, [f"wkT{c}"])
            W.op(S_, f"wkT{c}", [f"wkr{c}"], lambda e, b, c=c, bank=bank: e.activation(wkT[:, c], ps[:, bank], ACT.Copy))

        def split(name, dst_hi, dst_lo, src, ready, scale=WSCALE):
            W.op(S_, f"{name}_hi", ready, lambda e, b: e.activation(dst_hi, src, ACT.Copy, scale=scale))
            W.op(V, f"{name}_lo", [f"{name}_hi"], lambda e, b: e.scalar_tensor_tensor(
                dst_lo, src, scale, dst_hi, ALU.mult, ALU.subtract))

        kpart = lambda p: kv[:, :, p, 0:C * HPC * KEYS].rearrange("q b (c h n) -> q b c h n", c=C, h=HPC)
        for m in range(C):
            bank, waits = ring.take([f"k32{m}"])

            def mul(e, b, m=m, bank=bank):
                for c in range(C):
                    mm = e.matmul(ps[:, bank], wkT[:, c, cols(m)], ctx_s[:, c, :, 0], start=(c == 0), stop=(c == C - 1))
                return mm
            W.op("tensor", f"km{m}", waits + [f"wkT{c}" for c in range(C)] + [f"ctx0{c}" for c in range(C)], mul)
            W.op(S_, f"k32{m}", [f"km{m}", "bkc"], lambda e, b, m=m, bank=bank: e.activation(
                k32[:, m], ps[:, bank].rearrange("p (b n) -> p b n", b=B), ACT.Identity, bias=bk_col[:, m:m + 1]))
            for h in range(HPC):
                rows = slice(DK * h, DK * h + DK)
                W.op(S_, f"kh{m}_{h}", [f"k32{m}", "zero0", "zero1"], lambda e, b, m=m, h=h, rows=rows: e.activation(
                    kpart(HI)[rows, :, m, h], k32[rows, m], ACT.Copy))
                W.op(V, f"kl{m}_{h}", [f"kh{m}_{h}"], lambda e, b, m=m, h=h, rows=rows: e.tensor_tensor(
                    kpart(LO)[rows, :, m, h], k32[rows, m], kpart(HI)[rows, :, m, h], ALU.subtract))

        for c in range(C):
            bank = rotate("wq", wq_s, c, [f"wqs{c}_hi", f"wqs{c}_lo"])
            split(f"wqs{c}", g["WQ"][:, HI, c], g["WQ"][:, LO, c], ps[:, bank], [f"wqr{c}"])

        vpart = lambda p: kv[:, :, p, C * HPC * KEYS:KV].rearrange("q b (r h n) -> q b r h n", r=PAIRS, h=2)
        for bt in range(B):
            bank, waits = ring.take([f"vh{bt}_1", f"vl{bt}_1"])

            def mul(e, b, bt=bt, bank=bank):
                for c in range(C):
                    e.matmul(ps[:, bank], ctx_s[:, c, bt].rearrange("p a n -> p (a n)"), wv_s[:, c], start=(c == 0), stop=False)
                return e.matmul(ps[:, bank], ones[0:1], bv_s[:], start=False, stop=True)
            W.op("tensor", f"vm{bt}", waits + ["wv", "bv", "ones"] + [f"ctx{a}{c}" for a in range(2) for c in range(C)], mul)
            for h in range(2):
                rows = slice(KEYS * h, KEYS * h + KEYS)
                src = ps[rows, bank].rearrange("p (r h n) -> p r h n", r=PAIRS, h=2)[:, :, h]
                W.op(S_, f"vh{bt}_{h}", [f"vm{bt}", "zero0", "zero1"], lambda e, b, bt=bt, h=h, rows=rows, src=src: e.activation(
                    vpart(HI)[rows, bt, :, h], src, ACT.Copy))
                W.op(V, f"vl{bt}_{h}", [f"vh{bt}_{h}"], lambda e, b, bt=bt, h=h, rows=rows, src=src: e.tensor_tensor(
                    vpart(LO)[rows, bt, :, h], src, vpart(HI)[rows, bt, :, h], ALU.subtract))
            sems[f"kv_stored{bt}"] = g["kv_stored"][bt]
            W.op("sync", f"store{bt}", [f"vh{bt}_1", f"vl{bt}_1", f"kl{C - 1}_{HPC - 1}"], lambda e, b, bt=bt: e.dma_start(
                g["kv_dram"][bt], kv[:, bt].rearrange("p a n -> p (a n)")), dma=f"kv_stored{bt}")

        split("wos", g["WO"][:, HI], g["WO"][:, LO], wo_s[:], ["wo"])
        split("w1s", g["W1"][:, HI, 0:C], g["W1"][:, LO, 0:C], w1_s[:], ["w1"])
        for p in (HI, LO):
            W.op(V, f"w1n{p}", ["w1s_lo"], lambda e, b, p=p: e.tensor_scalar(
                g["W1"][:, p, C:C + 2], g["W1"][:, p, 1:3], -1.0, None, ALU.mult))
        split("w2s", g["W2"][:, HI], g["W2"][:, LO], w2_s[:], ["w2"])
        split("w3s", g["W3"][:, HI], g["W3"][:, LO], w3_s[:], ["w3"])
        split("g1s", g["G1"][:, HI], g["G1"][:, LO], gw1_s[:], ["g1"])
        split("g2s", g["G2"][:, HI], g["G2"][:, LO], gw2_s[:], ["g2"])
        W.op(V, "last", ["w4", "g3"], lambda e, b: e.tensor_scalar(last64[:], last_s[:], WSCALE, None, ALU.mult))
        for n, dst in enumerate((g["W4"], g["G3"])):
            W.op(V, f"last{n}_hi", ["last", "ones"], lambda e, b, n=n, dst=dst: e.tensor_scalar(
                dst[:, HI], ones[:], last64[:, n:n + 1], None, ALU.mult))
            W.op(V, f"last{n}_lo", [f"last{n}_hi"], lambda e, b, n=n, dst=dst: e.scalar_tensor_tensor(
                dst[:, LO], ones[:], last64[:, n:n + 1], dst[:, HI], ALU.mult, ALU.subtract))
        for n, (src, scale) in enumerate(((0, 1.0), (1, 0.5), (2, 0.5), (0, 0.3), (0, 0.7))):
            W.op(V, f"scal{n}", ["arange", "cb4", "gb3"], lambda e, b, n=n, src=src, scale=scale: e.tensor_scalar(
                g["scal"][:, n:n + 1], scal_s[:, src:src + 1], scale, None, ALU.mult))

        def run(name, eng):
            seen = {}
            for op in W.ops:
                if op[0] == name:
                    issue(eng, W, None, 0, op, seen)
            if name == "vector":
                for key in ("ident", "bo", "b1", "b2", "b3", "gb1", "gb2"):
                    eng.wait_ge(sems[f"in_{key}"], 16)
                for s in g["kv_stored"]:
                    eng.wait_ge(s, 16)

        with nc.Block() as block:
            @block.sync
            def _(eng):
                run("sync", eng)

            @block.tensor
            def _(eng):
                run("tensor", eng)

            @block.scalar
            def _(eng):
                run("scalar", eng)

            @block.vector
            def _(eng):
                run("vector", eng)

            @block.gpsimd
            def _(eng):
                run("gpsimd", eng)


def kernel(**inputs):
    import concourse.bacc as bacc
    from concourse.bass_utils import run_bass_kernel_spmd

    a = {k.replace("L0_xattn_", "").replace("L0_ffn_", ""): np.asarray(v) for k, v in inputs.items()}
    half = DK // 2
    turn = np.zeros((P, P), np.float32)
    for o in range(P):
        if o % DK < half:
            turn[o, o + half] = 1.0
        else:
            turn[o, o - half] = -1.0
    headsel = np.zeros((P, C, H), np.float32)
    for o in range(D):
        headsel[o % P, o // P, o // DK] = 1.0
    columns = lambda b: np.ascontiguousarray(b.reshape(-1, P).T)
    arrays = {
        "x": a["x"], "ctxT": np.ascontiguousarray(a["ctx_1024"].transpose(2, 0, 1)),
        "wq": a["Wq"], "bq": columns(a["bq"]), "wk": a["Wk"], "bk": columns(a["bk"]),
        "wvT": np.ascontiguousarray(a["Wv"].T), "bv": a["bv"],
        "woT": np.ascontiguousarray(a["Wo"].T), "bo": a["bo"], "phase": a["phase"],
        "cw1": a["cn_w1"], "cb1": columns(a["cn_b1"]), "cw2": a["cn_w2"], "cb2": columns(a["cn_b2"]),
        "cw3": a["cn_w3"], "cb3": columns(a["cn_b3"]), "cw4": a["cn_w4"], "cb4": a["cn_b4"],
        "gw1": a["gc_w1"], "gb1": columns(a["gc_b1"]), "gw2": a["gc_w2"], "gb2": columns(a["gc_b2"]),
        "gw3": a["gc_w3"], "gb3": a["gc_b3"], "arange": a["adaptive_range"],
        "ident_in": np.eye(P, dtype=np.float32), "turn_in": turn, "headsel_in": headsel.reshape(P, C * H),
    }
    nc = bacc.Bacc("TRN2", target_bir_lowering=False, num_devices=1)
    args = [nc.dram_tensor(n, v.shape, mybir.dt.from_np(v.dtype), kind="ExternalInput").ap() for n, v in arrays.items()]
    args.append(nc.dram_tensor("out", (B, S, D), F32, kind="ExternalOutput").ap())
    program(nc, *args)
    result = run_bass_kernel_spmd(nc, [arrays], core_ids=[0])
    return result.results[0]["out"]
```

```python
from contextlib import ExitStack
from typing import Callable, NamedTuple, Optional

import numpy as np

import concourse.bass as bass
from concourse import mybir
from concourse.alu_op_type import AluOpType as ALU

F32 = mybir.dt.float32
F16 = mybir.dt.float16
I32 = mybir.dt.int32
ACT = mybir.ActivationFunctionType
AX = mybir.AxisListType

P = 128
B, S, D = 8, 1024, 512
H, DK, KEYS = 16, 32, 64
BLK = 512
NB = S // BLK
TPB = BLK // P
C = D // P
HHEADS = H // 2
HPC = P // DK
PAIRS = H // 2
D2, D3 = D // 2, D // 4
C2 = D2 // P
WSCALE = 64.0
EPS = 1e-5
TWO_PI_HI = 6.28125
TWO_PI_LO = 2 * np.pi - 6.28125
HI, LO = 0, 1
LANES = 2
LBLK, TPL = BLK // LANES, TPB // LANES
SCALED_BY = ("vector", "vector", "vector", "gpsimd")
FT = 3
KV = C * HPC * KEYS + PAIRS * 2 * DK


class Op(NamedTuple):
    engine: str
    name: str
    waits: list
    emit: Callable
    dma: Optional[str] = None


class Stream:

    def __init__(self, name, sems, credit):
        self.name, self.sems, self.credit = name, sems, credit
        self.ops, self.at, self.count = [], {}, {}

    def op(self, engine, name, waits, emit, dma=None):
        key = dma or engine
        self.count[key] = self.count.get(key, 0) + 1
        assert name not in self.at, name
        self.at[name] = (key, self.count[key])
        self.ops.append(Op(engine, name, waits, emit, dma))

    def number(self, ops):
        self.ops, self.at, self.count = ops, {}, {}
        for o in ops:
            key = o.dma or o.engine
            self.count[key] = self.count.get(key, 0) + 1
            self.at[o.name] = (key, self.count[key])

    def earlier(self, fmt, n, gap, total):
        return (self, fmt.format(n - gap), 0) if n >= gap else (self, fmt.format(n - gap + total), 1)


class Ring:

    def __init__(self, size):
        self.size, self.uses = size, []

    def take(self, readers):
        n = len(self.uses)
        self.uses.append(readers)
        return n % self.size, list(self.uses[n - self.size]) if n >= self.size else []


class Use:

    def __init__(self, pool, stream, readers):
        self.pool, self.stream, self.readers, self.slot = pool, stream, readers, None


class Pool:

    def __init__(self, size):
        self.size, self.uses = size, []

    def take(self, stream, readers):
        return Use(self, stream, readers)

    def waits(self, use, shift):
        mine = [u for u in self.uses if u.slot == use.slot]
        at, waits = mine.index(use), []
        for stream in dict.fromkeys(u.stream for u in mine):
            before = [u for u in mine[:at] if u.stream is stream]
            back = shift[stream.name] - shift[use.stream.name]
            if before:
                waits += [(stream, r, back) for r in before[-1].readers]
            last = [u for u in mine if u.stream is stream][-1]
            if not before or stream is not use.stream:
                waits += [(stream, r, back + 1, "final") if before else (stream, r, back + 1) for r in last.readers]
        return waits


def issue(eng, stream, step, offset, op, seen):
    _, _, waits, emit, dma = op
    need = {}
    for w in waits:
        src, what, back, *final = w if isinstance(w, tuple) else (stream, w, 0)
        if final and (step is not None or offset == 0):
            continue
        if step is None and not 0 <= offset - back < B:
            continue
        key, n = src.at[what]
        value = (offset - back + src.credit) * src.count[key] + n
        if seen.get((src.name, key), -1 << 30) < value:
            seen[src.name, key] = value
            need[src.name, key] = (src, key, value)
    for src, key, value in need.values():
        unit = 1 if key in ENGINES else 16
        eng.wait_ge(src.sems[key], value * unit if step is None else step * (src.count[key] * unit) + value * unit)
        if step is not None and apart(op):
            eng.sem_inc(stream.sems["apart"], 1)
    batch = offset if step is None else (step + offset if offset else step)
    emit(eng, batch).then_inc(stream.sems[dma or op.engine], 16 if dma else 1)


def apart(op):
    return op.engine == "sync" or op.name.startswith(("mv1", "mv2", "tb", "keep0", "keep1"))


ENGINES = ("tensor", "scalar", "vector", "gpsimd", "sync")


HOLDS = {
    "tensor": {"tr": .44, "q": 2.6, "s": .66, "pt": .44, "pv": .73, "wo": 2.6, "y": 1.31, "gz1": .8, "gz2": .2,
               "gz3": .1, "l2": 1.31, "l3": .66, "l4": .33, "tb": .45},
    "scalar": {"xn": .71, "xh": .48, "qh": .57, "exp": .95, "ph": .48, "oh": .48, "y": .26, "g": .4,
               "h": .4, "gb": .36, "hb": .36, "gc": .36, "hc": .36, "u": .36, "t": .99, "keep": 1.8, "gt": .2, "gg": .2},
    "vector": {"st": .6, "mv": .08, "ve": .07, "nm": .07, "xl": .6, "ql": .67, "max": .6, "sub": .6, "sum": 1.14,
               "rec": .17, "pl": .6, "ol": .6, "res": .6, "h": .34, "mul": .34, "pre": .34, "cc": .32, "b2": .34,
               "a2": .26, "m": .34, "a3": .34, "b3": .34, "out": 1.05, "": .1},
    "gpsimd": {"h": .64, "rs": .5, "xb": 1.23, "nrm": 1., "mul": .69, "am": .69},
    "sync": {"": .1},
}
LAG = .2
LAND = 5.
TABLE = 1.3


def hold(op):
    table = HOLDS[op.engine]
    return table[max((p for p in table if op.name.startswith(p)), key=len)]


def weave(parts, free_order):
    place = {id(st): k for k, (_, st) in enumerate(parts)}
    nodes, reads = {}, {}
    for k, (offset, st) in enumerate(parts):
        last = {}
        for n, o in enumerate(st.ops):
            before = []
            for w in o.waits:
                if isinstance(w, Use):
                    for r in w.readers:
                        reads[k, r] = reads.get((k, r), []) + [w]
                    continue
                src, what, back, *_ = w if isinstance(w, tuple) else (st, w, 0)
                if id(src) in place and offset - back == parts[place[id(src)]][0]:
                    before.append((place[id(src)], what))
            if not free_order and o.engine in last:
                before.append((k, last[o.engine]))
            last[o.engine] = o.name
            nodes[k, o.name] = (o, before, n)
    follows = {key: [] for key in nodes}
    for key, (_, before, _) in nodes.items():
        for b in before:
            follows[b].append(key)
    way = {}

    def longest(key):
        stack = [key]
        while stack:
            top = stack[-1]
            if top in way:
                stack.pop()
                continue
            more = [f for f in follows[top] if f not in way]
            if more:
                stack.extend(more)
                continue
            way[top] = max((way[f] for f in follows[top]), default=0.) + hold(nodes[top][0]) + LAG
            stack.pop()
    for key in nodes:
        longest(key)
    missing = {key: len(set(before)) for key, (_, before, _) in nodes.items()}
    ready_at = dict.fromkeys(nodes, 0.)
    ready = {e: [] for e in ENGINES}
    for key, n in missing.items():
        if n == 0:
            ready[nodes[key][0].engine].append(key)
    free, order, table = dict.fromkeys(ENGINES, 0.), [], "Gelu"
    ahead = AHEAD[len(parts)]
    slots = {}

    def free_slot(pool):
        if pool not in slots:
            slots[pool] = [[0, 0.] for _ in range(pool.size)]
            pool.uses = []
        return min((s for s in range(pool.size) if slots[pool][s][0] == 0), key=lambda s: slots[pool][s][1], default=None)

    while len(order) < len(nodes):
        best = None
        for e, keys in ready.items():
            if not keys:
                continue
            starts = {}
            for key in keys:
                wanted = 0.
                for use in takes(nodes[key][0]):
                    slot = free_slot(use.pool)
                    wanted = 1e9 if slot is None else max(wanted, slots[use.pool][slot][1])
                if wanted == 1e9:
                    continue
                kind = table_of(nodes[key][0], table)
                starts[key] = max(free[e], ready_at[key], wanted) + (
                    TABLE * SWITCH if kind != table and e == "scalar" else 0.)
            if not starts:
                continue
            first = min(starts.values())
            if best is not None and first >= best[0]:
                continue
            pick = min((key for key in starts if starts[key] <= first + NEAR),
                       key=lambda key: (-way[key] - ahead[key[0]], nodes[key][2]))
            best = (first, e, pick)
        _, e, key = best
        o = nodes[key][0]
        start = max(free[e], ready_at[key])
        for use in takes(o):
            use.slot = free_slot(use.pool)
            start = max(start, slots[use.pool][use.slot][1])
            slots[use.pool][use.slot] = [len(use.readers), 0.]
            use.pool.uses.append(use)
        if e == "scalar":
            kind = table_of(o, table)
            start += TABLE if kind != table else 0.
            table = kind
        end = start + hold(o)
        free[e] = end
        ready[e].remove(key)
        for use in reads.get(key, ()):
            state = slots[use.pool][use.slot]
            state[0] -= 1
            state[1] = max(state[1], end + LAG)
        order.append((parts[key[0]][0], parts[key[0]][1], o))
        for f in set(follows[key]):
            ready_at[f] = max(ready_at[f], end + (LAND if o.dma else LAG))
            missing[f] -= 1
            if missing[f] == 0:
                ready[nodes[f][0].engine].append(f)
    if free_order:
        shift = {st.name: -offset for offset, st in parts}
        for k, (offset, st, o) in enumerate(order):
            waits = [w for w in o.waits if not isinstance(w, Use)]
            for use in takes(o):
                waits += use.pool.waits(use, shift)
            order[k] = (offset, st, o._replace(waits=waits))
        for k, (_, st) in enumerate(parts):
            st.number([o for _, s, o in order if s is st])
    return order


def takes(op):
    return [w for w in op.waits if isinstance(w, Use)]


def table_of(op, table):
    if op.name.startswith("exp"):
        return "Exp"
    return "Gelu" if op.name[0] in "hgu" else table


NEAR = .04
SWITCH = .5
AHEAD = {1: (0.,), 2: (0., 0.), 3: (10., 0., 3.)}


def passes(parts_a, parts_b):
    return ((parts_a[HI], parts_b[HI]), (parts_a[HI], parts_b[LO]), (parts_a[LO], parts_b[HI]))


def program(nc, x, ctxT, wq, bq, wk, bk, wvT, bv, woT, bo, phase, cw1, cb1, cw2, cb2, cw3, cb3, cw4, cb4,
            gw1, gb1, gw2, gb2, gw3, gb3, arange, ident_in, turn_in, headsel_in, out):
    kv_dram = nc.dram_tensor("kv_blocks", (B, P, 2 * KV), F16).ap()
    with ExitStack() as ctx:
        def sb(name, shape, dt=F32, stack=ctx):
            return stack.enter_context(nc.sbuf_tensor(name, shape, dt))

        def sem(name):
            return ctx.enter_context(nc.semaphore(name))

        WQ = sb("WQ", [P, 2, C, D], F16)
        WO = sb("WO", [P, 2, C, D], F16)
        W1 = sb("W1", [P, 2, C + 2, D], F16)
        W2 = sb("W2", [P, 2, C, D2], F16)
        W3 = sb("W3", [P, 2, C2, D3], F16)
        W4 = sb("W4", [P, 2, P], F16)
        G1 = sb("G1", [P, 2, C, D2], F16)
        G2 = sb("G2", [P, 2, C2, D3], F16)
        G3 = sb("G3", [P, 2, P], F16)
        ident = sb("ident", [P, P])
        bo_rows = sb("bo_rows", [P, D])
        bq_col = sb("bq_col", [P, C])
        b1_col = sb("b1_col", [P, C])
        b2_col = sb("b2_col", [P, C2])
        b3_col = sb("b3_col", [P, 1])
        gb1_col = sb("gb1_col", [P, C2])
        gb2_col = sb("gb2_col", [P, 1])
        scal = sb("scal", [P, 5])
        minus_half = sb("minus_half", [P, TPB])
        warm = sb("warm", [P, 1])
        warmed = sem("warmed")

        xin = sb("xin", [P, NB, TPB, D])
        late = sb("late", [P, NB * TPB * D + LANES * LBLK * (2 * C + FT + C + C2)])
        taken = [0]

        def place(shape, dt=F32):
            size = int(np.prod(shape)) // (2 if dt == F16 else 1)
            piece = late[:, taken[0]:taken[0] + size]
            taken[0] += size
            names = "abcd"[:len(shape)]
            return (piece.bitcast(F16) if dt == F16 else piece).rearrange(
                f"p ({' '.join(names)}) -> p {' '.join(names)}", **dict(zip(names, shape)))

        names = ["tensor", "scalar", "vector", "gpsimd"]
        kv_stored = [sem(f"kv_stored{b}") for b in range(B)]
        attn_sems = {e: sem(f"attn_{e}") for e in names}
        attn_sems.update({f"x_loaded{b}": sem(f"x_loaded{b}") for b in range(NB)})
        attn_sems["kv_loaded"] = sem("kv_loaded")
        attn_sems["apart"] = apart_sem = sem("apart")
        A = Stream("attn", attn_sems, 0)
        FL = []
        for L in range(LANES):
            ffn_sems = {e: sem(f"ffn{L}_{e}") for e in names}
            ffn_sems.update({f"stored{b}": sem(f"stored{L}_{b}") for b in range(2)})
            ffn_sems["apart"] = apart_sem
            FL.append(Stream(f"ffn{L}", ffn_sems, 1))

        x_dram = x.rearrange("b (k p j) d -> b k p (j d)", k=NB, j=TPB)

        def load_first(e):
            for k in range(NB):
                e.dma_start(xin[:, k].rearrange("p j d -> p (j d)"), x_dram[0][k]).then_inc(attn_sems[f"x_loaded{k}"], 16)

        setup(nc, sem, dict(
            load_first=load_first, late=late,
            kv_stored=kv_stored, kv_dram=kv_dram, ctxT=ctxT, wq=wq, bq=bq, wk=wk, bk=bk, wvT=wvT, bv=bv, woT=woT,
            bo=bo, phase=phase, cw1=cw1, cb1=cb1, cw2=cw2, cb2=cb2, cw3=cw3, cb3=cb3, cw4=cw4, cb4=cb4, gw1=gw1,
            gb1=gb1, gw2=gw2, gb2=gb2, gw3=gw3, gb3=gb3, arange=arange, ident_in=ident_in, turn_in=turn_in,
            headsel_in=headsel_in, WQ=WQ, WO=WO, W1=W1, W2=W2, W3=W3, W4=W4, G1=G1, G2=G2, G3=G3, ident=ident,
            bo_rows=bo_rows, bq_col=bq_col, b1_col=b1_col, b2_col=b2_col, b3_col=b3_col, gb1_col=gb1_col,
            gb2_col=gb2_col, scal=scal, minus_half=minus_half))

        kvb = sb("kvb", [P, 2, KV], F16)
        kb = [kvb[:, p, 0:C * HPC * KEYS].rearrange("p (c n) -> p c n", c=C) for p in (HI, LO)]
        vb = [kvb[:, p, C * HPC * KEYS:KV].rearrange("p (r n) -> p r n", r=PAIRS) for p in (HI, LO)]
        x1p = place([NB, TPB, D])
        xn = sb("xn", [P, TPB, D])
        xoT = sb("xoT", [P, 2, C, BLK], F16)
        qT = sb("qT", [P, 2, C, BLK], F16)
        prob = sb("prob", [P, TPB, H * KEYS])
        pT = sb("pT", [P, 2, PAIRS, BLK], F16)
        x2T = sb("x2T", [P, NB, 2, C, BLK], F16)
        Y0 = place([LANES, C, LBLK])
        Y1 = place([LANES, C, LBLK])
        ft = place([LANES * FT, LBLK])
        h1 = place([LANES, 2, C, LBLK], F16)
        h2 = place([LANES, 2, C2, LBLK], F16)
        h3 = sb("h3", [P, LANES, 2, LBLK], F16)
        cpl = sb("cpl", [P, LANES, LBLK])
        c1 = sb("c1", [P, LANES, LBLK])
        a2 = sb("a2", [P, LANES, LBLK])
        b2 = sb("b2", [P, LANES, LBLK])
        ot = sb("ot", [P, LANES, 2, D])
        stat = sb("stat", [P, NB, TPB, 6])
        mv1 = sb("mv1", [P, NB, TPB, 2])
        mv2 = sb("mv2", [P, NB, TPB, 2])
        ve = sb("ve", [P, NB, TPB])
        rs1 = sb("rs1", [P, NB, TPB])
        nm1 = sb("nm1", [P, NB, TPB])
        rs2 = sb("rs2", [P, NB, TPB])
        nm2 = sb("nm2", [P, NB, TPB])
        rs2p = sb("rs2p", [P, NB, TPB])
        nm2p = sb("nm2p", [P, NB, TPB])
        gs = sb("gs", [P, NB, C])
        mx = sb("mx", [P, TPB, H])
        sm = sb("sm", [P, TPB, H])
        rc = sb("rc", [P, TPB, H])
        gm = sb("gm", [P, C])
        gmh = sb("gmh", [P, 2, C], F16)
        g1 = sb("g1", [P, C2])
        g1h = sb("g1h", [P, 2, C2], F16)
        g2 = sb("g2", [P, 1])
        g2h = sb("g2h", [P, 2, 1], F16)
        gt = sb("gt", [P, 1])
        alpha = sb("alpha", [P, 1])
        ab = sb("ab", [P, LANES, 2, TPL])
        an = sb("an", [P, LANES, 2, TPL])
        co = sb("co", [P, LANES, 5, TPL])

        ps = ctx.enter_context(nc.psum_tensor("ps", [P, 8, BLK], F32))

        banks = Pool(8)
        acts = Pool(LANES * FT)
        out_dram = out.rearrange("b (k p j) d -> b k p (j d)", k=NB, j=TPB)
        cols = lambda j: slice(j * P, (j + 1) * P)

        def each(src, fmt, count, back=0):
            return [(src, fmt.format(n), back) for n in range(count)]

        def batch_of(dram, batch):
            return dram[batch] if isinstance(batch, int) else dram[bass.ds(batch, 1)].squeeze(0)

        def load(k):
            A.op("sync", f"load{k}", [(FL[0], f"keep{k}", 1)], lambda e, b: e.dma_start(
                xin[:, k].rearrange("p j d -> p (j d)"), batch_of(x_dram, b)[k]), dma=f"x_loaded{k}")

        def load_kv():
            A.op("sync", "kv", each(A, "s{}_0", NB * TPB, 1) + each(A, "s{}_1", NB * TPB, 1)
                 + each(A, "pv0_{}", C, 1) + each(A, "pv1_{}", C, 1),
                lambda e, b: e.dma_start(
                kvb[:].rearrange("p a n -> p (a n)"), batch_of(kv_dram, b)), dma="kv_loaded")

        def norm_rows(k, tag, ready, mv, rs, nm, guard):
            for j in range(TPB):
                A.op("vector", f"st{tag}{k}_{j}", ready(j) + [(A, f"mv{'2' if tag == '1' else '1'}{k}_{j}", 1 if tag == "1" else 0)],
                     lambda e, b, j=j: e.bn_stats(stat[:, k, j], xin[:, k, j]))
            for j in range(TPB):
                A.op("vector", f"mv{tag}{k}_{j}", [f"st{tag}{k}_{j}"] + guard,
                     lambda e, b, j=j: e.bn_aggr(mv[:, k, j], stat[:, k, j]))
            other = (A, f"rs2{k}", 1) if tag == "1" else (A, f"rs1{k}", 0)
            A.op("vector", f"ve{tag}{k}", [f"mv{tag}{k}_{j}" for j in range(TPB)] + [other], lambda e, b: e.tensor_scalar(
                ve[:, k], mv[:, k, :, 1], EPS, None, ALU.add))
            A.op("gpsimd", f"rs{tag}{k}", [f"ve{tag}{k}"] + guard, lambda e, b: e.tensor_tensor(
                rs[:, k], ve[:, k], minus_half[:], ALU.pow))
            A.op("vector", f"nm{tag}{k}", [f"rs{tag}{k}"], lambda e, b: e.scalar_tensor_tensor(
                nm[:, k], mv[:, k, :, 0], -1.0, rs[:, k], ALU.mult, ALU.mult))

        turns = {("1", 0): ("tr21_{}", 1), ("1", 1): ("tr10_{}", 0), ("2", 0): ("tr11_{}", 0), ("2", 1): ("tr20_{}", 0)}

        def rows_out(k, tag, rs, nm):
            last, back = turns[tag, k]
            for j in range(TPB):
                A.op("scalar", f"xn{tag}{k}_{j}", [f"nm{tag}{k}"] + each(A, last, C, back), lambda e, b, j=j: e.activation(
                    xn[:, j], xin[:, k, j], ACT.Identity, bias=nm[:, k, j:j + 1], scale=rs[:, k, j:j + 1]))

        def turn_rows(k, tag, c, dst, readers, sums=None):
            hi, lo = f"xh{tag}{k}_{c}", f"xl{tag}{k}_{c}"
            bank = banks.take(A, [hi, lo])

            def turn(e, b):
                for j in range(TPB):
                    mm = e.transpose(ps[:, bank.slot, cols(j)], xn[:, j, cols(c)], ident[:])
                return mm
            A.op("tensor", f"tr{tag}{k}_{c}", [bank] + [f"xn{tag}{k}_{j}" for j in range(TPB)] + readers, turn)
            A.op("scalar", hi, [f"tr{tag}{k}_{c}"], lambda e, b: e.activation(
                dst[HI][:, c], ps[:, bank.slot], ACT.Copy, accum_out=sums) if sums is not None else e.activation(
                dst[HI][:, c], ps[:, bank.slot], ACT.Copy))
            A.op("vector", lo, [hi], lambda e, b: e.tensor_tensor(
                dst[LO][:, c], ps[:, bank.slot], dst[HI][:, c], ALU.subtract))

        def queries(k, m):
            hi, lo = f"qh{k}_{m}", f"ql{k}_{m}"
            bank = banks.take(A, [hi, lo])

            def mul(e, b):
                n = 0
                for c in range(C):
                    for w, v in passes([WQ[:, p, c, cols(m)] for p in (HI, LO)], [xoT[:, p, c] for p in (HI, LO)]):
                        mm = e.matmul(ps[:, bank.slot], w, v, start=(n == 0), stop=(n == 3 * C - 1))
                        n += 1
                return mm
            free = [A.earlier("s{}_1", TPB * k + j, TPB, NB * TPB) for j in range(TPB)]
            A.op("tensor", f"q{k}_{m}", [bank] + [f"xl1{k}_{c}" for c in range(C)] + free, mul)
            A.op("scalar", hi, [f"q{k}_{m}"], lambda e, b: e.activation(
                qT[:, HI, m], ps[:, bank.slot], ACT.Identity, bias=bq_col[:, m:m + 1]))
            A.op("vector", lo, [hi], lambda e, b: e.scalar_tensor_tensor(
                qT[:, LO, m], ps[:, bank.slot], bq_col[:, m:m + 1], qT[:, HI, m], ALU.add, ALU.subtract))

        def scores(t):
            k, j = divmod(t, TPB)
            T = NB * TPB

            half_heads = lambda a, g: a[:, HHEADS * g:HHEADS * g + HHEADS]
            by_head = lambda a: a.rearrange("p (h n) -> p h n", n=KEYS)
            wide = lambda a: a.unsqueeze(2).to_broadcast([P, HHEADS, KEYS])
            for g in range(2):
                bank = banks.take(A, [f"sub{t}_{g}"])

                def mul(e, b, g=g, bank=bank):
                    for c in range(2):
                        rows, keys = [qT[:, p, 2 * g + c, cols(j)] for p in (HI, LO)], [kb[p][:, 2 * g + c] for p in (HI, LO)]
                        for n, (w, v) in enumerate(passes(rows, keys)):
                            mm = e.matmul(ps[:, bank.slot, c * HPC * KEYS:(c + 1) * HPC * KEYS], w, v, start=(n == 0), stop=(n == 2))
                    return mm
                A.op("tensor", f"s{t}_{g}", [bank, "kv", A.earlier(f"pt{{}}_{g}", t, TPB, T)]
                     + [f"ql{k}_{m}" for m in (2 * g, 2 * g + 1)], mul)
                A.op("vector", f"max{t}_{g}", [f"s{t}_{g}", A.earlier(f"sub{{}}_{g}", t, TPB, T)],
                    lambda e, b, g=g, bank=bank: e.tensor_reduce(
                    half_heads(mx[:, j], g), by_head(ps[:, bank.slot]), AX.X, ALU.max))
                A.op("vector", f"sub{t}_{g}", [f"max{t}_{g}"], lambda e, b, g=g, bank=bank: e.tensor_tensor(
                    half_heads(by_head(prob[:, j]), g), by_head(ps[:, bank.slot]), wide(half_heads(mx[:, j], g)), ALU.subtract))
            A.op("scalar", f"exp{t}", [f"sub{t}_0", f"sub{t}_1"], lambda e, b: e.activation(
                prob[:, j], prob[:, j], ACT.Exp, scale=1.0 / (WSCALE * DK ** 0.5)))
            A.op("vector", f"sum{t}", [f"exp{t}", A.earlier("rec{}", t, TPB, T)], lambda e, b: e.tensor_reduce(
                sm[:, j], by_head(prob[:, j]), AX.X, ALU.add))
            A.op("vector", f"rec{t}", [f"sum{t}", A.earlier("nrm{}_0", t, TPB, T), A.earlier("nrm{}_1", t, TPB, T)],
                lambda e, b: e.reciprocal(rc[:, j], sm[:, j]))
            for g in range(2):
                A.op("gpsimd", f"nrm{t}_{g}", [f"rec{t}"], lambda e, b, g=g: e.tensor_tensor(
                    half_heads(by_head(prob[:, j]), g), half_heads(by_head(prob[:, j]), g), wide(half_heads(rc[:, j], g)), ALU.mult))

        def turn_probs(t):
            k, j = divmod(t, TPB)
            for g in range(2):
                hi, lo = f"ph{t}_{g}", f"pl{t}_{g}"
                bank = banks.take(A, [hi, lo])
                pairs = slice(4 * g, 4 * g + 4)

                def turn(e, b, g=g, bank=bank):
                    for r in range(4):
                        mm = e.transpose(ps[:, bank.slot, cols(r)], prob[:, j, cols(4 * g + r)], ident[:])
                    return mm
                free = each(A, "pv0_{}", C) if k else each(A, "pv1_{}", C, 1)
                A.op("tensor", f"pt{t}_{g}", [bank] + [f"nrm{t}_{g}"] + free, turn)
                four = lambda a: a.rearrange("p (r n) -> p r n", r=4)
                A.op("scalar", hi, [f"pt{t}_{g}"], lambda e, b, bank=bank, pairs=pairs: e.activation(
                    pT[:, HI, pairs, cols(j)], four(ps[:, bank.slot]), ACT.Copy))
                A.op("vector", lo, [hi], lambda e, b, bank=bank, pairs=pairs: e.tensor_tensor(
                    pT[:, LO, pairs, cols(j)], four(ps[:, bank.slot]), pT[:, HI, pairs, cols(j)], ALU.subtract))

        def values(k, c):
            hi, lo = f"oh{k}_{c}", f"ol{k}_{c}"
            bank = banks.take(A, [hi, lo])

            def mul(e, b):
                for n in range(3):
                    for half in range(2):
                        r = 2 * c + half
                        w, v = passes([vb[p][:, r] for p in (HI, LO)], [pT[:, p, r] for p in (HI, LO)])[n]
                        mm = e.matmul(ps[64 * half:64 * half + 64, bank.slot], w, v, start=(n == 0), stop=(n == 2))
                return mm
            ready = [f"pl{TPB * k + j}_{g}" for j in range(TPB) for g in range(2)] + ["kv"]
            free = each(A, "q1_{}", C) if k == 0 else each(A, "wo{}", TPB)
            A.op("tensor", f"pv{k}_{c}", [bank] + ready + free, mul)
            A.op("scalar", hi, [f"pv{k}_{c}"], lambda e, b: e.activation(xoT[:, HI, c], ps[:, bank.slot], ACT.Copy))
            A.op("vector", lo, [hi],
                lambda e, b: e.tensor_tensor(xoT[:, LO, c], ps[:, bank.slot], xoT[:, HI, c], ALU.subtract))

        def project(t):
            k, j = divmod(t, TPB)
            bank = banks.take(A, [f"res{t}"])

            def mul(e, b):
                n = 0
                for c in range(C):
                    for w, v in passes([xoT[:, p, c, cols(j)] for p in (HI, LO)], [WO[:, p, c] for p in (HI, LO)]):
                        mm = e.matmul(ps[:, bank.slot], w, v, start=(n == 0), stop=(n == 3 * C - 1))
                        n += 1
                return mm
            A.op("tensor", f"wo{t}", [bank] + [f"ol{k}_{c}" for c in range(C)], mul)
            A.op("vector", f"res{t}", [f"wo{t}", f"xb{t}"], lambda e, b: e.scalar_tensor_tensor(
                xin[:, k, j], ps[:, bank.slot], 1.0 / WSCALE, xin[:, k, j], ALU.mult, ALU.add))

        def first_rows(k):
            norm_rows(k, "1", lambda j: [f"load{k}"], mv1, rs1, nm1, [(A, f"nm1{k}", 1)])
            rows_out(k, "1", rs1, nm1)
            for j in range(TPB):
                A.op("gpsimd", f"xb{TPB * k + j}", [f"xn1{k}_{j}", f"st1{k}_{j}"], lambda e, b, j=j: e.tensor_tensor(
                    xin[:, k, j], xin[:, k, j], bo_rows[:], ALU.add))

        def second_rows(k):
            norm_rows(k, "2", lambda j: [f"res{TPB * k + j}"], mv2, rs2, nm2, [(FL[0], "keep_stats", 1), (FL[0], "keep_rs", 1)])
            rows_out(k, "2", rs2, nm2)

        def second_turn(k, c):
            turn_rows(k, "2", c, [x2T[:, k, HI], x2T[:, k, LO]], [
                w for F in FL for w in each(F, f"y0{k}_{{}}", C, 1) + each(F, f"y1{k}_{{}}", C, 1)] + [(FL[0], "gsum", 1)],
                      sums=gs[:, k, c:c + 1])

        def first_turn(k, c):
            free = each(A, "q0_{}", C) if k else [(A, f"wo{TPB + j}", 1) for j in range(TPB)]
            turn_rows(k, "1", c, [xoT[:, HI], xoT[:, LO]], free)

        load(0)
        load(1)
        load_kv()
        first_rows(0)
        for c in range(C):
            first_turn(0, c)
        for m in range(C):
            queries(0, m)
        first_rows(1)
        scores(0)
        scores(1)
        first_turn(1, 0)
        first_turn(1, 1)
        scores(2)
        first_turn(1, 2)
        first_turn(1, 3)
        scores(3)
        for m in range(C):
            queries(1, m)
        turn_probs(0)
        turn_probs(1)
        scores(4)
        turn_probs(2)
        turn_probs(3)
        scores(5)
        for c in range(C):
            values(0, c)
        scores(6)
        project(0)
        project(1)
        scores(7)
        project(2)
        project(3)
        turn_probs(4)
        turn_probs(5)
        second_rows(0)
        for c in range(C):
            second_turn(0, c)
        turn_probs(6)
        turn_probs(7)
        for c in range(C):
            values(1, c)
        for t in range(TPB, NB * TPB):
            project(t)
        second_rows(1)
        for c in range(C):
            second_turn(1, c)

        def lane(F, L):
            part, tiles = slice(L * LBLK, (L + 1) * LBLK), slice(TPL * L, TPL * L + TPL)

            def keep(k):
                F.op("scalar", f"keep{k}", each(A, f"xn2{k}_{{}}", TPB) + each(A, f"st2{k}_{{}}", TPB)
                     + [w for G in FL for w in each(G, f"out{k}_{{}}", TPL, 1)],
                     lambda e, b: e.activation(x1p[:, k], xin[:, k], ACT.Copy))

            def keep_stats():
                ready = each(A, "nm2{}", NB) + [w for G in FL for w in each(G, "ar{}", NB, 1) + each(G, "coef0{}", NB, 1)]
                F.op("vector", "keep_rs", ready, lambda e, b: e.tensor_copy(rs2p[:], rs2[:]))
                F.op("vector", "keep_stats", ready, lambda e, b: e.tensor_copy(nm2p[:], nm2[:]))

            def split(src, dst, name, ready, free):
                F.op("vector", f"{name}h", ready + free, lambda e, b: e.tensor_copy(dst[HI], src))
                F.op("vector", f"{name}l", [f"{name}h"], lambda e, b: e.tensor_tensor(dst[LO], src, dst[HI], ALU.subtract))

            def global_context():
                F.op("vector", "gsum", each(A, "xh20_{}", C) + each(A, "xh21_{}", C) + [(F, "gml", 1)],
                    lambda e, b: e.tensor_tensor(
                    gm[:], gs[:, 0], gs[:, 1], ALU.add))
                F.op("vector", "gmh", ["gsum", (F, "gz1", 1)], lambda e, b: e.tensor_scalar(
                    gmh[:, HI], gm[:], WSCALE / S, None, ALU.mult))
                F.op("vector", "gml", ["gmh"], lambda e, b: e.scalar_tensor_tensor(
                    gmh[:, LO], gm[:], WSCALE / S, gmh[:, HI], ALU.mult, ALU.subtract))

                def small(name, w, src, n_out, n_in, ready, place, at=0):
                    bank, take = place

                    def mul(e, b):
                        for m in range(n_out):
                            n = 0
                            for c in range(n_in):
                                for a, v in passes([w(p, c, m) for p in (HI, LO)], [src[:, p, c:c + 1] for p in (HI, LO)]):
                                    mm = e.matmul(ps[:, bank.slot, at + m:at + m + 1], a, v, start=(n == 0), stop=(n == 3 * n_in - 1))
                                    n += 1
                        return mm
                    F.op("tensor", name, take + ready, mul)
                    return bank
                bank1 = banks.take(F, ["gb1"])
                small("gz1", lambda p, c, m: G1[:, p, c, cols(m)], gmh, C2, C, ["gml"],
                      (bank1, [bank1]))
                F.op("vector", "gb1", ["gz1", (F, "gg1", 1), (F, "g1l", 1)], lambda e, b: e.scalar_tensor_tensor(
                    g1[:], ps[:, bank1.slot, 0:C2], WSCALE ** -2, gb1_col[:], ALU.mult, ALU.add))
                F.op("scalar", "gg1", ["gb1"], lambda e, b: e.activation(g1[:], g1[:], ACT.Gelu))
                split(g1[:], [g1h[:, HI], g1h[:, LO]], "g1", ["gg1"], [(F, "gz2", 1)])
                bank2 = banks.take(F, ["gg2", "gt"])
                small("gz2", lambda p, c, m: G2[:, p, c], g1h, 1, C2, ["g1l"],
                      (bank2, [bank2]))
                F.op("scalar", "gg2", ["gz2", (F, "g2l", 1)], lambda e, b: e.activation(
                    g2[:], ps[:, bank2.slot, 0:1], ACT.Gelu, bias=gb2_col[:], scale=1.0 / WSCALE))
                split(g2[:], [g2h[:, HI], g2h[:, LO]], "g2", ["gg2"], [(F, "gz3", 1)])
                small("gz3", lambda p, c, m: G3[:, p], g2h, 1, 1, ["g2l"], (bank2, []), at=1)
                F.op("scalar", "gt", ["gz3", (F, "alpha", 1)], lambda e, b: e.activation(
                    gt[:], ps[:, bank2.slot, 1:2], ACT.Tanh, bias=scal[:, 2:3], scale=0.5 / WSCALE))
                F.op("vector", "alpha", ["gt"] + [w for G in FL for k in range(NB) for w in each(G, f"cc{k}_{{}}", 3, 1)],
                    lambda e, b: e.tensor_scalar(
                    alpha[:], gt[:], scal[:, 4:5], 0.1, ALU.mult, ALU.add))

            def first_products(k, m):
                for name, order, dst in (("y0", ((0, 0), (1, 1), (2, 2), (3, 3)), Y0),
                                         ("y1", ((0, 2), (4, 3), (5, 0), (3, 1)), Y1)):
                    copy = f"{name}c{k}_{m}"
                    bank = banks.take(F, [copy])

                    def mul(e, b, order=order, bank=bank):
                        n = 0
                        for wc, xc in order:
                            for w, v in passes([W1[:, p, wc, cols(m)] for p in (HI, LO)], [x2T[:, k, p, xc, part] for p in (HI, LO)]):
                                mm = e.matmul(ps[:, bank.slot, 0:LBLK], w, v, start=(n == 0), stop=(n == 3 * C - 1))
                                n += 1
                        return mm
                    free = F.earlier("pre{}_2_" + str(m), k, 1, NB)
                    F.op("tensor", f"{name}{k}_{m}", [bank, free] + each(A, f"xl2{k}_{{}}", C), mul)
                    F.op("scalar", copy, [f"{name}{k}_{m}"], lambda e, b, bank=bank, dst=dst: e.activation(
                        dst[:, L, m], ps[:, bank.slot, 0:LBLK], ACT.Copy, scale=1.0 / WSCALE))
                    if name == "y0":
                        slot = acts.take(F, [f"h{k}_0_{m}l"])
                        first_activation(k, 0, m, lambda: Y0[:, L, m], [copy], slot, [slot])

            def activate(name, src, slot, bias, scale, ready, take, dst, low="vector"):
                F.op("scalar", f"h{name}h", ready, lambda e, b: e.activation(
                    dst[HI], src(), ACT.Gelu, bias=bias, scale=scale))
                F.op("scalar", f"g{name}", ready + (take or [f"h{name}h"]), lambda e, b: e.activation(
                    ft[:, slot.slot], src(), ACT.Gelu, bias=bias, scale=scale))
                F.op(low, f"h{name}l", [f"g{name}", f"h{name}h"], lambda e, b: e.tensor_tensor(
                    dst[LO], ft[:, slot.slot], dst[HI], ALU.subtract))

            def first_activation(k, y, m, src, ready, slot, take):
                free = [F.earlier(f"l2{{}}_{n}", 3 * k + y, 1, 3 * NB) for n in range(C2)]
                activate(f"{k}_{y}_{m}", src, slot, b1_col[:, m:m + 1], 1.0, ready + free, take,
                         [h1[:, L, HI, m], h1[:, L, LO, m]], "gpsimd")

            def combine(k, y, m):
                slot = acts.take(F, [f"h{k}_{y}_{m}l"])
                u, v = f"mul{k}_{y}_{m}", f"pre{k}_{y}_{m}"
                F.op(SCALED_BY[m], u, [slot, f"y1c{k}_{m}", f"cc{k}_0" if y == 1 else f"b2_{k}"],
                    lambda e, b: e.tensor_tensor(
                    ft[:, slot.slot], Y1[:, L, m], c1[:, L] if y == 1 else b2[:, L], ALU.mult))
                if y == 2:
                    F.op("gpsimd", f"am{k}_{m}", [f"a2_{k}"] + [f"pre{k}_1_{m}"], lambda e, b: e.tensor_tensor(
                        Y0[:, L, m], Y0[:, L, m], a2[:, L], ALU.mult))
                F.op("vector", v, [u] + ([f"am{k}_{m}"] if y == 2 else []) + [f"y0c{k}_{m}"], lambda e, b: e.tensor_tensor(
                    ft[:, slot.slot], ft[:, slot.slot], Y0[:, L, m], ALU.add))
                first_activation(k, y, m, lambda: ft[:, slot.slot], [v], slot, [])

            def later_layers(k, y):
                i, N = 3 * k + y, 3 * NB
                for m in range(C2):
                    name = f"{i}_{m}"
                    bank = banks.take(F, [f"gb{name}", f"hb{name}h"])

                    def mul(e, b, m=m, bank=bank):
                        n = 0
                        for c in range(C):
                            for w, v in passes([W2[:, p, c, cols(m)] for p in (HI, LO)], [h1[:, L, p, c] for p in (HI, LO)]):
                                mm = e.matmul(ps[:, bank.slot, 0:LBLK], w, v, start=(n == 0), stop=(n == 3 * C - 1))
                                n += 1
                        return mm
                    F.op("tensor", f"l2{name}", [bank, F.earlier("l3{}", i, 1, N)] + [f"h{k}_{y}_{c}l" for c in range(C)], mul)
                    slot = acts.take(F, [f"hb{name}l"])
                    activate(f"b{name}", lambda bank=bank: ps[:, bank.slot, 0:LBLK], slot, b2_col[:, m:m + 1], 1.0 / WSCALE,
                             [f"l2{name}"], [slot], [h2[:, L, HI, m], h2[:, L, LO, m]])
                bank = banks.take(F, [f"gc{i}", f"hc{i}h"])

                def mul3(e, b, bank=bank):
                    for c in range(C2):
                        for n, (w, v) in enumerate(passes([W3[:, p, c] for p in (HI, LO)], [h2[:, L, p, c] for p in (HI, LO)])):
                            mm = e.matmul(ps[:, bank.slot, 0:LBLK], w, v, start=(n + c == 0), stop=(n + c == C2 + 1))
                    return mm
                F.op("tensor", f"l3{i}", [bank, F.earlier("l4{}", i, 1, N)] + [f"hb{i}_{m}l" for m in range(C2)], mul3)
                slot = acts.take(F, [f"hc{i}l"])
                activate(f"c{i}", lambda bank=bank: ps[:, bank.slot, 0:LBLK], slot, b3_col[:], 1.0 / WSCALE, [f"l3{i}"], [slot],
                         [h3[:, L, HI], h3[:, L, LO]])
                bank = banks.take(F, [f"u{i}"])

                def mul4(e, b, bank=bank):
                    for n, (w, v) in enumerate(passes([W4[:, p] for p in (HI, LO)], [h3[:, L, p] for p in (HI, LO)])):
                        mm = e.matmul(ps[:, bank.slot, 0:LBLK], w, v, start=(n == 0), stop=(n == 2))
                    return mm
                F.op("tensor", f"l4{i}", [bank, f"hc{i}l"], mul4)
                last = [f"a2_{k}", f"b2_{k}"] if y == 2 else [F.earlier("tb{}", k, 1, NB)]
                dst = c1 if y == 0 else cpl
                F.op("scalar", f"u{i}", [f"l4{i}"] + last,
                     lambda e, b: e.activation(dst[:, L], ps[:, bank.slot, 0:LBLK], ACT.Tanh, bias=scal[:, 1:2], scale=0.5 / WSCALE))
                F.op("vector", f"cc{k}_{y}", [f"u{i}", (FL[0], "alpha", 0)], lambda e, b: e.tensor_scalar(
                    dst[:, L], dst[:, L], scal[:, 3:4], alpha[:], ALU.mult, ALU.add))

            def second_factor(k):
                before = [F.earlier(f"mul{{}}_2_{m}", k, 1, NB) for m in range(C)] + [
                    F.earlier(f"am{{}}_{m}", k, 1, NB) for m in range(C)] + [F.earlier("tb{}", k, 1, NB), f"cc{k}_0"]
                F.op("vector", f"b2_{k}", [f"cc{k}_1"] + before, lambda e, b: e.tensor_tensor(
                    b2[:, L], c1[:, L], cpl[:, L], ALU.add))
                F.op("vector", f"cc12_{k}", [f"cc{k}_1"] + before, lambda e, b: e.tensor_tensor(
                    a2[:, L], c1[:, L], cpl[:, L], ALU.mult))
                F.op("vector", f"a2_{k}", [f"cc12_{k}"], lambda e, b: e.tensor_scalar(
                    a2[:, L], a2[:, L], -1.0, 1.0, ALU.mult, ALU.add))

            def finish(k):
                row = slice(0, 1)
                F.op("vector", f"m1_{k}", [f"cc{k}_2"] + each(F, f"mul{k}_1_{{}}", C), lambda e, b: e.tensor_tensor(
                    c1[row, L], cpl[row, L], b2[row, L], ALU.mult))
                F.op("vector", f"m2_{k}", [f"m1_{k}"],
                    lambda e, b: e.tensor_tensor(cpl[row, L], cpl[row, L], a2[row, L], ALU.mult))
                F.op("vector", f"a3_{k}", [f"m1_{k}"],
                    lambda e, b: e.tensor_tensor(c1[row, L], a2[row, L], c1[row, L], ALU.subtract))
                F.op("vector", f"b3_{k}", [f"m2_{k}"],
                    lambda e, b: e.tensor_tensor(cpl[row, L], b2[row, L], cpl[row, L], ALU.add))
                bank = banks.take(F, [f"ar{k}", f"coef0{k}"])

                def turn(e, b):
                    for n, src in enumerate((c1, cpl)):
                        for j in range(TPL):
                            mm = e.transpose(ps[:, bank.slot, n * TPL + j:n * TPL + j + 1], src[row, L, cols(j)], ident[row, 0:1])
                    return mm
                F.op("tensor", f"tb{k}", [bank] + [f"a3_{k}", f"b3_{k}"], turn)
                prev = [F.earlier(f"co{n}{{}}", k, 1, NB) for n in range(3)]
                F.op("vector", f"ar{k}", [f"tb{k}", (FL[0], "keep_rs", 0)] + prev, lambda e, b: e.tensor_tensor(
                    ab[:, L], ps[:, bank.slot, 0:2 * TPL].rearrange("p (n j) -> p n j", n=2),
                    rs2p[:, k, tiles].unsqueeze(1).to_broadcast([P, 2, TPL]), ALU.mult))
                done = [F.earlier(f"{n}{{}}_{j}", k, 1, NB) for n in ("t", "out") for j in range(TPL)]
                F.op("vector", f"co0{k}", [f"ar{k}"] + done,
                    lambda e, b: e.tensor_scalar(co[:, L, 0], ab[:, L, 0], 1.0, None, ALU.add))
                F.op("vector", f"co1{k}", [f"ar{k}"] + done, lambda e, b: e.tensor_copy(co[:, L, 1], ab[:, L, 1]))
                F.op("vector", f"co2{k}", [f"ar{k}"] + done,
                    lambda e, b: e.tensor_scalar(co[:, L, 2], ab[:, L, 1], -1.0, None, ALU.mult))
                F.op("vector", f"coef0{k}", [f"tb{k}", (FL[0], "keep_stats", 0),
                                                F.earlier("co3{}", k, 1, NB), F.earlier("co4{}", k, 1, NB)],
                    lambda e, b: e.tensor_tensor(
                    an[:, L], ps[:, bank.slot, 0:2 * TPL].rearrange("p (n j) -> p n j", n=2),
                    nm2p[:, k, tiles].unsqueeze(1).to_broadcast([P, 2, TPL]), ALU.mult))
                F.op("vector", f"co3{k}", [f"coef0{k}"] + done,
                    lambda e, b: e.tensor_tensor(co[:, L, 3], an[:, L, 0], an[:, L, 1], ALU.add))
                F.op("vector", f"co4{k}", [f"coef0{k}"] + done,
                    lambda e, b: e.tensor_tensor(co[:, L, 4], an[:, L, 0], an[:, L, 1], ALU.subtract))
                chunk = lambda a: a.rearrange("p (c n) -> p c n", c=C)
                for j in range(TPL):
                    dst, src = chunk(ot[:, L, j]), chunk(x1p[:, k, TPL * L + j])
                    def straight(e, b, dst=dst, src=src, j=j):
                        e.activation(dst[:, 0::3], src[:, 0::3], ACT.Identity, bias=co[:, L, 3, j:j + 1], scale=co[:, L, 0, j:j + 1])
                        return e.activation(dst[:, 1:3], src[:, 1:3], ACT.Identity, bias=co[:, L, 4, j:j + 1], scale=co[:, L, 0, j:j + 1])
                    F.op("scalar", f"t{k}_{j}", [
                        F.earlier(f"store{{}}_{j}", k, 1, NB), f"co0{k}", f"co3{k}", f"co4{k}", (FL[0], f"keep{k}", 0)], straight)

                    def add(e, b, dst=dst, src=src, j=j):
                        for to, of, sign in ((0, 2, 1), (3, 1, 1), (1, 3, 2), (2, 0, 2)):
                            ins = e.scalar_tensor_tensor(dst[:, to], src[:, of], co[:, L, sign, j:j + 1], dst[:, to], ALU.mult, ALU.add)
                        return ins
                    F.op("vector", f"out{k}_{j}", [f"t{k}_{j}", f"co1{k}", f"co2{k}"], add)
                    F.op("sync", f"store{k}_{j}", [f"out{k}_{j}"], lambda e, b, j=j: e.dma_start(
                        batch_of(out_dram, b)[k][:, (TPL * L + j) * D:(TPL * L + j + 1) * D], ot[:, L, j]), dma=f"stored{j}")

            if L == 0:
                keep(0)
                keep(1)
                keep_stats()
            for k in range(NB):
                for m in range(C):
                    first_products(k, m)
                    if k == 0 and m == 0 and L == 0:
                        global_context()
                later_layers(k, 0)
                for m in range(C):
                    combine(k, 1, m)
                later_layers(k, 1)
                second_factor(k)
                for m in range(C):
                    combine(k, 2, m)
                later_layers(k, 2)
                finish(k)

        for L in range(LANES):
            lane(FL[L], L)

        both = weave([(-1, FL[0]), (-1, FL[1]), (0, A)], True)
        first = weave([(0, A)], False)
        final = weave([(B - 1, F) for F in FL], False)

        def run(step, order, name, eng):
            seen = {}
            for offset, stream, op in order:
                if op.engine == name:
                    issue(eng, stream, step, offset, op, seen)

        def engine_program(name, eng):
            if name == "sync":
                eng.wait_ge(kv_stored[0], 16)
            run(None, [o for o in first if not o[2].name.startswith("load")], name, eng)
            for b in range(B):
                eng.wait_ge(kv_stored[b], 16)
            with eng.Fori(1, B) as i:
                if name == "scalar":
                    eng.wait_ge(warmed, i)
                    eng.activation(warm[:], minus_half[:, 0:1], ACT.Gelu).then_inc(warmed, 1)
                run(i, both, name, eng)
            run(None, final, name, eng)
            if name == "sync":
                for F in FL:
                    for slot in range(2):
                        key = f"stored{slot}"
                        eng.wait_ge(F.sems[key], 16 * F.count[key] * (B + 1))

        with nc.Block() as credit:
            @credit.sync
            def _(eng):
                eng.sem_inc(warmed, 1)
                for F in FL:
                    for key, n in F.count.items():
                        eng.sem_inc(F.sems[key], n * (1 if key in ENGINES else 16))

        with nc.Block() as main:
            @main.sync
            def _(eng):
                engine_program("sync", eng)

            @main.tensor
            def _(eng):
                engine_program("tensor", eng)

            @main.scalar
            def _(eng):
                engine_program("scalar", eng)

            @main.vector
            def _(eng):
                engine_program("vector", eng)

            @main.gpsimd
            def _(eng):
                engine_program("gpsimd", eng)


def setup(nc, sem, g):
    sems = {e: sem(f"setup_{e}") for e in ENGINES[:4]}
    W = Stream("setup", sems, 0)
    with ExitStack() as ctx:
        def sb(name, shape, dt=F32):
            return ctx.enter_context(nc.sbuf_tensor(name, shape, dt))

        wq_s, wk_s = sb("wq_s", [P, C, D]), sb("wk_s", [P, C, D])
        wv_s, wo_s, w1_s = sb("wv_s", [P, C, D]), sb("wo_s", [P, C, D]), sb("w1_s", [P, C, D])
        w2_s, w3_s, gw1_s, gw2_s = (sb("w2_s", [P, C, D2]), sb("w3_s", [P, C2, D3]), sb("gw1_s", [P, C, D2]),
                                    sb("gw2_s", [P, C2, D3]))
        last_s = sb("last_s", [P, 2])
        last64 = sb("last64", [P, 2])
        ctx_s = sb("ctx_s", [P, C, B, KEYS])
        wkT = sb("wkT", [P, C, D])
        k32 = sb("k32", [P, C, B, KEYS])
        kv = g["late"][:, 0:B * KV].bitcast(F16).rearrange("p (b a n) -> p b a n", b=B, a=2)
        turn = sb("turn", [P, P])
        headsel = sb("headsel", [P, C, H])
        phases = sb("phases", [P, H])
        picked = sb("picked", [P, C, H])
        ang = sb("ang", [P, 6, C])
        turns = sb("turns", [P, C], I32)
        rot = sb("rot", [P, C, P])
        b_s = sb("b_s", [P, 2, C])
        bk_col = sb("bk_col", [P, C])
        scal_s = sb("scal_s", [P, 3])
        ones = sb("ones", [P, P])
        bv_s = sb("bv_s", [1, D])
        ps = ctx.enter_context(nc.psum_tensor("ps_setup", [P, 8, BLK], F32))
        cols = lambda j: slice(j * P, (j + 1) * P)

        def load(name, dst, src):
            sems[f"in_{name}"] = sem(f"in_{name}")
            W.op("sync", name, [], lambda e, b: e.dma_start(dst, src), dma=f"in_{name}")
        by_chunk = lambda a: a.rearrange("(c p) n -> p c n", p=P)
        load("phase", phases[:], g["phase"].rearrange("h a b -> (a b) h").partition_broadcast(P))
        load("headsel", headsel[:].rearrange("p c h -> p (c h)"), g["headsel_in"])
        load("ident", g["ident"][:], g["ident_in"])
        load("turn", turn[:], g["turn_in"])
        ctx_view = g["ctxT"].rearrange("(c p) b n -> p c b n", p=P)
        for c in range(C):
            load(f"ctx{c}", ctx_s[:, c], ctx_view[:, c])
        load("wv", wv_s[:], by_chunk(g["wvT"]))
        load("bv", bv_s[:], g["bv"].rearrange("(a n) -> a n", a=1))
        load("wk", wk_s[:], by_chunk(g["wk"]))
        load("bq", b_s[:, 0], g["bq"])
        load("bk", b_s[:, 1], g["bk"])
        load("wq", wq_s[:], by_chunk(g["wq"]))
        load("wo", wo_s[:], by_chunk(g["woT"]))
        load("bo", g["bo_rows"][:], g["bo"].rearrange("(a n) -> a n", a=1).partition_broadcast(P))
        load("w1", w1_s[:], by_chunk(g["cw1"]))
        load("b1", g["b1_col"][:], g["cb1"])
        load("w2", w2_s[:], by_chunk(g["cw2"]))
        load("b2", g["b2_col"][:], g["cb2"])
        load("w3", w3_s[:], by_chunk(g["cw3"]))
        load("b3", g["b3_col"][:], g["cb3"])
        load("w4", last_s[:, 0:1], g["cw4"])
        load("g3", last_s[:, 1:2], g["gw3"])
        load("g1", gw1_s[:], by_chunk(g["gw1"]))
        load("gb1", g["gb1_col"][:], g["gb1"])
        load("g2", gw2_s[:], by_chunk(g["gw2"]))
        load("gb2", g["gb2_col"][:], g["gb2"])
        for n, a in enumerate(("arange", "cb4", "gb3")):
            load(a, scal_s[:, n:n + 1], g[a].rearrange("(a n) -> a n", a=1).partition_broadcast(P))

        V, S_, G = "vector", "scalar", "gpsimd"
        W.op(G, "ones", [], lambda e, b: e.memset(ones[:], 1.0))
        W.op(G, "half", [], lambda e, b: e.memset(g["minus_half"][:], -0.5))
        for bt in range(B):
            W.op((V, G)[bt % 2], f"zero{bt}", [], lambda e, b, bt=bt: e.memset(kv[:, bt].bitcast(F32), 0.0))

        W.op(V, "pick", ["phase", "headsel"], lambda e, b: e.tensor_tensor(
            picked[:], headsel[:], phases[:].unsqueeze(1).to_broadcast([P, C, H]), ALU.mult))
        W.op(V, "ph", ["pick"], lambda e, b: e.tensor_reduce(ang[:, 0], picked[:], AX.X, ALU.add))
        W.op(V, "turns", ["ph"], lambda e, b: e.tensor_scalar(turns[:], ang[:, 0], 1 / (2 * np.pi), None, ALU.mult))
        W.op(V, "turnsf", ["turns"], lambda e, b: e.tensor_copy(ang[:, 1], turns[:]))
        W.op(V, "red1", ["turnsf"], lambda e, b: e.scalar_tensor_tensor(
            ang[:, 2], ang[:, 1], -TWO_PI_HI, ang[:, 0], ALU.mult, ALU.add))
        W.op(V, "red2", ["red1"], lambda e, b: e.scalar_tensor_tensor(
            ang[:, 2], ang[:, 1], -TWO_PI_LO, ang[:, 2], ALU.mult, ALU.add))
        W.op(V, "clamp", ["red2"], lambda e, b: e.tensor_scalar(
            ang[:, 2], ang[:, 2], -3.1415925, 3.1415925, ALU.max, ALU.min))
        W.op(S_, "sin", ["clamp"], lambda e, b: e.activation(ang[:, 3], ang[:, 2], ACT.Sin))
        W.op(S_, "sinh", ["clamp"], lambda e, b: e.activation(ang[:, 4], ang[:, 2], ACT.Sin, scale=0.5))
        W.op(V, "sq", ["sinh"], lambda e, b: e.tensor_tensor(ang[:, 5], ang[:, 4], ang[:, 4], ALU.mult))
        W.op(V, "cos", ["sq"], lambda e, b: e.tensor_scalar(ang[:, 5], ang[:, 5], -2.0, 1.0, ALU.mult, ALU.add))
        for c in range(C):
            W.op(V, f"rc{c}", ["cos", "ident"], lambda e, b, c=c: e.tensor_scalar(
                rot[:, c], g["ident"][:], ang[:, 5, c:c + 1], None, ALU.mult))
            W.op(V, f"rot{c}", [f"rc{c}", "sin", "turn"], lambda e, b, c=c: e.scalar_tensor_tensor(
                rot[:, c], turn[:], ang[:, 3, c:c + 1], rot[:, c], ALU.mult, ALU.add))

        ring = Ring(8)

        vpart = lambda p: kv[:, :, p, C * HPC * KEYS:KV].rearrange("q b (r h n) -> q b r h n", r=PAIRS, h=2)
        for bt in range(B):
            bank, waits = ring.take([f"vh{bt}_1", f"vl{bt}_1"])

            def mul(e, b, bt=bt, bank=bank):
                half = lambda a, h: a.rearrange("p (r h n) -> p r h n", h=2, n=DK)[:, :, h]
                for c in range(C):
                    for h in range(2):
                        e.matmul(ps[KEYS * h:KEYS * h + KEYS, bank, 0:D2], ctx_s[:, c, bt], half(wv_s[:, c], h), start=(c == 0), stop=False)
                for h in range(2):
                    mm = e.matmul(ps[KEYS * h:KEYS * h + KEYS, bank, 0:D2], ones[0:1, 0:KEYS], half(bv_s[:], h), start=False, stop=True)
                return mm
            W.op("tensor", f"vm{bt}", waits + ["wv", "bv", "ones"] + [f"ctx{c}" for c in range(C)], mul)
            for h in range(2):
                rows = slice(KEYS * h, KEYS * h + KEYS)
                src = ps[rows, bank, 0:D2].rearrange("p (r n) -> p r n", r=PAIRS)
                W.op(S_, f"vh{bt}_{h}", [f"vm{bt}", f"zero{bt}"], lambda e, b, bt=bt, h=h, rows=rows, src=src: e.activation(
                    vpart(HI)[rows, bt, :, h], src, ACT.Copy))
                W.op(V, f"vl{bt}_{h}", [f"vh{bt}_{h}"], lambda e, b, bt=bt, h=h, rows=rows, src=src: e.tensor_tensor(
                    vpart(LO)[rows, bt, :, h], src, vpart(HI)[rows, bt, :, h], ALU.subtract))

        def bias_mul(e, b, n, bank):
            for c in range(C):
                mm = e.matmul(ps[:, bank, c:c + 1], rot[:, c], b_s[:, n, c:c + 1], start=True, stop=True)
            return mm
        for n, (name, dst, scale) in enumerate((("bq", g["bq_col"], WSCALE), ("bk", bk_col, 1.0))):
            bank, waits = ring.take([f"{name}c"])
            W.op("tensor", f"{name}m", waits + [f"rot{C - 1}", name], lambda e, b, n=n, bank=bank: bias_mul(e, b, n, bank))
            W.op(V, f"{name}c", [f"{name}m"], lambda e, b, bank=bank, dst=dst, scale=scale: e.tensor_scalar(
                dst[:], ps[:, bank, 0:C], scale, None, ALU.mult))

        def rotate(name, src, c, readers):
            bank, waits = ring.take(readers)

            def mul(e, b):
                for o in range(C):
                    mm = e.matmul(ps[:, bank, cols(o)], src[:, o, cols(c)], rot[:, o], start=True, stop=True)
                return mm
            W.op("tensor", f"{name}r{c}", waits + [f"rot{C - 1}", name], mul)
            return bank
        for c in range(C):
            bank = rotate("wk", wk_s, c, [f"wkT{c}"])
            W.op(S_, f"wkT{c}", [f"wkr{c}"], lambda e, b, c=c, bank=bank: e.activation(wkT[:, c], ps[:, bank], ACT.Copy))

        def split(name, dst_hi, dst_lo, src, ready, scale=WSCALE):
            W.op(S_, f"{name}_hi", ready, lambda e, b: e.activation(dst_hi, src, ACT.Copy, scale=scale))
            W.op(V, f"{name}_lo", [f"{name}_hi"], lambda e, b: e.scalar_tensor_tensor(
                dst_lo, src, scale, dst_hi, ALU.mult, ALU.subtract))

        split("wos", g["WO"][:, HI], g["WO"][:, LO], wo_s[:], ["wo"])
        split("w1s", g["W1"][:, HI, 0:C], g["W1"][:, LO, 0:C], w1_s[:], ["w1"])
        for p in (HI, LO):
            W.op(V, f"w1n{p}", ["w1s_lo"], lambda e, b, p=p: e.tensor_scalar(
                g["W1"][:, p, C:C + 2], g["W1"][:, p, 1:3], -1.0, None, ALU.mult))
        split("w2s", g["W2"][:, HI], g["W2"][:, LO], w2_s[:], ["w2"])
        split("w3s", g["W3"][:, HI], g["W3"][:, LO], w3_s[:], ["w3"])
        split("g1s", g["G1"][:, HI], g["G1"][:, LO], gw1_s[:], ["g1"])
        split("g2s", g["G2"][:, HI], g["G2"][:, LO], gw2_s[:], ["g2"])
        W.op(V, "last", ["w4", "g3"], lambda e, b: e.tensor_scalar(last64[:], last_s[:], WSCALE, None, ALU.mult))
        for n, dst in enumerate((g["W4"], g["G3"])):
            W.op(V, f"last{n}_hi", ["last", "ones"], lambda e, b, n=n, dst=dst: e.tensor_scalar(
                dst[:, HI], ones[:], last64[:, n:n + 1], None, ALU.mult))
            W.op(V, f"last{n}_lo", [f"last{n}_hi"], lambda e, b, n=n, dst=dst: e.scalar_tensor_tensor(
                dst[:, LO], ones[:], last64[:, n:n + 1], dst[:, HI], ALU.mult, ALU.subtract))
        for n, (src, scale) in enumerate(((0, 1.0), (1, 0.5), (2, 0.5), (0, 0.3), (0, 0.7))):
            W.op(V, f"scal{n}", ["arange", "cb4", "gb3"], lambda e, b, n=n, src=src, scale=scale: e.tensor_scalar(
                g["scal"][:, n:n + 1], scal_s[:, src:src + 1], scale, None, ALU.mult))

        kpart = lambda p: kv[:, :, p, 0:C * HPC * KEYS].rearrange("q b (c h n) -> q b c h n", c=C, h=HPC)
        for m in range(C):
            bank, waits = ring.take([f"k32{m}"])

            def mul(e, b, m=m, bank=bank):
                for c in range(C):
                    mm = e.matmul(ps[:, bank], wkT[:, c, cols(m)], ctx_s[:, c], start=(c == 0), stop=(c == C - 1))
                return mm
            W.op("tensor", f"km{m}", waits + [f"wkT{c}" for c in range(C)] + [f"ctx{c}" for c in range(C)], mul)
            W.op(S_, f"k32{m}", [f"km{m}", "bkc"], lambda e, b, m=m, bank=bank: e.activation(
                k32[:, m], ps[:, bank].rearrange("p (b n) -> p b n", b=B), ACT.Identity, bias=bk_col[:, m:m + 1]))
            for h in range(HPC):
                rows = slice(DK * h, DK * h + DK)
                W.op(S_, f"kh{m}_{h}", [f"k32{m}", f"zero{B - 2}", f"zero{B - 1}"],
                    lambda e, b, m=m, h=h, rows=rows: e.activation(
                    kpart(HI)[rows, :, m, h], k32[rows, m], ACT.Copy))
                W.op((V, G)[h % 2], f"kl{m}_{h}", [f"kh{m}_{h}"], lambda e, b, m=m, h=h, rows=rows: e.tensor_tensor(
                    kpart(LO)[rows, :, m, h], k32[rows, m], kpart(HI)[rows, :, m, h], ALU.subtract))

        for bt in range(B):
            sems[f"kv_stored{bt}"] = g["kv_stored"][bt]
            W.op("sync", f"store{bt}", [f"vh{bt}_1", f"vl{bt}_1", f"kl{C - 1}_{HPC - 2}", f"kl{C - 1}_{HPC - 1}"],
                lambda e, b, bt=bt: e.dma_start(
                g["kv_dram"][bt], kv[:, bt].rearrange("p a n -> p (a n)")), dma=f"kv_stored{bt}")

        for c in range(C):
            bank = rotate("wq", wq_s, c, [f"wqs{c}_hi", f"wqs{c}_lo"])
            split(f"wqs{c}", g["WQ"][:, HI, c], g["WQ"][:, LO, c], ps[:, bank], [f"wqr{c}"])

        def run(name, eng):
            seen = {}
            for op in W.ops:
                if op.name == "store0" and name == "sync":
                    g["load_first"](eng)
                if op.engine == name:
                    issue(eng, W, None, 0, op, seen)
            if name == "vector":
                for key in ("ident", "bo", "b1", "b2", "b3", "gb1", "gb2"):
                    eng.wait_ge(sems[f"in_{key}"], 16)

        with nc.Block() as block:
            @block.sync
            def _(eng):
                run("sync", eng)

            @block.tensor
            def _(eng):
                run("tensor", eng)

            @block.scalar
            def _(eng):
                run("scalar", eng)

            @block.vector
            def _(eng):
                run("vector", eng)

            @block.gpsimd
            def _(eng):
                run("gpsimd", eng)


def kernel(**inputs):
    import concourse.bacc as bacc
    from concourse.bass_utils import run_bass_kernel_spmd

    a = {k.replace("L0_xattn_", "").replace("L0_ffn_", ""): np.asarray(v) for k, v in inputs.items()}
    half = DK // 2
    turn = np.zeros((P, P), np.float32)
    for o in range(P):
        if o % DK < half:
            turn[o, o + half] = 1.0
        else:
            turn[o, o - half] = -1.0
    headsel = np.zeros((P, C, H), np.float32)
    for o in range(D):
        headsel[o % P, o // P, o // DK] = 1.0
    columns = lambda b: np.ascontiguousarray(b.reshape(-1, P).T)
    arrays = {
        "x": a["x"], "ctxT": np.ascontiguousarray(a["ctx_1024"].transpose(2, 0, 1)),
        "wq": a["Wq"], "bq": columns(a["bq"]), "wk": a["Wk"], "bk": columns(a["bk"]),
        "wvT": np.ascontiguousarray(a["Wv"].T), "bv": a["bv"],
        "woT": np.ascontiguousarray(a["Wo"].T), "bo": a["bo"], "phase": a["phase"],
        "cw1": a["cn_w1"], "cb1": columns(a["cn_b1"]), "cw2": a["cn_w2"], "cb2": columns(a["cn_b2"]),
        "cw3": a["cn_w3"], "cb3": columns(a["cn_b3"]), "cw4": a["cn_w4"], "cb4": a["cn_b4"],
        "gw1": a["gc_w1"], "gb1": columns(a["gc_b1"]), "gw2": a["gc_w2"], "gb2": columns(a["gc_b2"]),
        "gw3": a["gc_w3"], "gb3": a["gc_b3"], "arange": a["adaptive_range"],
        "ident_in": np.eye(P, dtype=np.float32), "turn_in": turn, "headsel_in": headsel.reshape(P, C * H),
    }
    nc = bacc.Bacc("TRN2", target_bir_lowering=False, num_devices=1)
    args = [nc.dram_tensor(n, v.shape, mybir.dt.from_np(v.dtype), kind="ExternalInput").ap() for n, v in arrays.items()]
    args.append(nc.dram_tensor("out", (B, S, D), F32, kind="ExternalOutput").ap())
    program(nc, *args)
    result = run_bass_kernel_spmd(nc, [arrays], core_ids=[0])
    return result.results[0]["out"]
```
